# Optimizing a Trainium2 kernel written in Bass

```python
import numpy as np
import jax
import jax.numpy as jnp

def _softmax(x, axis=-1):
    return jax.nn.softmax(x, axis=axis)

def _gelu(x):
    return jax.nn.gelu(x, approximate=True)

def _silu(x):
    return jax.nn.silu(x)

def _sigmoid(x):
    return jax.nn.sigmoid(x)

def _layernorm(x, axis=-1, eps=1e-05):
    m = jnp.mean(x, axis=axis, keepdims=True)
    v = jnp.var(x, axis=axis, keepdims=True)
    return (x - m) / jnp.sqrt(v + eps)

def _scatter_add(tgt, idx, src, axis=0):
    return tgt.at[idx].add(src)

def _segment_sum(src, seg, n):
    return jax.ops.segment_sum(src, seg, n)
kernel_name = 'mk_early_fusion_d1_tok_img768_r4_7585da'

def setup_inputs(seed: int=0):
    np.random.seed(seed)
    _w = jnp.asarray

    def _rec_inputs():
        import jax
        import jax.numpy as jnp
        _rk = jax.random.key(seed)
        x = -0.000222058 + 0.999998 * jax.random.normal(jax.random.fold_in(_rk, 1), (8, 3, 96, 96), jnp.float32)
        txt = -5.78238e-05 + 0.554219 * jax.random.normal(jax.random.fold_in(_rk, 2), (8, 512, 192), jnp.float32)
        return (x, txt)
    x, txt = _rec_inputs()

    def _L0_tok_setup():
        import jax, jax.numpy as jnp
        import numpy as np
        from jax import lax
        N_BITS = 4
        PATCH = 16

        def _hilbert_points(p):
            n = 1 << p
            pts = np.zeros((n * n, 2), dtype=np.int32)
            for d in range(n * n):
                t, x, y, s = (d, 0, 0, 1)
                while s < n:
                    rx = 1 & t // 2
                    ry = 1 & (t ^ rx)
                    if ry == 0:
                        if rx == 1:
                            x = s - 1 - x
                            y = s - 1 - y
                        x, y = (y, x)
                    x += s * rx
                    y += s * ry
                    t //= 4
                    s *= 2
                pts[d, 0] = x
                pts[d, 1] = y
            return pts
        _INDEX_MAP = _hilbert_points(N_BITS)
        key = jax.random.key(seed)
        k1, k2 = jax.random.split(key)
        x = jax.random.normal(k1, (128, 3, 64, 64), dtype=jnp.float32)
        W = jax.random.normal(k2, (192, 3, PATCH, PATCH), dtype=jnp.float32) * 0.02
        b = jnp.zeros((192,), dtype=jnp.float32)
        return {'x': x, 'W': W, 'b': b}
    _L0_tok_all = _L0_tok_setup()
    _L0_tok_in = {k: v for k, v in _L0_tok_all.items() if k in ('W', 'b')}
    del _L0_tok_all

    def _L0_attn_setup():
        import jax, jax.numpy as jnp
        import numpy as np

        def depthwise_conv1d(x, w, pad):
            return jax.lax.conv_general_dilated(x, w, window_strides=(1,), padding=[(pad, pad)], dimension_numbers=('NCH', 'OIH', 'NCH'), feature_group_count=x.shape[1])
        key = jax.random.key(seed)
        ks = jax.random.split(key, 6)
        B, L, D, F = (2, 512, 192, 64)
        return {'x': jax.random.normal(ks[0], (B, L, D), jnp.float32), 'w_in': jax.random.normal(ks[1], (D, 4 * D), jnp.float32) * D ** (-0.5), 'b_in': jnp.zeros((4 * D,), jnp.float32), 'w_filt': jax.random.normal(ks[2], (F, D), jnp.float32) * F ** (-0.5), 'b_filt': jnp.zeros((D,), jnp.float32), 'w_short': jax.random.normal(ks[3], (D, 1, 3), jnp.float32) * 0.5, 'b_short': jnp.zeros((D,), jnp.float32), 'w_out': jax.random.normal(ks[4], (D, D), jnp.float32) * D ** (-0.5), 'b_out': jnp.zeros((D,), jnp.float32)}
    _L0_attn_all = _L0_attn_setup()
    _L0_attn_in = {k: v for k, v in _L0_attn_all.items() if k in ('w_in', 'b_in', 'w_filt', 'b_filt', 'w_short', 'b_short', 'w_out', 'b_out')}
    del _L0_attn_all

    def _L0_ffn_setup():
        import jax, jax.numpy as jnp
        import numpy as np
        DIM = 192
        HEADS = 12
        HIDDEN = 768
        E = 8
        TOPK = 2
        EPS = 1e-05

        def _ln(x, g, b):
            m = x.mean(-1, keepdims=True)
            v = jnp.mean((x - m) ** 2, axis=-1, keepdims=True)
            return (x - m) * jax.lax.rsqrt(v + EPS) * g + b
        key = jax.random.key(seed)
        ks = jax.random.split(key, 10)
        s = 0.02
        return {'x': jax.random.normal(ks[0], (8, 256, DIM), jnp.float32), 'ln1_g': jnp.ones((DIM,), jnp.float32), 'ln1_b': jnp.zeros((DIM,), jnp.float32), 'qkv_w': jax.random.normal(ks[1], (DIM, 3 * DIM), jnp.float32) * s, 'proj_w': jax.random.normal(ks[2], (DIM, DIM), jnp.float32) * s, 'proj_b': jnp.zeros((DIM,), jnp.float32), 'ln2_g': jnp.ones((DIM,), jnp.float32), 'ln2_b': jnp.zeros((DIM,), jnp.float32), 'gate_w': jax.random.normal(ks[3], (DIM, E), jnp.float32) * s, 'gate_b': jnp.zeros((E,), jnp.float32), 'w1': jax.random.normal(ks[4], (E, DIM, HIDDEN), jnp.float32) * s, 'b1': jnp.zeros((E, HIDDEN), jnp.float32), 'w2': jax.random.normal(ks[5], (E, HIDDEN, DIM), jnp.float32) * s, 'b2': jnp.zeros((E, DIM), jnp.float32)}
    _L0_ffn_all = _L0_ffn_setup()
    _L0_ffn_in = {k: v for k, v in _L0_ffn_all.items() if k in ('ln1_g', 'ln1_b', 'qkv_w', 'proj_w', 'proj_b', 'ln2_g', 'ln2_b', 'gate_w', 'gate_b', 'w1', 'b1', 'w2', 'b2')}
    del _L0_ffn_all
    return {'x': x, 'txt': txt, 'L0_tok_W': _L0_tok_in['W'], 'L0_tok_b': _L0_tok_in['b'], 'L0_attn_w_in': _L0_attn_in['w_in'], 'L0_attn_b_in': _L0_attn_in['b_in'], 'L0_attn_w_filt': _L0_attn_in['w_filt'], 'L0_attn_b_filt': _L0_attn_in['b_filt'], 'L0_attn_w_short': _L0_attn_in['w_short'], 'L0_attn_b_short': _L0_attn_in['b_short'], 'L0_attn_w_out': _L0_attn_in['w_out'], 'L0_attn_b_out': _L0_attn_in['b_out'], 'L0_ffn_ln1_g': _L0_ffn_in['ln1_g'], 'L0_ffn_ln1_b': _L0_ffn_in['ln1_b'], 'L0_ffn_qkv_w': _L0_ffn_in['qkv_w'], 'L0_ffn_proj_w': _L0_ffn_in['proj_w'], 'L0_ffn_proj_b': _L0_ffn_in['proj_b'], 'L0_ffn_ln2_g': _L0_ffn_in['ln2_g'], 'L0_ffn_ln2_b': _L0_ffn_in['ln2_b'], 'L0_ffn_gate_w': _L0_ffn_in['gate_w'], 'L0_ffn_gate_b': _L0_ffn_in['gate_b'], 'L0_ffn_w1': _L0_ffn_in['w1'], 'L0_ffn_b1': _L0_ffn_in['b1'], 'L0_ffn_w2': _L0_ffn_in['w2'], 'L0_ffn_b2': _L0_ffn_in['b2']}

def reference(x, txt, L0_tok_W, L0_tok_b, L0_attn_w_in, L0_attn_b_in, L0_attn_w_filt, L0_attn_b_filt, L0_attn_w_short, L0_attn_b_short, L0_attn_w_out, L0_attn_b_out, L0_ffn_ln1_g, L0_ffn_ln1_b, L0_ffn_qkv_w, L0_ffn_proj_w, L0_ffn_proj_b, L0_ffn_ln2_g, L0_ffn_ln2_b, L0_ffn_gate_w, L0_ffn_gate_b, L0_ffn_w1, L0_ffn_b1, L0_ffn_w2, L0_ffn_b2):
    import jax
    import jax.numpy as jnp

    def _L0_tok_ref(x, W, b):
        import jax, jax.numpy as jnp
        import numpy as np
        from jax import lax
        N_BITS = 4
        PATCH = 16

        def _hilbert_points(p):
            n = 1 << p
            pts = np.zeros((n * n, 2), dtype=np.int32)
            for d in range(n * n):
                t, x, y, s = (d, 0, 0, 1)
                while s < n:
                    rx = 1 & t // 2
                    ry = 1 & (t ^ rx)
                    if ry == 0:
                        if rx == 1:
                            x = s - 1 - x
                            y = s - 1 - y
                        x, y = (y, x)
                    x += s * rx
                    y += s * ry
                    t //= 4
                    s *= 2
                pts[d, 0] = x
                pts[d, 1] = y
            return pts
        _INDEX_MAP = _hilbert_points(N_BITS)
        y = lax.conv_general_dilated(x, W, window_strides=(PATCH, PATCH), padding='VALID', dimension_numbers=('NCHW', 'OIHW', 'NCHW'))
        y = y + b[None, :, None, None]
        ix = jnp.asarray(_INDEX_MAP[:, 0])
        iy = jnp.asarray(_INDEX_MAP[:, 1])
        flat = y[:, :, ix, iy]
        return jnp.transpose(flat, (0, 2, 1))

    def _L0_attn_ref(x, w_in, b_in, w_filt, b_filt, w_short, b_short, w_out, b_out):
        import jax, jax.numpy as jnp
        import numpy as np

        def depthwise_conv1d(x, w, pad):
            return jax.lax.conv_general_dilated(x, w, window_strides=(1,), padding=[(pad, pad)], dimension_numbers=('NCH', 'OIH', 'NCH'), feature_group_count=x.shape[1])
        B, L, D = x.shape
        F = w_filt.shape[0]
        x_short = depthwise_conv1d(x.transpose(0, 2, 1), w_short, 1).transpose(0, 2, 1) + b_short
        proj = x @ w_in + b_in
        x_proj, z_proj, v1, v2 = jnp.split(proj, 4, axis=-1)
        z = jax.nn.silu(z_proj)
        t = jnp.arange(L, dtype=jnp.float32)[:, None]
        f = jnp.arange(F, dtype=jnp.float32)[None, :]
        pos_basis = jnp.sin(t * f / F)
        filt = (pos_basis @ w_filt + b_filt).T
        conv = depthwise_conv1d(x_proj.transpose(0, 2, 1), filt[:, None, :], L // 2)[:, :, :L]
        y = conv.transpose(0, 2, 1) * v1 * v2 * z
        return (y + x_short) @ w_out + b_out

    def _L0_ffn_ref(x, ln1_g, ln1_b, qkv_w, proj_w, proj_b, ln2_g, ln2_b, gate_w, gate_b, w1, b1, w2, b2):
        import jax, jax.numpy as jnp
        import numpy as np
        DIM = 192
        HEADS = 12
        HIDDEN = 768
        E = 8
        TOPK = 2
        EPS = 1e-05

        def _ln(x, g, b):
            m = x.mean(-1, keepdims=True)
            v = jnp.mean((x - m) ** 2, axis=-1, keepdims=True)
            return (x - m) * jax.lax.rsqrt(v + EPS) * g + b
        B, S, D = x.shape
        hd = D // HEADS
        h = _ln(x, ln1_g, ln1_b)
        qkv = (h @ qkv_w).reshape(B, S, 3, HEADS, hd).transpose(2, 0, 3, 1, 4)
        q, k, v = (qkv[0], qkv[1], qkv[2])
        att = jax.nn.softmax(jnp.einsum('bhqd,bhkd->bhqk', q, k) * hd ** (-0.5), axis=-1)
        o = jnp.einsum('bhqk,bhkd->bhqd', att, v).transpose(0, 2, 1, 3).reshape(B, S, D)
        x = x + o @ proj_w + proj_b
        h2 = _ln(x, ln2_g, ln2_b).reshape(B * S, D)
        logits = h2 @ gate_w + gate_b
        wts, sel = jax.lax.top_k(logits, TOPK)
        wts = jax.nn.softmax(wts.astype(jnp.float32), axis=-1).astype(x.dtype)
        cw = (jax.nn.one_hot(sel, E, dtype=x.dtype) * wts[..., None]).sum(axis=1)
        res = jnp.zeros_like(h2)
        for e in range(E):
            he = jax.nn.gelu(h2 @ w1[e] + b1[e], approximate=False)
            res = res + cw[:, e:e + 1] * (he @ w2[e] + b2[e])
        return x + res.reshape(B, S, D)
    h = _L0_tok_ref(x, L0_tok_W, L0_tok_b)
    h = jnp.concatenate([h, txt], axis=1)
    h = h + _L0_attn_ref(_layernorm(h, axis=-1), L0_attn_w_in, L0_attn_b_in, L0_attn_w_filt, L0_attn_b_filt, L0_attn_w_short, L0_attn_b_short, L0_attn_w_out, L0_attn_b_out)
    h = h + _L0_ffn_ref(_layernorm(h, axis=-1), L0_ffn_ln1_g, L0_ffn_ln1_b, L0_ffn_qkv_w, L0_ffn_proj_w, L0_ffn_proj_b, L0_ffn_ln2_g, L0_ffn_ln2_b, L0_ffn_gate_w, L0_ffn_gate_b, L0_ffn_w1, L0_ffn_b1, L0_ffn_w2, L0_ffn_b2)
    return h

_drawn_inputs = setup_inputs


def setup_inputs(seed=0):
    import zlib

    import numpy as np

    out = dict(_drawn_inputs(seed))
    spreads = {'L0_tok_b': (0.0, 0.1),
     'L0_attn_b_in': (0.0, 0.1),
     'L0_attn_b_filt': (0.0, 0.1),
     'L0_attn_b_short': (0.0, 0.8),
     'L0_attn_b_out': (0.0, 0.8),
     'L0_ffn_ln1_g': (1.0, 0.6),
     'L0_ffn_ln1_b': (0.0, 0.8),
     'L0_ffn_proj_b': (0.0, 0.8),
     'L0_ffn_ln2_g': (1.0, 0.6),
     'L0_ffn_ln2_b': (0.0, 0.8),
     'L0_ffn_gate_b': (0.0, 0.8),
     'L0_ffn_b1': (0.0, 0.8),
     'L0_ffn_b2': (0.0, 0.8)}
    factors = {'L0_ffn_qkv_w': 8.0,
     'L0_ffn_proj_w': 8.0,
     'L0_ffn_gate_w': 8.0,
     'L0_ffn_w1': 8.0,
     'L0_ffn_w2': 8.0}
    for name, (base, spread) in spreads.items():
        noise = np.random.default_rng([zlib.crc32(name.encode()), seed]).standard_normal(out[name].shape)
        drawn = base * np.exp(spread * noise) if base else spread * noise
        out[name] = jnp.asarray(drawn.astype(out[name].dtype))
    for name, factor in factors.items():
        out[name] = (out[name] * factor).astype(out[name].dtype)
    return out
```

```python
from contextlib import ExitStack

import numpy as np

import concourse.bass as bass
from concourse import mybir

F32 = mybir.dt.float32
BF16 = mybir.dt.bfloat16
U32 = mybir.dt.uint32
I32 = mybir.dt.int32
ALU = mybir.AluOpType
ACT = mybir.ActivationFunctionType
AX = mybir.AxisListType

P = 128
B, C, IMG, PATCH, D = 8, 3, 96, 16, 192
GRID = IMG // PATCH
NPATCH = GRID * GRID
N_IMG, N_TXT = 256, 512
S = N_IMG + N_TXT
TB = S // P
NT = B * TB
T_IMG = N_IMG // P
KPATCH = C * PATCH * PATCH
KP = KPATCH // P
HALF = D // 2
FREQ = 64
EPS = 1e-5
CH = 16
NCHUNK = D // CH
TG = 4
TROW = 384
HB = TB // 2
HEADS, HD = 12, 16
GH = 4
NG = HEADS // GH
QH = S // 2
SPLIT = 6 * HD
AUG = 3
KROWS = SPLIT + AUG
VW = HD + 1
E, TOPK, HID = 8, 2, 768
KH = HID // P
NSLOT = NT * TOPK + E
SLOTS = NSLOT * P


def hilbert_points(p):
    n = 1 << p
    pts = np.zeros((n * n, 2), dtype=np.int32)
    for d in range(n * n):
        t, x, y, s = d, 0, 0, 1
        while s < n:
            rx = 1 & t // 2
            ry = 1 & (t ^ rx)
            if ry == 0:
                if rx == 1:
                    x, y = s - 1 - x, s - 1 - y
                x, y = y, x
            x, y = x + s * rx, y + s * ry
            t //= 4
            s *= 2
        pts[d] = x, y
    return pts


def shape_tables():
    f32 = np.float32
    f = np.arange(FREQ, dtype=np.float64)
    taps = np.r_[np.arange(S - P + 1, S), np.arange(P)].astype(np.float64)
    basis = np.ones((FREQ + 1, len(taps)))
    basis[:FREQ] = np.sin(f[:, None] * taps[None, :] / FREQ)
    s = np.arange(S, dtype=np.float64)
    phi = np.concatenate([np.sin(s[:, None] * f / FREQ), np.cos(s[:, None] * f / FREQ)], 1)
    u = s - S // 2
    psi = np.concatenate([np.cos(f[:, None] * u / FREQ), -np.sin(f[:, None] * u / FREQ)], 0)
    psi[FREQ] = 1.0
    pts = np.minimum(hilbert_points(4), GRID - 1)
    pick = np.zeros((2 * NPATCH, 2, T_IMG, P))
    for d in range(N_IMG):
        for r in range(2):
            pick[r * NPATCH + pts[d, 0] * GRID + pts[d, 1], r, d // P, d % P] = 1.0
    return {
        "basis": basis.astype(f32),
        "phi": phi.reshape(TB, P, 2 * FREQ).transpose(1, 0, 2).astype(f32).copy(),
        "psi": psi.reshape(2 * FREQ, TB, P).astype(f32).copy(),
        "pick": pick.astype(f32).reshape(2 * NPATCH, 2 * T_IMG * P),
        "ident": np.eye(P, dtype=f32),
        "steps": np.broadcast_to(np.arange(NSLOT, dtype=f32), (P, NSLOT)),
        "ids": (np.arange(P)[:, None, None] + P * np.arange(NT)[None, :, None] + NT * P * np.arange(TOPK)).astype(f32),
        "spare": (TOPK * NT * P + np.arange(SLOTS)).reshape(NSLOT // 8, P, 8).transpose(1, 0, 2).astype(f32),
        "before": np.triu(np.ones((P, P), f32), 1),
    }


def col(n, width):
    return bass.ds(n * width, width)


class Core:

    def __init__(self, nc, a, out, ctx):
        self.nc, self.a, self.out, self.ctx = nc, a, out, ctx

        def sb(name, shape, dt=F32):
            return ctx.enter_context(nc.sbuf_tensor(name, shape, dt))

        self.H = sb("h_resid", [P, NT * D])
        self.XA = sb("x_proj_then_x", [P, NT * D])
        self.GY = sb("gate_then_w2", [P, NT * D])
        self.XS = sb("short_then_w1", [P, NT * P * 2])
        self.ident = sb("ident", [P, P])
        self.stats = sb("ln_stats", [P, NT * 6])
        self.mean = sb("ln_mean", [P, NT])
        self.var = sb("ln_var", [P, NT])
        self.dif = sb("ln_dif", [P, NT])
        self.rstd = sb("rstd", [P, NT])
        self.powers = sb("minus_half", [P, NT])
        self.ps = ctx.enter_context(nc.psum_tensor("ps", [P, 8, 512], F32))
        self.filt_dram = nc.dram_tensor("filt_rows", (D, TROW), F32, kind="Internal").ap()
        self.slot_x = nc.dram_tensor("slot_x", (SLOTS, D + 1), F32, kind="Internal").ap()
        self.tok_y = nc.dram_tensor("tok_y", (TOPK * NT * P + SLOTS, D), F32, kind="Internal").ap()
        self.weight = sb("expert_weight", [P, TOPK, NT])
        self.b2 = sb("expert_b2", [P, E, D])
        self.tile_expert = sb("tile_expert", [P, NSLOT], I32)
        self.W1 = self.XS[0:HALF + 1, :].rearrange("p (e c n) -> p e c n", e=E, c=2)
        self.W2 = self.GY[:, :].rearrange("p (e j n) -> p e j n", e=E, j=KH)


def rsqrt_on_pool(nc, pool, core, var_set, step, rstd_set):
    pool.wait_ge(var_set, 1)
    nc.gpsimd.tensor_scalar(core.rstd[:, :], core.var[:, :], EPS, None, ALU.add).then_inc(step, 1)
    pool.wait_ge(step, 1)
    nc.gpsimd.tensor_tensor(core.rstd[:, :], core.rstd[:, :], core.powers[:, :], ALU.pow).then_inc(rstd_set, 1)


def all_stats(nc, dve, core, src, st_set):
    with dve.Fori(0, NT) as n:
        nc.vector.bn_stats(core.stats[:, col(n, 6)], src[:, col(n, D)]).then_inc(st_set, 1)


def mean_and_var(nc, dve, core, st_set, step, var_set):
    st = core.stats[:, :].rearrange("p (n k) -> p n k", k=6)
    even, odd, sq_even, sq_odd = st[:, :, 1], st[:, :, 4], st[:, :, 2], st[:, :, 5]
    dve.wait_ge(st_set, NT)
    nc.vector.tensor_tensor(core.mean[:, :], even, odd, ALU.add).then_inc(step, 1)
    nc.vector.tensor_tensor(core.dif[:, :], even, odd, ALU.subtract).then_inc(step, 1)
    nc.vector.tensor_tensor(core.var[:, :], sq_even, sq_odd, ALU.add).then_inc(step, 1)
    dve.wait_ge(step, 3)
    nc.vector.tensor_scalar(core.mean[:, :], core.mean[:, :], 0.5, None, ALU.mult).then_inc(step, 1)
    nc.vector.scalar_tensor_tensor(core.dif[:, :], core.dif[:, :], 0.25, core.dif[:, :], ALU.mult, ALU.mult).then_inc(step, 1)
    dve.wait_ge(step, 5)
    nc.vector.scalar_tensor_tensor(core.var[:, :], core.var[:, :], 1.0 / D, core.dif[:, :], ALU.mult, ALU.add).then_inc(var_set, 1)


def embed_phase(core):
    nc, a, H, ps = core.nc, core.a, core.H, core.ps
    with ExitStack() as ctx:
        def sb(name, shape, dt=F32):
            return ctx.enter_context(nc.sbuf_tensor(name, shape, dt))

        def sem(name):
            return ctx.enter_context(nc.semaphore(name))

        patches = sb("patches", [P, KP * B * NPATCH])
        wtok = sb("wtok", [P, KP * D])
        tokb = sb("tokb", [2 * NPATCH, D])
        emb = sb("emb", [2 * NPATCH, 4 * D])
        pick = sb("pick", [2 * NPATCH, 2 * T_IMG * P])
        basis = sb("basis", [FREQ + 1, 2 * P - 1])
        wfilt = sb("wfilt_bias", [FREQ + 1, D])
        rows = sb("filter_rows", [HALF, 2, TROW])
        empty = sb("empty_slots", [P, 2, 8, D + 1])
        spare = sb("spare_rows", [P, NSLOT // 8, 8])
        filt_in, tok_in, pick_in, txt_in = sem("e_filt_in"), sem("e_tok_in"), sem("e_pick_in"), sem("e_txt_in")
        filt_mm, rows_set, rows_zero, rows_out = sem("e_filt_mm"), sem("e_rows_set"), sem("e_rows_zero"), sem("e_rows_out")
        emb_mm, emb_set, tok_mm, tok_set = sem("e_emb_mm"), sem("e_emb_set"), sem("e_tok_mm"), sem("e_tok_set")
        st_set, dve_step, var_set, pool_step, rstd_set = sem("e_st_set"), sem("e_dve_step"), sem("e_var_set"), sem("e_pool_step"), sem("e_rstd_set")
        powers_set = sem("e_powers_set")
        spare_in, zero_set, spare_set, empty_out = sem("e_spare_in"), sem("e_zero_set"), sem("e_spare_set"), [sem(f"e_empty_out{u}") for u in range(2)]
        h_tiles = H[:, :].rearrange("p (b i c) -> p b i c", b=B, i=TB)
        with nc.Block() as block:
            @block.sync
            def _(sp):
                sp.dma_start(wfilt[0:FREQ, :], a["w_filt"]).then_inc(filt_in, 16)
                sp.dma_start(wfilt[FREQ:FREQ + 1, :], a["b_filt"].rearrange("(a c) -> a c", a=1)).then_inc(filt_in, 16)
                sp.dma_start(basis[:, :], a["basis"]).then_inc(filt_in, 16)
                sp.dma_start(wtok[:, :], a["wtok"]).then_inc(tok_in, 16)
                sp.dma_start(patches[:, :], a["patches"]).then_inc(tok_in, 16)
                sp.dma_start(tokb[:, :], a["tok_b"].rearrange("(a c) -> a c", a=1).broadcast_to((2 * NPATCH, D))).then_inc(tok_in, 16)
                sp.dma_start(pick[:, :], a["pick"]).then_inc(pick_in, 16)
                sp.dma_start(spare[:, :, :], a["spare"]).then_inc(spare_in, 16)
                for k in range(NSLOT // 8):
                    sp.wait_ge(spare_set, k + 1)
                    sp.dma_start(core.slot_x[k * 8 * P:(k + 1) * 8 * P, :].rearrange("(p r) c -> p r c", r=8),
                                 empty[:, k % 2, :, :]).then_inc(empty_out[k % 2], 16)
                sp.wait_ge(rows_out, 16)
                for u in range(2):
                    sp.wait_ge(empty_out[u], 16 * ((NSLOT // 8 + 1 - u) // 2))

            @block.scalar
            def _(act):
                act.dma_start(core.ident[:, :], a["ident"]).then_inc(pick_in, 16)
                for b in range(B):
                    act.dma_start(h_tiles[:, b, T_IMG:TB, :], a["txt"][b].rearrange("(i p) c -> p i c", p=P)).then_inc(txt_in, 16)
                act.wait_ge(rows_set, 2)
                act.dma_start(core.filt_dram.rearrange("(h c) t -> c h t", h=2), rows[:, :, :]).then_inc(rows_out, 16)

            @block.gpsimd
            def _(pool):
                nc.gpsimd.memset(rows[:, :, :], 0.0).then_inc(rows_zero, 1)
                nc.gpsimd.memset(core.powers[:, :], -0.5).then_inc(powers_set, 1)
                nc.gpsimd.memset(empty[:, :, :, :], 0.0).then_inc(zero_set, 1)
                pool.wait_ge(zero_set, 1)
                pool.wait_ge(spare_in, 16)
                for k in range(NSLOT // 8):
                    if k >= 2:
                        pool.wait_ge(empty_out[k % 2], 16 * (k // 2))
                    nc.gpsimd.tensor_copy(empty[:, k % 2, :, D], spare[:, k, :]).then_inc(spare_set, 1)
                pool.wait_ge(powers_set, 1)
                rsqrt_on_pool(nc, pool, core, var_set, pool_step, rstd_set)
                pool.wait_ge(rstd_set, 1)

            @block.tensor
            def _(pe):
                pe.wait_ge(filt_in, 48)
                for h in range(2):
                    nc.tensor.matmul(ps[0:HALF, h, 0:2 * P - 1], wfilt[:, h * HALF:(h + 1) * HALF], basis[:, :],
                                     start=True, stop=True).then_inc(filt_mm, 1)
                pe.wait_ge(tok_in, 48)
                for m in range(4):
                    for k in range(KP):
                        off = k * B * NPATCH + m * 2 * NPATCH
                        last = nc.tensor.matmul(ps[0:2 * NPATCH, 2 + m % 2, 0:D], patches[:, off:off + 2 * NPATCH],
                                                wtok[:, k * D:(k + 1) * D], start=(k == 0), stop=(k == KP - 1))
                    last.then_inc(emb_mm, 1)
                    if m >= 1:
                        pe.wait_ge(emb_set, m)
                pe.wait_ge(emb_set, 4)
                pe.wait_ge(pick_in, 32)
                for t in range(B * T_IMG):
                    b, i = t // T_IMG, t % T_IMG
                    m, r = b // 2, b % 2
                    if t >= 4:
                        pe.wait_ge(tok_set, t - 3)
                    off = (r * T_IMG + i) * P
                    nc.tensor.matmul(ps[:, 4 + t % 4, 0:D], pick[:, off:off + P], emb[:, m * D:(m + 1) * D],
                                     start=True, stop=True).then_inc(tok_mm, 1)

            @block.vector
            def _(dve):
                dve.wait_ge(rows_zero, 1)
                for h in range(2):
                    dve.wait_ge(filt_mm, h + 1)
                    nc.vector.tensor_copy(rows[:, h, 0:P - 1], ps[0:HALF, h, 0:P - 1])
                    nc.vector.tensor_copy(rows[:, h, 2 * P - 1:3 * P - 1], ps[0:HALF, h, P - 1:2 * P - 1]).then_inc(rows_set, 1)
                for m in range(4):
                    dve.wait_ge(emb_mm, m + 1)
                    nc.vector.tensor_tensor(emb[:, m * D:(m + 1) * D], ps[0:2 * NPATCH, 2 + m % 2, 0:D], tokb[:, :],
                                            ALU.add).then_inc(emb_set, 1)
                for t in range(B * T_IMG):
                    b, i = t // T_IMG, t % T_IMG
                    dve.wait_ge(tok_mm, t + 1)
                    nc.vector.tensor_copy(h_tiles[:, b, i, :], ps[:, 4 + t % 4, 0:D]).then_inc(tok_set, 1)
                dve.wait_ge(tok_set, B * T_IMG)
                dve.wait_ge(txt_in, 16 * B)
                all_stats(nc, dve, core, H, st_set)
                mean_and_var(nc, dve, core, st_set, dve_step, var_set)


def project_phase(core):
    nc, a, H, ps = core.nc, core.a, core.H, core.ps
    with ExitStack() as ctx:
        def sb(name, shape, dt=F32):
            return ctx.enter_context(nc.sbuf_tensor(name, shape, dt))

        def sem(name):
            return ctx.enter_context(nc.semaphore(name))

        w_in = sb("w_in", [HALF + 1, 2, 4 * D])
        hn = sb("hn", [P, 2, D])
        hnT = sb("hnT", [HALF + 1, 2, S + 2])
        sz = sb("silu_z", [P, 2, D])
        szv = sb("silu_z_v1", [P, 2, D])
        wsh = sb("w_short", [HALF, 2, 4])
        w_ready, hn_set, t_ready, hnT_set = sem("p_w_ready"), sem("p_hn_set"), sem("p_t_ready"), sem("p_hnT_set")
        zx_ready, zx_free, sz_set, szv_set, g_set = sem("p_zx_ready"), sem("p_zx_free"), sem("p_sz_set"), sem("p_szv_set"), sem("p_g_set")
        edges, xs_step, xs_set = sem("p_edges"), sem("p_xs_step"), sem("p_xs_set")
        XS = core.XS[0:HALF, :].rearrange("p (c t) -> p c t", c=2)
        with nc.Block() as block:
            @block.sync
            def _(sp):
                sp.dma_start(w_in[0:HALF, :, :], a["w_in"].rearrange("(c k) n -> k c n", c=2)).then_inc(w_ready, 16)
                sp.dma_start(w_in[HALF:HALF + 1, 1, :], a["b_in"].rearrange("(a c) -> a c", a=1)).then_inc(w_ready, 16)
                sp.dma_start(wsh[:, :, :], a["short"].rearrange("(c k) t -> k c t", c=2)).then_inc(w_ready, 16)

            @block.gpsimd
            def _(pool):
                nc.gpsimd.memset(hnT[HALF:HALF + 1, :, :], 1.0).then_inc(edges, 1)
                nc.gpsimd.memset(hnT[0:HALF, :, 0:1], 0.0).then_inc(edges, 1)
                nc.gpsimd.memset(hnT[0:HALF, :, S + 1:S + 2], 0.0).then_inc(edges, 1)

            @block.vector
            def _(dve):
                def norm(n, u):
                    nc.vector.tensor_scalar(hn[:, u, :], H[:, col(n, D)], core.mean[:, bass.ds(n, 1)],
                                            core.rstd[:, bass.ds(n, 1)], ALU.subtract, ALU.mult).then_inc(hn_set, 1)

                def gate(n, u):
                    dve.wait_ge(sz_set, n + 1)
                    nc.vector.tensor_tensor(szv[:, u, :], sz[:, u, :], ps[:, 2 + u, D:2 * D], ALU.mult).then_inc(szv_set, 1)
                    dve.wait_ge(szv_set, n + 1)
                    nc.vector.tensor_tensor(core.GY[:, col(n, D)], szv[:, u, :], ps[:, 4 + u, 0:D], ALU.mult).then_inc(g_set, 1)

                def batch(b, last):
                    for i in range(TB):
                        n, u = b * TB + i, i % 2
                        if not (last and i == TB - 1):
                            norm(n + 1, 1 - u)
                        dve.wait_ge(t_ready, n + 1)
                        nc.vector.tensor_copy(hnT[0:HALF, :, 1 + i * P:1 + (i + 1) * P],
                                              ps[0:HALF, u, 0:2 * P].rearrange("p (c t) -> p c t", c=2)).then_inc(hnT_set, 1)
                        if i > 0:
                            gate(n - 1, 1 - u)
                    dve.wait_ge(hnT_set, b * TB + TB)
                    for c in range(2):
                        out = XS[:, c, bass.ds(b * S, S)]
                        nc.vector.tensor_scalar(out, hnT[0:HALF, c, 0:S], wsh[:, c, 0:1], wsh[:, c, 3:4],
                                                ALU.mult, ALU.add).then_inc(xs_step, 1)
                    for k in (1, 2):
                        for c in range(2):
                            out = XS[:, c, bass.ds(b * S, S)]
                            dve.wait_ge(xs_step, b * 6 + (2 * k + c - 1))
                            nc.vector.scalar_tensor_tensor(out, hnT[0:HALF, c, k:k + S], wsh[:, c, k:k + 1], out,
                                                           ALU.mult, ALU.add).then_inc(xs_step, 1)
                    gate(b * TB + TB - 1, 1)

                dve.wait_ge(w_ready, 48)
                dve.wait_ge(edges, 3)
                norm(0, 0)
                with dve.Fori(0, B - 1) as b:
                    batch(b, False)
                batch(B - 1, True)

            @block.tensor
            def _(pe):
                def transpose(n, u):
                    pe.wait_ge(hn_set, n + 1)
                    for c in range(2):
                        last = nc.tensor.transpose(ps[0:HALF, u, c * P:(c + 1) * P], hn[:, u, c * HALF:(c + 1) * HALF], core.ident[:, :])
                    last.then_inc(t_ready, 1)

                def batch(b, last):
                    for i in range(TB):
                        n, u = b * TB + i, i % 2
                        if not (last and i == TB - 1):
                            transpose(n + 1, 1 - u)
                        pe.wait_ge(hnT_set, n + 1)
                        pe.wait_ge(zx_free, n + 1)
                        t = slice(1 + i * P, 1 + (i + 1) * P)
                        for bank, at, c0, w in ((2, 0, D, 2 * D), (4, 0, 3 * D, D), (4, D, 0, D)):
                            nc.tensor.matmul(ps[:, bank + u, at:at + w], hnT[0:HALF, 0, t], w_in[0:HALF, 0, c0:c0 + w], start=True, stop=False)
                            mm = nc.tensor.matmul(ps[:, bank + u, at:at + w], hnT[:, 1, t], w_in[:, 1, c0:c0 + w], start=False, stop=True)
                        mm.then_inc(zx_ready, 1)

                pe.wait_ge(w_ready, 48)
                pe.wait_ge(edges, 3)
                transpose(0, 0)
                with pe.Fori(0, B - 1) as b:
                    batch(b, False)
                batch(B - 1, True)

            @block.scalar
            def _(act):
                act.sem_inc(zx_free, 2)

                def silu(n, u):
                    act.wait_ge(zx_ready, n + 1)
                    nc.scalar.activation(sz[:, u, :], ps[:, 2 + u, 0:D], ACT.Silu).then_inc(sz_set, 1)

                def keep_x(n, u):
                    act.wait_ge(g_set, n + 1)
                    nc.scalar.activation(core.XA[:, col(n, D)], ps[:, 4 + u, D:2 * D], ACT.Copy).then_inc(zx_free, 1)

                silu(0, 0)
                with act.Fori(0, B - 1) as b:
                    for i in range(TB):
                        silu(b * TB + (i + 1), (i + 1) % 2)
                        keep_x(b * TB + i, i % 2)
                for n in range(NT - TB, NT):
                    if n + 1 < NT:
                        silu(n + 1, (n + 1) % 2)
                    keep_x(n, n % 2)


def conv_phase(core):
    nc, a, ps = core.nc, core.a, core.ps
    with ExitStack() as ctx:
        def sb(name, shape, dt=F32):
            return ctx.enter_context(nc.sbuf_tensor(name, shape, dt))

        def sem(name):
            return ctx.enter_context(nc.semaphore(name))

        phi = sb("phi", [P, TB, P])
        psi = sb("psi", [P, TB, P])
        wf = sb("w_features", [P, D])
        toep = sb("toeplitz", [P, TG, TG, 2 * P])
        xc = sb("x_chunk", [P, CH, 2, 32])
        zw = sb("weighted_features", [P, TB, CH, B])
        edge = sb("edge_rows", [P, 2, TG, P])
        tab_in, xc_zero, xc_set, xc_free = sem("c_tab_in"), sem("c_xc_zero"), sem("c_xc_set"), sem("c_xc_free")
        toep_in = [sem(f"c_toep_in{g}") for g in range(TG)]
        toep_free = sem("c_toep_free")
        z_ready, zw_set, edge_mm, edge_set = sem("c_z_ready"), sem("c_zw_set"), sem("c_edge_mm"), sem("c_edge_set")
        y_ready, y_set, y_free = sem("c_y_ready"), sem("c_y_set"), sem("c_y_free")
        x4 = core.XA[:, :].rearrange("p (b i c) -> p b i c", b=B, i=TB)
        g4 = core.GY[:, :].rearrange("p (b i c) -> p b i c", b=B, i=TB)
        CHAINS = [(0, (0, 1, 2), 0), (1, (5, 4, 3), 5), (0, (3,), 1), (1, (2,), 4), (0, (4,), 2), (1, (1,), 3)]
        with nc.Block() as block:
            @block.sync
            def _(sp):
                sp.dma_start(phi[:, :, :], a["phi"]).then_inc(tab_in, 16)
                sp.dma_start(psi[:, :, :], a["psi"]).then_inc(tab_in, 16)
                sp.dma_start(wf[0:FREQ, :], a["w_filt"]).then_inc(tab_in, 16)
                sp.dma_start(wf[FREQ + 1:P, :], a["w_filt"][1:FREQ, :]).then_inc(tab_in, 16)
                sp.dma_start(wf[FREQ:FREQ + 1, :], a["b_filt"].rearrange("(a c) -> a c", a=1)).then_inc(tab_in, 16)
                with sp.Fori(0, NCHUNK) as q:
                    for g in range(TG):
                        sp.wait_ge(toep_free, q * TG + (g + 1))
                        rows = core.filt_dram[bass.ds(q * CH + g * TG, TG), 0:2 * P]
                        src = bass.AP(rows.tensor, rows.offset, [[1, P], [TROW, TG], [1, 2 * P]])
                        sp.dma_start(toep[:, g, :, :], src).then_inc(toep_in[g], 16)

            @block.gpsimd
            def _(pool):
                nc.gpsimd.memset(xc[:, :, :, :], 0.0).then_inc(xc_zero, 1)
                pool.wait_ge(xc_zero, 1)
                with pool.Fori(0, NCHUNK) as q:
                    pool.wait_ge(xc_free, q + 1)
                    for half in range(2):
                        src = x4[:, :, HB * (1 - half):HB * (2 - half), bass.ds(q * CH, CH)].rearrange("p b i c -> p c i b")
                        dst = xc[:, :, half, 0:HB * B].rearrange("p c (i b) -> p c i b", i=HB)
                        nc.gpsimd.tensor_copy(dst, src).then_inc(xc_set, 1)

            @block.tensor
            def _(pe):
                pe.sem_inc(toep_free, TG)
                pe.sem_inc(xc_free, 1)
                pe.wait_ge(tab_in, 80)
                with pe.Fori(0, NCHUNK) as q:
                    for k, (bank, blocks, out) in enumerate(CHAINS):
                        if k >= 2:
                            pe.wait_ge(zw_set, q * 6 + (k - 1))
                        else:
                            pe.wait_ge(y_free, q * 2 + (k + 1))
                        for j in blocks:
                            mm = nc.tensor.matmul(ps[:, bank, 0:B * CH], phi[:, j, :], x4[:, :, j, bass.ds(q * CH, CH)],
                                                  start=(k < 2 and j == blocks[0]), stop=True, skip_group_check=True)
                        mm.then_inc(z_ready, 1)
                    pe.wait_ge(xc_set, q * 2 + 2)
                    pe.wait_ge(edge_set, q * 2 + 2)
                    for g in range(TG):
                        pe.wait_ge(toep_in[g], (q + 1) * 16)
                        for half in range(2):
                            for j in range(TG):
                                mm = nc.tensor.matmul(ps[32 * j:32 * j + 32, 2 + half, g * P:(g + 1) * P], xc[:, g * TG + j, half, :],
                                                      toep[:, g, j, half * P:(half + 1) * P], start=True, stop=True)
                        mm.then_inc(toep_free, 1)
                    pe.wait_ge(toep_free, q * TG + 2 * TG)
                    pe.sem_inc(xc_free, 1)
                    pe.sem_inc(edge_mm, 1)
                    for half in range(2):
                        for i in range(HB):
                            out = half * HB + i
                            k = [c[2] for c in CHAINS].index(out)
                            pe.wait_ge(zw_set, q * 6 + (k + 1))
                            dst = ps[:, 4 + half, :].rearrange("p (c k) -> p c k", k=32)[:, :, i * B:(i + 1) * B]
                            nc.tensor.matmul(dst, psi[:, out, :], zw[:, out, :, :], start=(i == 0), stop=True, skip_group_check=True)
                        pe.wait_ge(edge_set, q * 2 + (half + 3))
                        for g in range(TG):
                            mm = nc.tensor.matmul(ps[:, 4 + half, g * P:(g + 1) * P], edge[:, half, g, :], core.ident[:, :],
                                                  start=False, stop=True, skip_group_check=True)
                        mm.then_inc(y_ready, 1)

            @block.scalar
            def _(act):
                act.sem_inc(edge_set, 2)
                with act.Fori(0, NCHUNK) as q:
                    act.wait_ge(edge_mm, q + 1)
                    for half in range(2):
                        act.wait_ge(y_free, q * 2 + (half + 1))
                        src = ps[:, 2 + half, :].rearrange("p (g t) -> p g t", g=TG)[:, :, ::-1]
                        nc.scalar.activation(edge[:, half, :, :], src, ACT.Copy).then_inc(edge_set, 1)

            @block.vector
            def _(dve):
                dve.sem_inc(y_free, 2)
                dve.wait_ge(tab_in, 80)
                with dve.Fori(0, NCHUNK) as q:
                    for k, (bank, _, out) in enumerate(CHAINS):
                        dve.wait_ge(z_ready, q * 6 + (k + 1))
                        dst = zw[:, out, :, :].rearrange("p c b -> p b c")
                        src = ps[:, bank, 0:B * CH].rearrange("p (b c) -> p b c", b=B)
                        w = wf[:, bass.ds(q * CH, CH)].rearrange("p (a c) -> p a c", a=1).broadcast_to((P, B, CH))
                        nc.vector.tensor_tensor(dst, src, w, ALU.mult).then_inc(zw_set, 1)
                    for half in range(2):
                        dve.wait_ge(y_ready, q * 2 + (half + 1))
                        src = ps[:, 4 + half, :].rearrange("p (c k) -> p c k", k=32)[:, :, 0:HB * B]
                        src = src.rearrange("p c (i b) -> p b i c", i=HB)
                        y = g4[:, :, half * HB:(half + 1) * HB, bass.ds(q * CH, CH)]
                        nc.vector.tensor_tensor(y, src, y, ALU.mult).then_inc(y_free, 1)


def mix_out_phase(core):
    nc, a, H, ps = core.nc, core.a, core.H, core.ps
    with ExitStack() as ctx:
        def sb(name, shape, dt=F32):
            return ctx.enter_context(nc.sbuf_tensor(name, shape, dt))

        def sem(name):
            return ctx.enter_context(nc.semaphore(name))

        w_out = sb("w_out", [HALF + 1, 2, D])
        yt = sb("y_tile", [P, 2, D])
        sT = sb("sumT", [HALF + 1, 2, 2, P])
        w_ready, ones, yt_set, t_ready, sT_set = sem("o_w_ready"), sem("o_ones"), sem("o_yt_set"), sem("o_t_ready"), sem("o_sT_set")
        o_ready, h_set, st_set, var_set = sem("o_o_ready"), sem("o_h_set"), sem("o_st_set"), sem("o_var_set")
        x_set, st2_set, var2_set, dve_step, dve_step2 = sem("o_x_set"), sem("o_st2_set"), sem("o_var2_set"), sem("o_dve_step"), sem("o_dve_step2")
        pool_step, pool_step2, rstd_set, rstd2_set = sem("o_pool_step"), sem("o_pool_step2"), sem("o_rstd_set"), sem("o_rstd2_set")
        XS = core.XS[0:HALF, :].rearrange("p (c t) -> p c t", c=2)
        NP = NT // 2
        with nc.Block() as block:
            @block.sync
            def _(sp):
                sp.dma_start(w_out[0:HALF, :, :], a["w_out"].rearrange("(c k) n -> k c n", c=2)).then_inc(w_ready, 16)
                sp.dma_start(w_out[HALF:HALF + 1, 1, :], a["b_out"].rearrange("(a c) -> a c", a=1)).then_inc(w_ready, 16)

            @block.gpsimd
            def _(pool):
                nc.gpsimd.memset(sT[HALF:HALF + 1, :, :, :], 1.0).then_inc(ones, 1)
                rsqrt_on_pool(nc, pool, core, var_set, pool_step, rstd_set)
                rsqrt_on_pool(nc, pool, core, var2_set, pool_step2, rstd2_set)
                pool.wait_ge(rstd2_set, 1)

            @block.scalar
            def _(act):
                for u in range(2):
                    nc.scalar.activation(yt[:, u, :], core.GY[:, col(u, D)], ACT.Copy).then_inc(yt_set, 1)
                with act.Fori(1, NP) as i:
                    for u in range(2):
                        act.wait_ge(t_ready, i * 2 + (u - 1))
                        nc.scalar.activation(yt[:, u, :], core.GY[:, col(i * 2 + u, D)], ACT.Copy).then_inc(yt_set, 1)

            @block.tensor
            def _(pe):
                def transpose(n, u):
                    pe.wait_ge(yt_set, n + 1)
                    for c in range(2):
                        mm = nc.tensor.transpose(ps[0:HALF, u, c * P:(c + 1) * P], yt[:, u, c * HALF:(c + 1) * HALF], core.ident[:, :])
                    mm.then_inc(t_ready, 1)

                def pair(i, last):
                    for u in range(2):
                        n = i * 2 + u
                        if not (last and u == 1):
                            transpose(n + 1, 1 - u)
                        pe.wait_ge(sT_set, n + 1)
                        pe.wait_ge(h_set, n + 1)
                        nc.tensor.matmul(ps[:, 2 + u, 0:D], sT[0:HALF, u, 0, :], w_out[0:HALF, 0, :], start=True, stop=False)
                        nc.tensor.matmul(ps[:, 2 + u, 0:D], sT[:, u, 1, :], w_out[:, 1, :], start=False, stop=True).then_inc(o_ready, 1)

                pe.wait_ge(w_ready, 32)
                pe.wait_ge(ones, 1)
                transpose(0, 0)
                with pe.Fori(0, NP - 1) as i:
                    pair(i, False)
                pair(NP - 1, True)

            @block.vector
            def _(dve):
                dve.sem_inc(h_set, 2)

                def add_short(n, u):
                    dve.wait_ge(t_ready, n + 1)
                    nc.vector.tensor_tensor(sT[0:HALF, u, :, :], ps[0:HALF, u, 0:2 * P].rearrange("p (c t) -> p c t", c=2),
                                            XS[:, :, col(n, P)], ALU.add).then_inc(sT_set, 1)

                def resid(n, u):
                    dve.wait_ge(o_ready, n + 1)
                    nc.vector.tensor_tensor(H[:, col(n, D)], ps[:, 2 + u, 0:D], H[:, col(n, D)], ALU.add).then_inc(h_set, 1)

                def stat(n, u):
                    dve.wait_ge(h_set, n + 3)
                    nc.vector.bn_stats(core.stats[:, col(n, 6)], H[:, col(n, D)]).then_inc(st_set, 1)

                add_short(0, 0)
                with dve.Fori(0, NP - 1) as i:
                    for u in range(2):
                        add_short(i * 2 + (u + 1), 1 - u)
                        resid(i * 2 + u, u)
                    for u in range(2):
                        stat(i * 2 + u, u)
                add_short(NT - 1, 1)
                for u in range(2):
                    resid(NT - 2 + u, u)
                for u in range(2):
                    stat(NT - 2 + u, u)
                mean_and_var(nc, dve, core, st_set, dve_step, var_set)
                dve.wait_ge(rstd_set, 1)
                with dve.Fori(0, NT) as n:
                    nc.vector.tensor_scalar(core.XA[:, col(n, D)], H[:, col(n, D)], core.mean[:, bass.ds(n, 1)],
                                            core.rstd[:, bass.ds(n, 1)], ALU.subtract, ALU.mult).then_inc(x_set, 1)
                dve.wait_ge(x_set, NT)
                all_stats(nc, dve, core, core.XA, st2_set)
                mean_and_var(nc, dve, core, st2_set, dve_step2, var2_set)


def attention_phase(core):
    nc, a, ps = core.nc, core.a, core.ps
    X = core.XA
    with ExitStack() as ctx:
        def sb(name, shape, dt=F32):
            return ctx.enter_context(nc.sbuf_tensor(name, shape, dt))

        def sem(name):
            return ctx.enter_context(nc.semaphore(name))

        QS = core.XS[0:KROWS, 0:HEADS * S // 2].bitcast(BF16).rearrange("p (h t) -> p h t", h=HEADS)
        KS = core.XS[0:KROWS, HEADS * S // 2:HEADS * S].bitcast(BF16).rearrange("p (h t) -> p h t", h=HEADS)
        PT = core.XS[:, HEADS * S:NT * P * 2].rearrange("p (u h t) -> p u h t", u=2, h=GH)
        V = core.GY[:, 0:TB * HEADS * 32].rearrange("p (i h c) -> p i h c", i=TB, h=HEADS)
        at = TB * HEADS * 32
        VN = core.GY[:, at:at + TB * D].rearrange("p (i c) -> p i c", i=TB)
        at += TB * D
        R = core.GY[:, at:at + 3 * S].rearrange("p (k t) -> p k t", k=3)
        at += 3 * S
        parts = core.GY[:, at:at + 9 * S // 2].bitcast(BF16).rearrange("p (k j t) -> p k j t", k=3, j=3)

        qkv_w = sb("qkv_w", [HALF, 2, 3 * D])
        proj_w = sb("proj_w", [HALF + 1, 2, D])
        aff = sb("affine1", [HALF, 2, 4])
        xn = sb("xn", [P, 2, D])
        hT = sb("hT", [HALF, 2, S])
        mx = sb("score_max", [P, NG, GH, TB])
        nm = sb("minus_max", [GH * TB, 2, P])
        nm_parts = sb("minus_max_parts", [GH * TB, NG, 3, P], BF16)
        ov = sb("numer_denom", [P, QH])
        rc = sb("recip_denom", [P, HB, GH])
        O = sb("attn_out", [P, TB, D])
        oT = sb("attn_outT", [HALF + 1, 2, 2, P])
        qk_dram = nc.dram_tensor("qk_parts", (3, 2 * D, S), BF16, kind="Internal").ap()

        w_in = sem("a_w_in")
        const_set = sem("a_const_set")
        xn_set, t_ready, ht_set, v_ready, v_set, v_full = (sem("a_" + n) for n in ("xn_set", "t_ready", "ht_set", "v_ready", "v_set", "v_full"))
        qk_ready, h_part, r_set, m_part, l_set, qk_out = (sem("a_" + n) for n in ("qk_ready", "h_part", "r_set", "m_part", "l_set", "qk_out"))
        qk_in = [sem(f"a_qk_in{g}") for g in range(NG)]
        s_ready, mx_set, nm_step, nm_set, aug_in = (sem("a_" + n) for n in ("s_ready", "mx_set", "nm_step", "nm_set", "aug_in"))
        st_ready, exp_set, pv_done, ov_set = (sem("a_" + n) for n in ("st_ready", "exp_set", "pv_done", "ov_set"))
        b7_ready, b7_free, rc_set, o_set = (sem("a_" + n) for n in ("b7_ready", "b7_free", "rc_set", "o_set"))
        ot_ready, oT_set, proj_ready, x_set, st_set = (sem("a_" + n) for n in ("ot_ready", "oT_set", "proj_ready", "x_set", "st_set"))
        dve_step, var_set, pool_step, rstd_set = (sem("a_" + n) for n in ("dve_step", "var_set", "pool_step", "rstd_set"))

        UNITS = GH * TB
        CHUNKS = 2 * TB * GH
        MICRO = 2 * TB
        B7 = ["m0", "o00", "m1", "o01", "o10", "m2", "o11", "o20", "o21"]
        LEAD = 2

        def b7(b, what):
            return b * len(B7) + (B7.index(what) + 1)

        with nc.Block() as block:
            @block.sync
            def _(sp):
                sp.dma_start(qkv_w[:, :, :], a["qkv_w"].rearrange("(c k) n -> k c n", c=2)).then_inc(w_in, 16)
                sp.dma_start(proj_w[0:HALF, :, :], a["proj_w"].rearrange("(c k) n -> k c n", c=2)).then_inc(w_in, 16)
                sp.dma_start(proj_w[HALF:HALF + 1, 1, :], a["proj_b"].rearrange("(a c) -> a c", a=1)).then_inc(w_in, 16)
                sp.dma_start(aff[:, :, :], a["affine"].rearrange("(c k) t -> k c t", c=2)).then_inc(w_in, 16)

                def spread(nb, before):
                    if before is not None:
                        for g in range(NG):
                            sp.wait_ge(qk_in[g], before * 192 + 192)
                    for t in range(3):
                        sp.wait_ge(l_set, nb * 3 + (t + 1))
                        sp.dma_start(qk_dram[:, t * P:(t + 1) * P, :].rearrange("j p t -> p j t"), parts[:, t, :, :]).then_inc(qk_out, 16)
                    sp.wait_ge(qk_out, nb * 48 + 48)
                    for g in range(NG):
                        if before is not None:
                            sp.wait_ge(st_ready, before * (NG * CHUNKS) + (g + 1) * CHUNKS)
                        hs = slice(g * GH, (g + 1) * GH)
                        row = 0
                        for part, times in ((0, 3), (1, 2), (2, 1)):
                            for _ in range(times):
                                src = qk_dram[part, g * GH * HD:(g + 1) * GH * HD, :].rearrange("(h r) t -> r h t", h=GH)
                                sp.dma_start(QS[row:row + HD, hs, :], src).then_inc(qk_in[g], 16)
                                row += HD
                        row = 0
                        for n in (3, 2, 1):
                            for part in range(n):
                                src = qk_dram[part, D + g * GH * HD:D + (g + 1) * GH * HD, :].rearrange("(h r) t -> r h t", h=GH)
                                sp.dma_start(KS[row:row + HD, hs, :], src).then_inc(qk_in[g], 16)
                                row += HD

                def batch(b, last):
                    for g in range(NG):
                        sp.wait_ge(nm_set, b * NG + (g + 1))
                        for j in range(3):
                            dst = QS[SPLIT + j:SPLIT + j + 1, g * GH:(g + 1) * GH, :].rearrange("a h (i t) -> a (h i) t", i=TB)
                            sp.dma_start(dst, nm_parts[:, g, j, :]).then_inc(aug_in, 16)
                    if not last:
                        spread(b + 1, b)

                spread(0, None)
                with sp.Fori(0, B - 1) as b:
                    batch(b, False)
                batch(B - 1, True)

            @block.gpsimd
            def _(pool):
                nc.gpsimd.memset(KS[SPLIT:KROWS, :, :], 1.0).then_inc(const_set, 1)
                pool.wait_ge(const_set, 1)
                nc.gpsimd.memset(V[:, :, :, HD:HD + 1], 1.0).then_inc(const_set, 1)
                nc.gpsimd.memset(V[:, :, :, HD + 1:32], 0.0).then_inc(const_set, 1)
                pool.wait_ge(const_set, 3)
                nc.gpsimd.memset(oT[HALF:HALF + 1, :, :, :], 1.0).then_inc(const_set, 1)

                def low_parts(nb):
                    for t in range(3):
                        pool.wait_ge(m_part, nb * 3 + (t + 1))
                        nc.gpsimd.tensor_tensor(parts[:, t, 2, :], R[:, t, :], parts[:, t, 1, :], ALU.subtract).then_inc(l_set, 1)

                def batch(b, last):
                    pool.wait_ge(v_set, b * TB + TB)
                    pool.wait_ge(pv_done, b * (NG * MICRO) + 2)
                    ones = V[:, :, :, HD:HD + 1].broadcast_to((P, TB, HEADS, HD))
                    nc.gpsimd.tensor_tensor(V[:, :, :, 0:HD], VN.rearrange("p i (h c) -> p i h c", h=HEADS), ones, ALU.mult).then_inc(v_full, 1)
                    if not last:
                        low_parts(b + 1)

                pool.wait_ge(const_set, 4)
                low_parts(0)
                with pool.Fori(0, B - 1) as b:
                    batch(b, False)
                batch(B - 1, True)
                rsqrt_on_pool(nc, pool, core, var_set, pool_step, rstd_set)
                pool.wait_ge(rstd_set, 1)

            @block.tensor
            def _(pe):
                def transpose_x(nb, i):
                    pe.wait_ge(xn_set, nb * TB + (i + 1))
                    if i >= 2:
                        pe.wait_ge(v_set, nb * TB + (i - 1))
                    for c in range(2):
                        mm = nc.tensor.transpose(ps[0:HALF, i % 2, c * P:(c + 1) * P], xn[:, i % 2, c * HALF:(c + 1) * HALF], core.ident[:, :])
                    mm.then_inc(t_ready, 1)

                def values(nb, i):
                    pe.wait_ge(ht_set, nb * TB + (i + 1))
                    for c in range(2):
                        mm = nc.tensor.matmul(ps[:, i % 2, 2 * P:2 * P + D], hT[:, c, i * P:(i + 1) * P], qkv_w[:, c, 2 * D:3 * D],
                                              start=(c == 0), stop=(c == 1))
                    mm.then_inc(v_ready, 1)

                def queries_keys(nb, t):
                    if t > 0:
                        pe.wait_ge(r_set, nb * 3 + t)
                    for half in range(2):
                        for c in range(2):
                            mm = nc.tensor.matmul(ps[:, 2 + half, 0:QH], qkv_w[:, c, t * P:(t + 1) * P], hT[:, c, half * QH:(half + 1) * QH],
                                                  start=(c == 0), stop=(c == 1))
                    mm.then_inc(qk_ready, 1)

                def prepare(nb, m):
                    if m < TB:
                        transpose_x(nb, m)
                    if 0 < m <= TB:
                        values(nb, m - 1)
                    if TB < m <= TB + 3:
                        queries_keys(nb, m - TB - 1)

                def scores(b, g, k):
                    h, i = k // TB, k % TB
                    pe.wait_ge(mx_set, b * (NG * UNITS) + (g * UNITS + k + 1))
                    for half in range(2):
                        mm = nc.tensor.matmul(ps[:, 2 * (k % 2) + half, 0:QH], QS[0:SPLIT, g * GH + h, i * P:(i + 1) * P],
                                              KS[0:SPLIT, g * GH + h, half * QH:(half + 1) * QH], start=True, stop=True)
                    mm.then_inc(s_ready, 1)

                def transpose_max(b, g):
                    pe.wait_ge(mx_set, b * (NG * UNITS) + ((g + 1) * UNITS + 2))
                    pe.wait_ge(b7_free, b7(b, f"m{g}"))
                    nc.tensor.transpose(ps[0:UNITS, 7, 0:P], mx[:, g, :, :].rearrange("p h i -> p (h i)"), core.ident[:, :]).then_inc(b7_ready, 1)

                def exp_scores(b, g, m):
                    half, j = m // TB, m % TB
                    for h in range(GH):
                        c = m * GH + h
                        pe.wait_ge(exp_set, b * (NG * CHUNKS) + (g * CHUNKS + c + 1))
                        nc.tensor.matmul(ps[:, 4 + c % 2, 0:QH], KS[:, g * GH + h, j * P:(j + 1) * P],
                                         QS[:, g * GH + h, half * QH:(half + 1) * QH], start=True, stop=True).then_inc(st_ready, 1)

                def weigh_values(b, g, m):
                    half, j = m // TB, m % TB
                    pe.wait_ge(exp_set, b * (NG * CHUNKS) + (g * CHUNKS + (m + 1) * GH + 2))
                    if j == 0:
                        pe.wait_ge(ov_set, b * (2 * NG) + (2 * g + half))
                    for h in range(GH):
                        mm = nc.tensor.matmul(ps[32 * h:32 * h + 32, 6, 0:QH], V[:, j, g * GH + h, :], PT[:, m % 2, h, :],
                                              start=(j == 0), stop=(j == TB - 1))
                    mm.then_inc(pv_done, 1)

                def transpose_out(b, g, half):
                    pe.wait_ge(ov_set, b * (2 * NG) + (2 * g + half + 1))
                    pe.wait_ge(b7_free, b7(b, f"o{g}{half}"))
                    for i in range(HB):
                        mm = nc.tensor.transpose(ps[:, 7, i * P:(i + 1) * P], ov[:, i * P:(i + 1) * P], core.ident[:, :])
                    mm.then_inc(b7_ready, 1)

                def tail(b, last):
                    pe.wait_ge(o_set, b * (2 * NG) + 2 * NG)
                    if not last:
                        pe.wait_ge(v_set, b * TB + 2 * TB)
                        pe.wait_ge(r_set, b * 3 + 6)
                    for i in range(TB + 1):
                        if i < TB:
                            if i >= 2:
                                pe.wait_ge(oT_set, b * TB + (i - 1))
                            for c in range(2):
                                mm = nc.tensor.transpose(ps[0:HALF, i % 2, c * P:(c + 1) * P], O[:, i, c * HALF:(c + 1) * HALF], core.ident[:, :])
                            mm.then_inc(ot_ready, 1)
                        if i > 0:
                            k = i - 1
                            pe.wait_ge(oT_set, b * TB + (k + 1))
                            if k >= 2:
                                pe.wait_ge(x_set, b * TB + (k - 1))
                            nc.tensor.matmul(ps[:, 2 + k % 2, 0:D], oT[0:HALF, k % 2, 0, :], proj_w[0:HALF, 0, :], start=True, stop=False)
                            nc.tensor.matmul(ps[:, 2 + k % 2, 0:D], oT[:, k % 2, 1, :], proj_w[:, 1, :], start=False, stop=True).then_inc(proj_ready, 1)

                def batch(b, last):
                    pe.wait_ge(qk_in[0], b * 192 + 192)
                    pe.wait_ge(v_set, b * TB + TB)
                    pe.wait_ge(r_set, b * 3 + 3)
                    pe.wait_ge(x_set, b * TB)
                    for k in range(UNITS):
                        scores(b, 0, k)
                    transpose_max(b, 0)
                    for g in range(NG - 1):
                        pe.wait_ge(qk_in[g + 1], b * 192 + 192)
                        for m in range(MICRO + LEAD):
                            if m < MICRO:
                                scores(b, g + 1, 2 * m)
                                scores(b, g + 1, 2 * m + 1)
                            if m == 1 and g > 0:
                                transpose_out(b, g - 1, 1)
                            if m == LEAD:
                                pe.wait_ge(aug_in, b * 144 + (g + 1) * 48)
                                pe.wait_ge(v_full, b + 1)
                            if m >= LEAD:
                                exp_scores(b, g, m - LEAD)
                            if m > LEAD:
                                weigh_values(b, g, m - LEAD - 1)
                            if m == LEAD + TB + 2:
                                transpose_out(b, g, 0)
                            if m == MICRO:
                                transpose_max(b, g + 1)
                        weigh_values(b, g, MICRO - 1)
                    g = NG - 1
                    if not last:
                        pe.wait_ge(mx_set, b * (NG * UNITS) + (NG * UNITS + 2))
                    for m in range(MICRO):
                        if not last:
                            prepare(b + 1, m)
                        if m == 0:
                            transpose_out(b, g - 1, 1)
                            pe.wait_ge(aug_in, b * 144 + (g + 1) * 48)
                        exp_scores(b, g, m)
                        if m > 0:
                            weigh_values(b, g, m - 1)
                        if m == TB + 2:
                            transpose_out(b, g, 0)
                    weigh_values(b, g, MICRO - 1)
                    transpose_out(b, g, 1)
                    tail(b, last)

                pe.wait_ge(w_in, 64)
                pe.wait_ge(const_set, 4)
                for m in range(TB + 4):
                    prepare(0, m)
                with pe.Fori(0, B - 1) as b:
                    batch(b, False)
                batch(B - 1, True)

            @block.scalar
            def _(act):
                act.sem_inc(exp_set, 2)

                def middle_part(nb, t):
                    act.wait_ge(r_set, nb * 3 + (t + 1))
                    nc.scalar.activation(parts[:, t, 1, :], R[:, t, :], ACT.Copy).then_inc(m_part, 1)

                def batch(b, last):
                    for g in range(NG):
                        for m in range(MICRO):
                            if g == NG - 1 and not last and TB + 2 <= m < TB + 5:
                                middle_part(b + 1, m - TB - 2)
                            act.wait_ge(pv_done, b * (NG * MICRO) + (g * MICRO + m + 1))
                            for h in range(GH):
                                c = m * GH + h
                                act.wait_ge(st_ready, b * (NG * CHUNKS) + (g * CHUNKS + c + 1))
                                nc.scalar.activation(PT[:, m % 2, h, :], ps[:, 4 + c % 2, 0:QH], ACT.Exp, scale=HD ** -0.5).then_inc(exp_set, 1)

                for t in range(3):
                    middle_part(0, t)
                with act.Fori(0, B - 1) as b:
                    batch(b, False)
                batch(B - 1, True)

            @block.vector
            def _(dve):
                dve.sem_inc(mx_set, 2)
                dve.sem_inc(pv_done, 2)
                dve.sem_inc(b7_free, 1)

                def norm(nb, i):
                    n = nb * TB + i
                    nc.vector.tensor_scalar(xn[:, i % 2, :], X[:, col(n, D)], core.mean[:, bass.ds(n, 1)],
                                            core.rstd[:, bass.ds(n, 1)], ALU.subtract, ALU.mult).then_inc(xn_set, 1)

                def affine(nb, i):
                    dve.wait_ge(t_ready, nb * TB + (i + 1))
                    for c in range(2):
                        op = nc.vector.tensor_scalar(hT[:, c, i * P:(i + 1) * P], ps[0:HALF, i % 2, c * P:(c + 1) * P],
                                                     aff[:, c, 0:1], aff[:, c, 1:2], ALU.mult, ALU.add)
                    op.then_inc(ht_set, 1)

                def keep_values(nb, i):
                    dve.wait_ge(v_ready, nb * TB + (i + 1))
                    if i == 0:
                        dve.wait_ge(v_full, nb)
                    nc.vector.tensor_copy(VN[:, i, :], ps[:, i % 2, 2 * P:2 * P + D]).then_inc(v_set, 1)

                def high_part(nb, t):
                    dve.wait_ge(qk_ready, nb * 3 + (t + 1))
                    dve.wait_ge(qk_out, nb * 48)
                    src = ps[:, 2:4, 0:QH]
                    h1 = parts[:, t, 0, :].rearrange("p (a t) -> p a t", a=2)
                    nc.vector.tensor_copy(h1, src).then_inc(h_part, 1)
                    dve.wait_ge(h_part, nb * 3 + (t + 1))
                    nc.vector.tensor_tensor(R[:, t, :].rearrange("p (a t) -> p a t", a=2), src, h1, ALU.subtract).then_inc(r_set, 1)

                def prepare(nb, m):
                    if m == 0:
                        norm(nb, 0)
                    if m + 1 < TB:
                        norm(nb, m + 1)
                    if m < TB:
                        affine(nb, m)
                    if 0 < m <= TB:
                        keep_values(nb, m - 1)
                    if TB < m <= TB + 3:
                        high_part(nb, m - TB - 1)

                def maximum(b, g, k):
                    dve.wait_ge(s_ready, b * (NG * UNITS) + (g * UNITS + k + 1))
                    nc.vector.tensor_reduce(mx[:, g, k // TB, k % TB:k % TB + 1], ps[:, 2 * (k % 2):2 * (k % 2) + 2, 0:QH], AX.XY, ALU.max).then_inc(mx_set, 1)

                def split_max(b, g):
                    dve.wait_ge(b7_ready, b7(b, f"m{g}"))
                    at = (b * NG + g) * 4
                    p = nm_parts[:, g, :, :]
                    nc.vector.tensor_scalar(nm[:, 0, :], ps[0:UNITS, 7, 0:P], -1.0, None, ALU.mult).then_inc(b7_free, 1)
                    dve.wait_ge(b7_free, b7(b, f"m{g}") + 1)
                    nc.vector.tensor_copy(p[:, 0, :], nm[:, 0, :]).then_inc(nm_step, 1)
                    dve.wait_ge(nm_step, at + 1)
                    nc.vector.tensor_tensor(nm[:, 1, :], nm[:, 0, :], p[:, 0, :], ALU.subtract).then_inc(nm_step, 1)
                    dve.wait_ge(nm_step, at + 2)
                    nc.vector.tensor_copy(p[:, 1, :], nm[:, 1, :]).then_inc(nm_step, 1)
                    dve.wait_ge(nm_step, at + 3)
                    nc.vector.tensor_tensor(p[:, 2, :], nm[:, 1, :], p[:, 1, :], ALU.subtract).then_inc(nm_step, 1)
                    dve.wait_ge(nm_step, at + 4)
                    dve.sem_inc(nm_set, 1)

                def keep_sums(b, g, half):
                    dve.wait_ge(pv_done, b * (NG * MICRO) + (g * MICRO + (half + 1) * TB + 2))
                    nc.vector.tensor_copy(ov[:, :], ps[:, 6, 0:QH]).then_inc(ov_set, 1)

                def divide(b, g, half):
                    dve.wait_ge(b7_ready, b7(b, f"o{g}{half}"))
                    src = ps[:, 7, 0:QH].rearrange("p (i h c) -> p i h c", i=HB, h=GH)
                    nc.vector.reciprocal(rc[:, :, :], src[:, :, :, HD]).then_inc(rc_set, 1)
                    dve.wait_ge(rc_set, b * (2 * NG) + (2 * g + half + 1))
                    dst = O[:, half * HB:(half + 1) * HB, g * GH * HD:(g + 1) * GH * HD].rearrange("p i (h c) -> p i h c", h=GH)
                    scale = rc[:, :, :].rearrange("p i (h a) -> p i h a", a=1).broadcast_to((P, HB, GH, HD))
                    nc.vector.tensor_tensor(dst, src[:, :, :, 0:HD], scale, ALU.mult).then_inc(o_set, 1)
                    dve.wait_ge(o_set, b * (2 * NG) + (2 * g + half + 1))
                    dve.sem_inc(b7_free, 1)

                def tail(b):
                    for i in range(TB + 1):
                        if i < TB:
                            dve.wait_ge(ot_ready, b * TB + (i + 1))
                            nc.vector.tensor_copy(oT[0:HALF, i % 2, :, :], ps[0:HALF, i % 2, 0:2 * P].rearrange("p (c t) -> p c t", c=2)).then_inc(oT_set, 1)
                        if i > 0:
                            n = b * TB + (i - 1)
                            dve.wait_ge(proj_ready, n + 1)
                            nc.vector.tensor_tensor(X[:, col(n, D)], ps[:, 2 + (i - 1) % 2, 0:D], X[:, col(n, D)], ALU.add).then_inc(x_set, 1)
                    for i in range(TB):
                        n = b * TB + i
                        dve.wait_ge(x_set, n + 1)
                        nc.vector.bn_stats(core.stats[:, col(n, 6)], X[:, col(n, D)]).then_inc(st_set, 1)

                def batch(b, last):
                    for k in range(UNITS):
                        maximum(b, 0, k)
                    split_max(b, 0)
                    for g in range(NG - 1):
                        for m in range(MICRO + LEAD):
                            if m < MICRO:
                                maximum(b, g + 1, 2 * m)
                                maximum(b, g + 1, 2 * m + 1)
                            if m == 1 and g > 0:
                                divide(b, g - 1, 1)
                            if m == LEAD + TB + 1:
                                keep_sums(b, g, 0)
                            if m == LEAD + TB + 2:
                                divide(b, g, 0)
                            if m == MICRO:
                                split_max(b, g + 1)
                        keep_sums(b, g, 1)
                    g = NG - 1
                    for m in range(MICRO):
                        if not last:
                            prepare(b + 1, m)
                        if m == 0:
                            divide(b, g - 1, 1)
                        if m == TB + 1:
                            keep_sums(b, g, 0)
                        if m == TB + 2:
                            divide(b, g, 0)
                    keep_sums(b, g, 1)
                    divide(b, g, 1)
                    tail(b)

                dve.wait_ge(w_in, 64)
                for m in range(TB + 4):
                    prepare(0, m)
                with dve.Fori(0, B - 1) as b:
                    batch(b, False)
                batch(B - 1, True)
                mean_and_var(nc, dve, core, st_set, dve_step, var_set)


def route_phase(core):
    nc, a, ps = core.nc, core.a, core.ps
    X = core.XA
    with ExitStack() as ctx:
        def sb(name, shape, dt=F32):
            return ctx.enter_context(nc.sbuf_tensor(name, shape, dt))

        def sem(name):
            return ctx.enter_context(nc.semaphore(name))

        gate_w = sb("gate_w", [HALF + 1, 2, E])
        aff = sb("affine2", [HALF, 2, 4])
        xn = sb("r_xn", [P, 2, D])
        hT = sb("r_hT", [HALF + 1, 2, 2, P])
        steps = sb("steps", [P, NSLOT])
        ids = sb("ids", [P, NT, TOPK])
        before, ones = sb("before", [P, P]), sb("ones", [P, P])
        logit, at_max, either = sb("logit", [P, NT, E]), sb("at_max", [P, NT, E]), sb("either", [P, NT, E])
        pick = [sb(f"pick{k}", [P, NT, E]) for k in range(TOPK)]
        top = sb("top", [P, TOPK, NT])
        first = sb("first", [P, NT])
        ex, den = sb("exp_dif", [P, NT]), sb("denom", [P, NT])
        run = sb("running", [P, 2, NT, E])
        place, chosen = sb("place", [P, NT, E]), sb("chosen", [P, NT, E])
        slot_f = sb("slot_f", [P, NT, TOPK])
        full = sb("full", [P, E, NT])
        tiles, ends = sb("tiles", [P, E]), sb("ends", [P, 4, E])
        past = sb("past", [P, NSLOT, E - 1])
        past_n = sb("past_n", [P, NSLOT])
        send = sb("send", [P, 4, TOPK, D + 1])
        send_at = sb("send_at", [P, 4, TOPK], U32)
        const_in, w_in, b2_in, const_set = sem("r_const_in"), sem("r_w_in"), sem("r_b2_in"), sem("r_const_set")
        xn_set, t_ready, hT_set, g_ready = sem("r_xn_set"), sem("r_t_ready"), sem("r_hT_set"), sem("r_g_ready")
        pick_set, count_ready, step, dif_set, exp_set = sem("r_pick_set"), sem("r_count_ready"), sem("r_step"), sem("r_dif_set"), sem("r_exp_set")
        send_set, sending = sem("r_send_set"), sem("r_sending")
        sent = [sem(f"r_sent{u}") for u in range(4)]
        NP = NT // 2
        with nc.Block() as block:
            @block.sync
            def _(sp):
                sp.dma_start(gate_w[0:HALF, :, :], a["gate_w"].rearrange("(c k) n -> k c n", c=2)).then_inc(const_in, 16)
                sp.dma_start(gate_w[HALF:HALF + 1, 1, :], a["gate_b"].rearrange("(a c) -> a c", a=1)).then_inc(const_in, 16)
                sp.dma_start(aff[:, :, :], a["affine"].rearrange("(c k) t -> k c t", c=2)).then_inc(const_in, 16)
                sp.dma_start(steps[:, :], a["steps"]).then_inc(const_in, 16)
                sp.dma_start(ids[:, :, :], a["ids"]).then_inc(const_in, 16)
                sp.dma_start(before[:, :], a["before"]).then_inc(const_in, 16)
                for e in range(E):
                    sp.dma_start(core.W1[0:HALF, e, :, :], a["w1"][e].rearrange("(c k) n -> k c n", c=2)).then_inc(w_in, 16)
                    sp.dma_start(core.W2[:, e, :, :], a["w2"][e].rearrange("(j k) n -> k j n", k=P)).then_inc(w_in, 16)
                sp.dma_start(core.W1[HALF:HALF + 1, :, 1, :], a["b1"].rearrange("(a e) n -> a e n", a=1)).then_inc(w_in, 16)
                sp.wait_ge(w_in, 16 * (2 * E + 1))

            @block.gpsimd
            def _(pool):
                nc.gpsimd.memset(hT[HALF:HALF + 1, :, :, :], 1.0).then_inc(const_set, 1)
                pool.wait_ge(const_set, 1)
                nc.gpsimd.memset(ones[:, :], 1.0).then_inc(const_set, 1)
                with pool.Fori(0, NT // 4) as i:
                    for u in range(4):
                        pool.wait_ge(send_set, i * 4 + (u + 1))
                        pool.sem_inc(sending, 1)
                        for k in range(TOPK):
                            pool.indirect_dma_start(core.slot_x, bass.IndirectOffsetOnAxis(ap=send_at[:, u, k:k + 1], axis=0),
                                                    send[:, u, k, :], None).then_inc(sent[u], 16)
                for u in range(4):
                    pool.wait_ge(sent[u], TOPK * 16 * (NT // 4))

            @block.tensor
            def _(pe):
                def transpose(n, u):
                    pe.wait_ge(xn_set, n + 1)
                    pe.wait_ge(hT_set, n)
                    for c in range(2):
                        mm = nc.tensor.transpose(ps[0:HALF, u, c * P:(c + 1) * P], xn[:, u, c * HALF:(c + 1) * HALF], core.ident[:, :])
                    mm.then_inc(t_ready, 1)

                def gate(n, u):
                    pe.wait_ge(hT_set, n + 1)
                    nc.tensor.matmul(ps[:, 2, col(n, E)], hT[0:HALF, u, 0, :], gate_w[0:HALF, 0, :], start=True, stop=False)
                    nc.tensor.matmul(ps[:, 2, col(n, E)], hT[:, u, 1, :], gate_w[:, 1, :], start=False, stop=True).then_inc(g_ready, 1)

                pe.wait_ge(const_in, 96)
                pe.wait_ge(const_set, 2)
                with pe.Fori(0, NP) as i:
                    for u in range(2):
                        transpose(i * 2 + u, u)
                        gate(i * 2 + u, u)
                pe.wait_ge(pick_set, 1)
                flat = either[:, :, :].rearrange("p n e -> p (n e)")
                nc.tensor.matmul(ps[:, 3, 0:NT * E], before[:, :], flat, start=True, stop=True).then_inc(count_ready, 1)
                nc.tensor.matmul(ps[:, 4, 0:NT * E], ones[:, :], flat, start=True, stop=True).then_inc(count_ready, 1)

            @block.scalar
            def _(act):
                act.dma_start(core.b2[:, :, :], a["b2"].rearrange("(a e) n -> a e n", a=1).broadcast_to((P, E, D))).then_inc(b2_in, 16)
                act.wait_ge(dif_set, 1)
                nc.scalar.activation(ex[:, :], ex[:, :], ACT.Exp).then_inc(exp_set, 1)
                act.wait_ge(exp_set, 1)
                act.wait_ge(b2_in, 16)

            @block.vector
            def _(dve):
                def norm(n, u):
                    nc.vector.tensor_scalar(xn[:, u, :], X[:, col(n, D)], core.mean[:, bass.ds(n, 1)],
                                            core.rstd[:, bass.ds(n, 1)], ALU.subtract, ALU.mult).then_inc(xn_set, 1)

                def affine(n, u):
                    dve.wait_ge(t_ready, n + 1)
                    for c in range(2):
                        op = nc.vector.tensor_scalar(hT[0:HALF, u, c, :], ps[0:HALF, u, c * P:(c + 1) * P],
                                                     aff[:, c, 2:3], aff[:, c, 3:4], ALU.mult, ALU.add)
                    op.then_inc(hT_set, 1)

                dve.wait_ge(const_in, 96)
                norm(0, 0)
                with dve.Fori(0, NP - 1) as i:
                    for u in range(2):
                        norm(i * 2 + (u + 1), 1 - u)
                        dve.wait_ge(g_ready, i * 2 + u)
                        affine(i * 2 + u, u)
                norm(NT - 1, 1)
                for u in range(2):
                    dve.wait_ge(g_ready, NT - 2 + u)
                    affine(NT - 2 + u, u)

                done = 0

                def then(op):
                    nonlocal done
                    done += 1
                    op.then_inc(step, 1)
                    dve.wait_ge(step, done)

                def per_expert(ap):
                    return ap.rearrange("p (n a) -> p n a", a=1).broadcast_to((P, NT, E))

                expert = steps[:, 0:E].rearrange("p (a e) -> p a e", a=1).broadcast_to((P, NT, E))
                dve.wait_ge(g_ready, NT)
                then(nc.vector.tensor_copy(logit[:, :, :], ps[:, 2, 0:NT * E].rearrange("p (n e) -> p n e", e=E)))
                for k in range(TOPK):
                    then(nc.vector.tensor_reduce(top[:, k, :], logit[:, :, :], AX.X, ALU.max))
                    then(nc.vector.tensor_tensor(at_max[:, :, :], logit[:, :, :], per_expert(top[:, k, :]), ALU.is_ge))
                    then(nc.vector.scalar_tensor_tensor(at_max[:, :, :], expert, float(E), at_max[:, :, :], ALU.subtract, ALU.mult))
                    then(nc.vector.tensor_reduce(first[:, :], at_max[:, :, :], AX.X, ALU.min))
                    then(nc.vector.scalar_tensor_tensor(pick[k][:, :, :], expert, float(E), per_expert(first[:, :]), ALU.subtract, ALU.is_equal))
                    if k == 0:
                        then(nc.vector.scalar_tensor_tensor(logit[:, :, :], pick[0][:, :, :], -3.0e38, logit[:, :, :], ALU.mult, ALU.add))
                then(nc.vector.tensor_tensor(either[:, :, :], pick[0][:, :, :], pick[1][:, :, :], ALU.add))
                dve.sem_inc(pick_set, 1)
                then(nc.vector.tensor_tensor(ex[:, :], top[:, 1, :], top[:, 0, :], ALU.subtract))
                dve.sem_inc(dif_set, 1)
                dve.wait_ge(exp_set, 1)
                then(nc.vector.tensor_scalar(den[:, :], ex[:, :], 1.0, None, ALU.add))
                then(nc.vector.reciprocal(core.weight[:, 0, :], den[:, :]))
                then(nc.vector.tensor_tensor(core.weight[:, 1, :], core.weight[:, 0, :], ex[:, :], ALU.mult))
                dve.wait_ge(count_ready, 2)
                total = ps[:, 4, 0:NT * E].rearrange("p (n e) -> p n e", e=E)
                then(nc.vector.tensor_copy(run[:, 0, :, :], total))
                reach, r = 1, 0
                while reach < NT:
                    then(nc.vector.tensor_copy(run[:, 1 - r, 0:reach, :], run[:, r, 0:reach, :]))
                    then(nc.vector.tensor_tensor(run[:, 1 - r, reach:NT, :], run[:, r, reach:NT, :], run[:, r, 0:NT - reach, :], ALU.add))
                    reach, r = 2 * reach, 1 - r
                count = run[:, r, NT - 1, :].rearrange("p (e a) -> p e a", a=1).broadcast_to((P, E, NT))
                mult = steps[:, 0:NT].rearrange("p (a n) -> p a n", a=1).broadcast_to((P, E, NT))
                then(nc.vector.scalar_tensor_tensor(full[:, :, :], mult, float(P), count, ALU.mult, ALU.is_lt))
                then(nc.vector.tensor_reduce(tiles[:, :], full[:, :, :], AX.X, ALU.add))
                then(nc.vector.tensor_copy(ends[:, 0, :], tiles[:, :]))
                reach, s = 1, 0
                while reach < E:
                    then(nc.vector.tensor_copy(ends[:, s + 1, 0:reach], ends[:, s, 0:reach]))
                    then(nc.vector.tensor_tensor(ends[:, s + 1, reach:E], ends[:, s, reach:E], ends[:, s, 0:E - reach], ALU.add))
                    reach, s = 2 * reach, s + 1
                then(nc.vector.tensor_tensor(tiles[:, :], ends[:, s, :], tiles[:, :], ALU.subtract))
                tile_no = steps[:, :].rearrange("p (s a) -> p s a", a=1).broadcast_to((P, NSLOT, E - 1))
                end = ends[:, s, 0:E - 1].rearrange("p (a e) -> p a e", a=1).broadcast_to((P, NSLOT, E - 1))
                then(nc.vector.tensor_tensor(past[:, :, :], tile_no, end, ALU.is_ge))
                then(nc.vector.tensor_reduce(past_n[:, :], past[:, :, :], AX.X, ALU.add))
                then(nc.vector.tensor_copy(core.tile_expert[:, :], past_n[:, :]))
                then(nc.vector.tensor_tensor(place[:, :, :], run[:, r, :, :], total, ALU.subtract))
                then(nc.vector.tensor_tensor(place[:, :, :], ps[:, 3, 0:NT * E].rearrange("p (n e) -> p n e", e=E), place[:, :, :], ALU.add))
                begin = tiles[:, :].rearrange("p (a e) -> p a e", a=1).broadcast_to((P, NT, E))
                then(nc.vector.scalar_tensor_tensor(place[:, :, :], begin, float(P), place[:, :, :], ALU.mult, ALU.add))
                for k in range(TOPK):
                    then(nc.vector.tensor_tensor(chosen[:, :, :], pick[k][:, :, :], place[:, :, :], ALU.mult))
                    then(nc.vector.tensor_reduce(slot_f[:, :, k], chosen[:, :, :], AX.X, ALU.add))
                with dve.Fori(0, NT // 4) as i:
                    for u in range(4):
                        n = i * 4 + u
                        dve.wait_ge(sent[u], i * (TOPK * 16))
                        for k in range(TOPK):
                            nc.vector.tensor_scalar(send[:, u, k, 0:D], X[:, col(n, D)], core.mean[:, bass.ds(n, 1)],
                                                    core.rstd[:, bass.ds(n, 1)], ALU.subtract, ALU.mult)
                        nc.vector.tensor_copy(send[:, u, :, D], ids[:, bass.ds(n, 1), :].rearrange("p a k -> p (a k)"))
                        nc.vector.tensor_copy(send_at[:, u, :], slot_f[:, bass.ds(n, 1), :].rearrange("p a k -> p (a k)")).then_inc(send_set, 1)


def expert_phase(core):
    nc, a, ps = core.nc, core.a, core.ps
    with ExitStack() as ctx:
        def sb(name, shape, dt=F32):
            return ctx.enter_context(nc.sbuf_tensor(name, shape, dt))

        def sem(name):
            return ctx.enter_context(nc.semaphore(name))

        U = 8
        assert NSLOT % U == 0
        aff = sb("x_affine2", [HALF, 2, 4])
        xs = sb("slot_rows", [P, U, D + 1])
        hT = sb("x_hT", [HALF + 1, 2, 2, P])
        he = sb("hidden", [P, 2, HID])
        heT = sb("hiddenT", [P, 2, KH, P])
        ys = sb("slot_out", [P, 4, D])
        ys_at = sb("slot_out_at", [P, 4, 1], U32)
        aff_in, ones_set = sem("x_aff_in"), sem("x_ones_set")
        x_in = [sem(f"x_x_in{u}") for u in range(U)]
        xT_ready, hT_set, h_ready, he_set = sem("x_xT_ready"), sem("x_hT_set"), sem("x_h_ready"), sem("x_he_set")
        heT_ready, heT_set, y_ready, y_set = sem("x_heT_ready"), sem("x_heT_set"), sem("x_y_ready"), sem("x_y_set")
        sum_set, sending = sem("x_sum_set"), sem("x_sending")
        y_out = [sem(f"x_y_out{u}") for u in range(4)]

        def has(j, back):
            return j is None or 0 <= j - back < NSLOT

        def steps(engine, step):
            for u in range(U):
                step(u, u, 0)
            with engine.Fori(1, NSLOT // U) as i:
                for u in range(U):
                    step(None, u, i)
            for u in range(3):
                step(NSLOT + u, u, NSLOT // U)

        def tile(i, u, back):
            return i * U + (u - back)

        def expert_of(engine, s):
            return engine.value_load(core.tile_expert[0:1, bass.ds(s, 1)], min_val=0, max_val=E - 1)

        with nc.Block() as block:
            @block.sync
            def _(sp):
                sp.dma_start(aff[:, :, :], a["affine"].rearrange("(c k) t -> k c t", c=2)).then_inc(aff_in, 16)
                for u in range(U):
                    sp.dma_start(xs[:, u, :], core.slot_x[u * P:(u + 1) * P, :]).then_inc(x_in[u], 16)
                with sp.Fori(1, NSLOT // U) as i:
                    for u in range(U):
                        sp.wait_ge(y_set, tile(i, u, U) + 1)
                        sp.dma_start(xs[:, u, :], core.slot_x[bass.ds((i * U + u) * P, P), :]).then_inc(x_in[u], 16)

            @block.gpsimd
            def _(pool):
                nc.gpsimd.memset(hT[HALF:HALF + 1, :, :, :], 1.0).then_inc(ones_set, 1)
                with pool.Fori(0, NSLOT // 4) as i:
                    for u in range(4):
                        pool.wait_ge(y_set, i * 4 + (u + 1))
                        pool.sem_inc(sending, 1)
                        pool.indirect_dma_start(core.tok_y, bass.IndirectOffsetOnAxis(ap=ys_at[:, u, 0:1], axis=0),
                                                ys[:, u, :], None).then_inc(y_out[u], 16)
                for u in range(4):
                    pool.wait_ge(y_out[u], 16 * (NSLOT // 4))

            @block.tensor
            def _(pe):
                def step(j, u, i):
                    if has(j, 0):
                        s = tile(i, u, 0)
                        pe.wait_ge(x_in[u], (i + 1) * 16)
                        pe.wait_ge(hT_set, s)
                        for c in range(2):
                            mm = nc.tensor.transpose(ps[0:HALF, 0, c * P:(c + 1) * P], xs[:, u, c * HALF:(c + 1) * HALF], core.ident[:, :])
                        mm.then_inc(xT_ready, 1)
                    if has(j, 1):
                        s, v = tile(i, u, 1), (u - 1) % 2
                        e = expert_of(pe, s)
                        pe.wait_ge(hT_set, s + 1)
                        if has(j, 3):
                            pe.wait_ge(he_set, tile(i, u, 3) + 1)
                        for half in range(2):
                            for c in range(2):
                                rows = HALF + c
                                w = core.W1[0:rows, bass.ds(e, 1), c, half * QH:(half + 1) * QH].rearrange("p a n -> p (a n)")
                                mm = nc.tensor.matmul(ps[:, 1 + 2 * v + half, 0:QH], hT[0:rows, v, c, :], w, start=(c == 0), stop=(c == 1))
                        mm.then_inc(h_ready, 1)
                    if has(j, 2):
                        s, v = tile(i, u, 2), u % 2
                        pe.wait_ge(he_set, s + 1)
                        pe.wait_ge(heT_set, s)
                        for k in range(KH):
                            mm = nc.tensor.transpose(ps[:, 5 + k // 3, k % 3 * P:(k % 3 + 1) * P], he[:, v, k * P:(k + 1) * P], core.ident[:, :])
                        mm.then_inc(heT_ready, 1)
                    if has(j, 3):
                        s, v = tile(i, u, 3), (u - 3) % 2
                        e = expert_of(pe, s)
                        pe.wait_ge(heT_set, s + 1)
                        pe.wait_ge(sum_set, s)
                        for k in range(KH):
                            w = core.W2[:, bass.ds(e, 1), k, :].rearrange("p a n -> p (a n)")
                            mm = nc.tensor.matmul(ps[:, 7, 0:D], heT[:, v, k, :], w, start=(k == 0), stop=(k == KH - 1))
                        mm.then_inc(y_ready, 1)

                pe.wait_ge(ones_set, 1)
                steps(pe, step)

            @block.scalar
            def _(act):
                def step(j, u, i):
                    if has(j, 1):
                        s, v = tile(i, u, 1), (u - 1) % 2
                        act.wait_ge(h_ready, s + 1)
                        if has(j, 3):
                            act.wait_ge(heT_ready, tile(i, u, 3) + 1)
                        src = ps[:, 1 + 2 * v:3 + 2 * v, 0:QH]
                        nc.scalar.activation(he[:, v, :].rearrange("p (a n) -> p a n", a=2), src, ACT.Gelu).then_inc(he_set, 1)

                steps(act, step)

            @block.vector
            def _(dve):
                def step(j, u, i):
                    if has(j, 0):
                        s, v = tile(i, u, 0), u % 2
                        dve.wait_ge(xT_ready, s + 1)
                        if has(j, 2):
                            dve.wait_ge(h_ready, tile(i, u, 2) + 1)
                        for c in range(2):
                            op = nc.vector.tensor_scalar(hT[0:HALF, v, c, :], ps[0:HALF, 0, c * P:(c + 1) * P],
                                                         aff[:, c, 2:3], aff[:, c, 3:4], ALU.mult, ALU.add)
                        op.then_inc(hT_set, 1)
                    if has(j, 2):
                        s, v = tile(i, u, 2), u % 2
                        dve.wait_ge(heT_ready, s + 1)
                        if has(j, 4):
                            dve.wait_ge(y_ready, tile(i, u, 4) + 1)
                        nc.vector.tensor_copy(heT[:, v, :, :].rearrange("p (a k) t -> p a (k t)", a=2), ps[:, 5:7, 0:QH]).then_inc(heT_set, 1)
                    if has(j, 3):
                        s, v = tile(i, u, 3), (u - 3) % 4
                        e = expert_of(dve, s)
                        dve.wait_ge(y_ready, s + 1)
                        if has(j, 7):
                            dve.wait_ge(y_out[v], (tile(i, u, 3) - v) * 4)
                        bias = core.b2[:, bass.ds(e, 1), :].rearrange("p a n -> p (a n)")
                        nc.vector.tensor_tensor(ys[:, v, :], ps[:, 7, 0:D], bias, ALU.add).then_inc(sum_set, 1)
                        nc.vector.tensor_copy(ys_at[:, v, :], xs[:, (u - 3) % U, D:D + 1]).then_inc(y_set, 1)

                dve.wait_ge(aff_in, 16)
                steps(dve, step)


def combine_phase(core):
    nc, H = core.nc, core.H
    with ExitStack() as ctx:
        def sb(name, shape, dt=F32):
            return ctx.enter_context(nc.sbuf_tensor(name, shape, dt))

        def sem(name):
            return ctx.enter_context(nc.semaphore(name))

        y = sb("expert_rows", [P, 2, TOPK, TB, D])
        y_in = [sem(f"f_y_in{u}") for u in range(2)]
        hx_set, part_set, out_set, out_done = sem("f_hx_set"), sem("f_part_set"), sem("f_out_set"), sem("f_out_done")
        rows = core.tok_y[0:TOPK * NT * P, :].rearrange("(k b i p) c -> b k p i c", k=TOPK, b=B, i=TB)
        with nc.Block() as block:
            @block.sync
            def _(sp):
                for b in range(B):
                    if b >= 2:
                        sp.wait_ge(out_set, (b - 1) * TB)
                    for k in range(TOPK):
                        sp.dma_start(y[:, b % 2, k, :, :], rows[b, k]).then_inc(y_in[b % 2], 16)

            @block.gpsimd
            def _(pool):
                with pool.Fori(0, NT) as n:
                    nc.gpsimd.tensor_tensor(H[:, col(n, D)], H[:, col(n, D)], core.XA[:, col(n, D)], ALU.add).then_inc(hx_set, 1)

            @block.vector
            def _(dve):
                with dve.Fori(0, B // 2) as i:
                    for u in range(2):
                        for k in range(TOPK):
                            for t in range(TB):
                                n = i * (2 * TB) + (u * TB + t)
                                if k == 0:
                                    dve.wait_ge(y_in[u], (i + 1) * (16 * TOPK))
                                    dve.wait_ge(hx_set, n + 1)
                                else:
                                    dve.wait_ge(part_set, n + 1)
                                nc.vector.scalar_tensor_tensor(H[:, col(n, D)], y[:, u, k, t, :], core.weight[:, k, bass.ds(n, 1)],
                                                               H[:, col(n, D)], ALU.mult, ALU.add).then_inc((part_set, out_set)[k], 1)

            @block.scalar
            def _(act):
                for b in range(B):
                    act.wait_ge(out_set, (b + 1) * TB)
                    act.dma_start(core.out[b].rearrange("(i p) c -> p i c", p=P),
                                  H[:, b * TB * D:(b + 1) * TB * D].rearrange("p (i c) -> p i c", i=TB)).then_inc(out_done, 16)
                act.wait_ge(out_done, 16 * B)



PHASES = (embed_phase, project_phase, conv_phase, mix_out_phase, attention_phase, route_phase, expert_phase,
          combine_phase)


def build_program(nc, a, out):
    with ExitStack() as ctx:
        core = Core(nc, a, out, ctx)
        for phase in PHASES:
            phase(core)


_OUT = ((B, S, D), "float32")


def lay_out(x, txt, L0_tok_W, L0_tok_b, L0_attn_w_in, L0_attn_b_in, L0_attn_w_filt, L0_attn_b_filt,
            L0_attn_w_short, L0_attn_b_short, L0_attn_w_out, L0_attn_b_out, L0_ffn_ln1_g, L0_ffn_ln1_b,
            L0_ffn_qkv_w, L0_ffn_proj_w, L0_ffn_proj_b, L0_ffn_ln2_g, L0_ffn_ln2_b, L0_ffn_gate_w,
            L0_ffn_gate_b, L0_ffn_w1, L0_ffn_b1, L0_ffn_w2, L0_ffn_b2):
    x, w = np.asarray(x), np.asarray(L0_tok_W)
    patches = x.reshape(B, C, GRID, PATCH, GRID, PATCH).transpose(1, 3, 5, 0, 2, 4).reshape(KP, P, B * NPATCH)
    wtok = w.reshape(D, KP, P).transpose(2, 1, 0)
    ins = {
        "patches": patches.transpose(1, 0, 2).reshape(P, KP * B * NPATCH),
        "wtok": wtok.reshape(P, KP * D),
        "txt": txt, "tok_b": L0_tok_b, "w_in": L0_attn_w_in, "b_in": L0_attn_b_in, "w_filt": L0_attn_w_filt,
        "b_filt": L0_attn_b_filt, "short": np.concatenate([np.asarray(L0_attn_w_short)[:, 0, :], np.asarray(L0_attn_b_short)[:, None]], 1), "w_out": L0_attn_w_out,
        "b_out": L0_attn_b_out, "affine": np.stack([L0_ffn_ln1_g, L0_ffn_ln1_b, L0_ffn_ln2_g, L0_ffn_ln2_b], 1), "qkv_w": L0_ffn_qkv_w,
        "proj_w": L0_ffn_proj_w, "proj_b": L0_ffn_proj_b,
        "gate_w": L0_ffn_gate_w, "gate_b": L0_ffn_gate_b, "w1": L0_ffn_w1, "b1": L0_ffn_b1, "w2": L0_ffn_w2,
        "b2": L0_ffn_b2,
    } | shape_tables()
    return {k: np.ascontiguousarray(v) for k, v in ins.items()}


def kernel(**inputs):
    import concourse.bacc as bacc
    from concourse.bass_utils import run_bass_kernel_spmd
    arrays = lay_out(**inputs)
    nc = bacc.Bacc("TRN2", target_bir_lowering=False, num_devices=1)
    a = {k: nc.dram_tensor("in_" + k, v.shape, mybir.dt.from_np(v.dtype), kind="ExternalInput").ap() for k, v in arrays.items()}
    out = nc.dram_tensor("out_0_dram", _OUT[0], F32, kind="ExternalOutput").ap()
    build_program(nc, a, out)
    if not nc.is_finalized():
        nc.finalize()
    r = run_bass_kernel_spmd(nc, [{"in_" + k: v for k, v in arrays.items()}], core_ids=[0])
    return np.asarray(r.results[0]["out_0_dram"])
```

```python
from contextlib import ExitStack

import numpy as np

import concourse.bass as bass
from concourse import mybir

F32 = mybir.dt.float32
BF16 = mybir.dt.bfloat16
U32 = mybir.dt.uint32
I32 = mybir.dt.int32
ALU = mybir.AluOpType
ACT = mybir.ActivationFunctionType
AX = mybir.AxisListType

P = 128
B, C, IMG, PATCH, D = 8, 3, 96, 16, 192
GRID = IMG // PATCH
NPATCH = GRID * GRID
N_IMG, N_TXT = 256, 512
S = N_IMG + N_TXT
TB = S // P
NT = B * TB
T_IMG = N_IMG // P
KPATCH = C * PATCH * PATCH
KP = KPATCH // P
HALF = D // 2
FREQ = 64
EPS = 1e-5
CH = 16
NCHUNK = D // CH
TG = 4
TROW = 384
HB = TB // 2
HEADS, HD = 12, 16
GH = 4
NG = HEADS // GH
QH = S // 2
SPLIT = 6 * HD
AUG = 3
KROWS = SPLIT + AUG
VW = HD + 1
E, TOPK, HID = 8, 2, 768
KH = HID // P
NSLOT = NT * TOPK + E
SLOTS = NSLOT * P


def hilbert_points(p):
    n = 1 << p
    pts = np.zeros((n * n, 2), dtype=np.int32)
    for d in range(n * n):
        t, x, y, s = d, 0, 0, 1
        while s < n:
            rx = 1 & t // 2
            ry = 1 & (t ^ rx)
            if ry == 0:
                if rx == 1:
                    x, y = s - 1 - x, s - 1 - y
                x, y = y, x
            x, y = x + s * rx, y + s * ry
            t //= 4
            s *= 2
        pts[d] = x, y
    return pts


def shape_tables():
    f32 = np.float32
    f = np.arange(FREQ, dtype=np.float64)
    taps = np.r_[np.arange(S - P + 1, S), np.arange(P)].astype(np.float64)
    basis = np.ones((FREQ + 1, len(taps)))
    basis[:FREQ] = np.sin(f[:, None] * taps[None, :] / FREQ)
    s = np.arange(S, dtype=np.float64)
    phi = np.concatenate([np.sin(s[:, None] * f / FREQ), np.cos(s[:, None] * f / FREQ)], 1)
    u = s - S // 2
    psi = np.concatenate([np.cos(f[:, None] * u / FREQ), -np.sin(f[:, None] * u / FREQ)], 0)
    psi[FREQ] = 1.0
    pts = np.minimum(hilbert_points(4), GRID - 1)
    pick = np.zeros((2 * NPATCH, 2, T_IMG, P))
    for d in range(N_IMG):
        for r in range(2):
            pick[r * NPATCH + pts[d, 0] * GRID + pts[d, 1], r, d // P, d % P] = 1.0
    return {
        "basis": basis.astype(f32),
        "phi": phi.reshape(TB, P, 2 * FREQ).transpose(1, 0, 2).astype(f32).copy(),
        "psi": psi.reshape(2 * FREQ, TB, P).astype(f32).copy(),
        "pick": pick.astype(f32).reshape(2 * NPATCH, 2 * T_IMG * P),
        "ident": np.eye(P, dtype=f32),
        "steps": np.broadcast_to(np.arange(NSLOT, dtype=f32), (P, NSLOT)),
        "ids": (np.arange(P)[:, None, None] + P * np.arange(NT)[None, :, None] + NT * P * np.arange(TOPK)).astype(f32),
        "spare": (TOPK * NT * P + np.arange(SLOTS)).reshape(NSLOT // 8, P, 8).transpose(1, 0, 2).astype(f32),
        "before": np.triu(np.ones((P, P), f32), 1),
    }


def col(n, width):
    return bass.ds(n * width, width)


class Core:

    def __init__(self, nc, a, out, ctx):
        self.nc, self.a, self.out, self.ctx = nc, a, out, ctx

        def sb(name, shape, dt=F32):
            return ctx.enter_context(nc.sbuf_tensor(name, shape, dt))

        self.H = sb("h_resid", [P, NT * D])
        self.XA = sb("x_proj_then_x", [P, NT * D])
        self.GY = sb("gate_then_w2", [P, NT * D])
        self.XS = sb("short_then_w1", [P, NT * P * 2])
        self.ident = sb("ident", [P, P])
        self.stats = sb("ln_stats", [P, NT * 6])
        self.mean = sb("ln_mean", [P, NT])
        self.var = sb("ln_var", [P, NT])
        self.dif = sb("ln_dif", [P, NT])
        self.rstd = sb("rstd", [P, NT])
        self.powers = sb("minus_half", [P, NT])
        self.ps = ctx.enter_context(nc.psum_tensor("ps", [P, 8, 512], F32))
        self.filt_dram = nc.dram_tensor("filt_rows", (D, TROW), F32, kind="Internal").ap()
        self.slot_x = nc.dram_tensor("slot_x", (SLOTS, D + 1), F32, kind="Internal").ap()
        self.tok_y = nc.dram_tensor("tok_y", (TOPK * NT * P + SLOTS, D), F32, kind="Internal").ap()
        self.weight = sb("expert_weight", [P, TOPK, NT])
        self.b2 = sb("expert_b2", [P, E, D])
        self.tile_expert = sb("tile_expert", [P, NSLOT], I32)
        self.W1 = self.XS[0:HALF + 1, :].rearrange("p (e c n) -> p e c n", e=E, c=2)
        self.W2 = self.GY[:, :].rearrange("p (e j n) -> p e j n", e=E, j=KH)


def rsqrt_on_pool(nc, pool, core, var_set, step, rstd_set):
    pool.wait_ge(var_set, 1)
    nc.gpsimd.tensor_scalar(core.rstd[:, :], core.var[:, :], EPS, None, ALU.add).then_inc(step, 1)
    pool.wait_ge(step, 1)
    nc.gpsimd.tensor_tensor(core.rstd[:, :], core.rstd[:, :], core.powers[:, :], ALU.pow).then_inc(rstd_set, 1)


def all_stats(nc, dve, core, src, st_set):
    with dve.Fori(0, B) as b:
        for i in range(TB):
            n = b * TB + i
            nc.vector.bn_stats(core.stats[:, col(n, 6)], src[:, col(n, D)]).then_inc(st_set, 1)


def mean_and_var(nc, dve, core, st_set, step, var_set):
    st = core.stats[:, :].rearrange("p (n k) -> p n k", k=6)
    even, odd, sq_even, sq_odd = st[:, :, 1], st[:, :, 4], st[:, :, 2], st[:, :, 5]
    dve.wait_ge(st_set, NT)
    nc.vector.tensor_tensor(core.mean[:, :], even, odd, ALU.add).then_inc(step, 1)
    nc.vector.tensor_tensor(core.dif[:, :], even, odd, ALU.subtract).then_inc(step, 1)
    nc.vector.tensor_tensor(core.var[:, :], sq_even, sq_odd, ALU.add).then_inc(step, 1)
    dve.wait_ge(step, 3)
    nc.vector.tensor_scalar(core.mean[:, :], core.mean[:, :], 0.5, None, ALU.mult).then_inc(step, 1)
    nc.vector.scalar_tensor_tensor(core.dif[:, :], core.dif[:, :], 0.25, core.dif[:, :], ALU.mult, ALU.mult).then_inc(step, 1)
    dve.wait_ge(step, 5)
    nc.vector.scalar_tensor_tensor(core.var[:, :], core.var[:, :], 1.0 / D, core.dif[:, :], ALU.mult, ALU.add).then_inc(var_set, 1)


def embed_phase(core):
    nc, a, H, ps = core.nc, core.a, core.H, core.ps
    with ExitStack() as ctx:
        def sb(name, shape, dt=F32):
            return ctx.enter_context(nc.sbuf_tensor(name, shape, dt))

        def sem(name):
            return ctx.enter_context(nc.semaphore(name))

        patches = sb("patches", [P, KP * B * NPATCH])
        wtok = sb("wtok", [P, KP * D])
        tokb = sb("tokb", [2 * NPATCH, D])
        emb = sb("emb", [2 * NPATCH, 4 * D])
        pick = sb("pick", [2 * NPATCH, 2 * T_IMG * P])
        basis = sb("basis", [FREQ + 1, 2 * P - 1])
        wfilt = sb("wfilt_bias", [FREQ + 1, D])
        rows = sb("filter_rows", [HALF, 2, TROW])
        filt_in, tok_in, pick_in, txt_in = sem("e_filt_in"), sem("e_tok_in"), sem("e_pick_in"), sem("e_txt_in")
        filt_mm, rows_set, rows_zero, rows_out = sem("e_filt_mm"), sem("e_rows_set"), sem("e_rows_zero"), sem("e_rows_out")
        emb_mm, emb_set, tok_mm, tok_set = sem("e_emb_mm"), sem("e_emb_set"), sem("e_tok_mm"), sem("e_tok_set")
        st_set, dve_step, var_set, pool_step, rstd_set = sem("e_st_set"), sem("e_dve_step"), sem("e_var_set"), sem("e_pool_step"), sem("e_rstd_set")
        powers_set = sem("e_powers_set")
        h_tiles = H[:, :].rearrange("p (b i c) -> p b i c", b=B, i=TB)
        with nc.Block() as block:
            @block.sync
            def _(sp):
                sp.dma_start(wfilt[0:FREQ, :], a["w_filt"]).then_inc(filt_in, 16)
                sp.dma_start(wfilt[FREQ:FREQ + 1, :], a["b_filt"].rearrange("(a c) -> a c", a=1)).then_inc(filt_in, 16)
                sp.dma_start(basis[:, :], a["basis"]).then_inc(filt_in, 16)
                sp.dma_start(wtok[:, :], a["wtok"]).then_inc(tok_in, 16)
                sp.dma_start(patches[:, :], a["patches"]).then_inc(tok_in, 16)
                sp.dma_start(tokb[:, :], a["tok_b"].rearrange("(a c) -> a c", a=1).broadcast_to((2 * NPATCH, D))).then_inc(tok_in, 16)
                sp.dma_start(pick[:, :], a["pick"]).then_inc(pick_in, 16)
                sp.wait_ge(rows_out, 16)

            @block.scalar
            def _(act):
                act.dma_start(core.ident[:, :], a["ident"]).then_inc(pick_in, 16)
                for b in range(B):
                    act.dma_start(h_tiles[:, b, T_IMG:TB, :], a["txt"][b].rearrange("(i p) c -> p i c", p=P)).then_inc(txt_in, 16)
                act.wait_ge(rows_set, 2)
                act.dma_start(core.filt_dram.rearrange("(h c) t -> c h t", h=2), rows[:, :, :]).then_inc(rows_out, 16)

            @block.gpsimd
            def _(pool):
                nc.gpsimd.memset(rows[:, :, :], 0.0).then_inc(rows_zero, 1)
                nc.gpsimd.memset(core.powers[:, :], -0.5).then_inc(powers_set, 1)
                pool.wait_ge(powers_set, 1)
                rsqrt_on_pool(nc, pool, core, var_set, pool_step, rstd_set)
                pool.wait_ge(rstd_set, 1)

            @block.tensor
            def _(pe):
                pe.wait_ge(filt_in, 48)
                for h in range(2):
                    nc.tensor.matmul(ps[0:HALF, h, 0:2 * P - 1], wfilt[:, h * HALF:(h + 1) * HALF], basis[:, :],
                                     start=True, stop=True).then_inc(filt_mm, 1)
                pe.wait_ge(tok_in, 48)
                for m in range(4):
                    for k in range(KP):
                        off = k * B * NPATCH + m * 2 * NPATCH
                        last = nc.tensor.matmul(ps[0:2 * NPATCH, 2 + m % 2, 0:D], patches[:, off:off + 2 * NPATCH],
                                                wtok[:, k * D:(k + 1) * D], start=(k == 0), stop=(k == KP - 1))
                    last.then_inc(emb_mm, 1)
                    if m >= 1:
                        pe.wait_ge(emb_set, m)
                pe.wait_ge(emb_set, 4)
                pe.wait_ge(pick_in, 32)
                for t in range(B * T_IMG):
                    b, i = t // T_IMG, t % T_IMG
                    m, r = b // 2, b % 2
                    if t >= 4:
                        pe.wait_ge(tok_set, t - 3)
                    off = (r * T_IMG + i) * P
                    nc.tensor.matmul(ps[:, 4 + t % 4, 0:D], pick[:, off:off + P], emb[:, m * D:(m + 1) * D],
                                     start=True, stop=True).then_inc(tok_mm, 1)

            @block.vector
            def _(dve):
                dve.wait_ge(rows_zero, 1)
                for h in range(2):
                    dve.wait_ge(filt_mm, h + 1)
                    nc.vector.tensor_copy(rows[:, h, 0:P - 1], ps[0:HALF, h, 0:P - 1])
                    nc.vector.tensor_copy(rows[:, h, 2 * P - 1:3 * P - 1], ps[0:HALF, h, P - 1:2 * P - 1]).then_inc(rows_set, 1)
                for m in range(4):
                    dve.wait_ge(emb_mm, m + 1)
                    nc.vector.tensor_tensor(emb[:, m * D:(m + 1) * D], ps[0:2 * NPATCH, 2 + m % 2, 0:D], tokb[:, :],
                                            ALU.add).then_inc(emb_set, 1)
                for t in range(B * T_IMG):
                    b, i = t // T_IMG, t % T_IMG
                    dve.wait_ge(tok_mm, t + 1)
                    nc.vector.tensor_copy(h_tiles[:, b, i, :], ps[:, 4 + t % 4, 0:D]).then_inc(tok_set, 1)
                dve.wait_ge(tok_set, B * T_IMG)
                dve.wait_ge(txt_in, 16 * B)
                all_stats(nc, dve, core, H, st_set)
                mean_and_var(nc, dve, core, st_set, dve_step, var_set)


def project_phase(core):
    nc, a, H, ps = core.nc, core.a, core.H, core.ps
    with ExitStack() as ctx:
        def sb(name, shape, dt=F32):
            return ctx.enter_context(nc.sbuf_tensor(name, shape, dt))

        def sem(name):
            return ctx.enter_context(nc.semaphore(name))

        w_in = sb("w_in", [HALF + 1, 2, 4 * D])
        hn = sb("hn", [P, 2, D])
        hnT = sb("hnT", [HALF + 1, 2, 2, S + 2])
        sz = sb("silu_z", [P, 2, D])
        szv = sb("silu_z_v1", [P, 2, D])
        wsh = sb("w_short", [HALF, 2, 4])
        empty = sb("empty_slots", [P, 2, 8, D + 1])
        spare = sb("spare_rows", [P, NSLOT // 8, 8])
        spare_in, zero_set, spare_set, empty_out = sem("p_spare_in"), sem("p_zero_set"), sem("p_spare_set"), [sem(f"p_empty_out{u}") for u in range(2)]
        w_ready, hn_set, t_ready, hnT_set = sem("p_w_ready"), sem("p_hn_set"), sem("p_t_ready"), sem("p_hnT_set")
        zx_ready, zx_free, sz_set, szv_set, g_set = sem("p_zx_ready"), sem("p_zx_free"), sem("p_sz_set"), sem("p_szv_set"), sem("p_g_set")
        edges, ones_set, xs_step = sem("p_edges"), sem("p_ones_set"), sem("p_xs_step")
        XS = core.XS[0:HALF, :].rearrange("p (c t) -> p c t", c=2)
        with nc.Block() as block:
            @block.sync
            def _(sp):
                sp.dma_start(w_in[0:HALF, :, :], a["w_in"].rearrange("(c k) n -> k c n", c=2)).then_inc(w_ready, 16)
                sp.dma_start(w_in[HALF:HALF + 1, 1, :], a["b_in"].rearrange("(a c) -> a c", a=1)).then_inc(w_ready, 16)
                sp.dma_start(wsh[:, :, :], a["short"].rearrange("(c k) t -> k c t", c=2)).then_inc(w_ready, 16)
                sp.dma_start(spare[:, :, :], a["spare"]).then_inc(spare_in, 16)
                for k in range(NSLOT // 8):
                    sp.wait_ge(spare_set, k + 1)
                    sp.dma_start(core.slot_x[k * 8 * P:(k + 1) * 8 * P, :].rearrange("(p r) c -> p r c", r=8),
                                 empty[:, k % 2, :, :]).then_inc(empty_out[k % 2], 16)
                for u in range(2):
                    sp.wait_ge(empty_out[u], 16 * ((NSLOT // 8 + 1 - u) // 2))

            @block.gpsimd
            def _(pool):
                nc.gpsimd.memset(hnT[0:HALF, :, :, 0:1], 0.0).then_inc(edges, 1)
                nc.gpsimd.memset(hnT[0:HALF, :, :, S + 1:S + 2], 0.0).then_inc(edges, 1)
                pool.wait_ge(edges, 2)
                nc.gpsimd.memset(empty[:, :, :, :], 0.0).then_inc(zero_set, 1)
                pool.wait_ge(zero_set, 1)
                pool.wait_ge(spare_in, 16)
                for k in range(NSLOT // 8):
                    if k >= 2:
                        pool.wait_ge(empty_out[k % 2], 16 * (k // 2))
                    nc.gpsimd.tensor_copy(empty[:, k % 2, :, D], spare[:, k, :]).then_inc(spare_set, 1)

            @block.vector
            def _(dve):
                def norm(n, u):
                    nc.vector.tensor_scalar(hn[:, u, :], H[:, col(n, D)], core.mean[:, bass.ds(n, 1)],
                                            core.rstd[:, bass.ds(n, 1)], ALU.subtract, ALU.mult).then_inc(hn_set, 1)

                def gate(n, u):
                    dve.wait_ge(sz_set, n + 1)
                    nc.vector.tensor_tensor(szv[:, u, :], sz[:, u, :], ps[:, 2 + u, D:2 * D], ALU.mult).then_inc(szv_set, 1)
                    dve.wait_ge(szv_set, n + 1)
                    nc.vector.tensor_tensor(core.GY[:, col(n, D)], szv[:, u, :], ps[:, 4 + u, 0:D], ALU.mult).then_inc(g_set, 1)

                def short_conv(b, w, k):
                    tap, c = k // 2, k % 2
                    out = XS[:, c, bass.ds(b * S, S)]
                    if tap == 0:
                        nc.vector.tensor_scalar(out, hnT[0:HALF, w, c, 0:S], wsh[:, c, 0:1], wsh[:, c, 3:4],
                                                ALU.mult, ALU.add).then_inc(xs_step, 1)
                    else:
                        dve.wait_ge(xs_step, b * 6 + k)
                        nc.vector.scalar_tensor_tensor(out, hnT[0:HALF, w, c, tap:tap + S], wsh[:, c, tap:tap + 1], out,
                                                       ALU.mult, ALU.add).then_inc(xs_step, 1)

                def batch(b, w, first, last):
                    for i in range(TB):
                        n, u = b * TB + i, i % 2
                        if not (last and i == TB - 1):
                            norm(n + 1, 1 - u)
                        dve.wait_ge(t_ready, n + 1)
                        if i == 0 and not first:
                            dve.wait_ge(xs_step, (b - 1) * 6 + 1)
                        nc.vector.tensor_copy(hnT[0:HALF, w, :, 1 + i * P:1 + (i + 1) * P],
                                              ps[0:HALF, u, 0:2 * P].rearrange("p (c t) -> p c t", c=2)).then_inc(hnT_set, 1)
                        if not (first and i == 0):
                            gate(n - 1, 1 - u)
                        if not first:
                            short_conv(b - 1, 1 - w, i)

                dve.sem_inc(xs_step, 1)
                norm(0, 0)
                nc.vector.memset(hnT[HALF:HALF + 1, :, :, :], 1.0).then_inc(ones_set, 1)
                dve.wait_ge(w_ready, 48)
                dve.wait_ge(edges, 2)
                batch(0, 0, True, False)
                with dve.Fori(0, B // 2 - 1) as i:
                    batch(i * 2 + 1, 1, False, False)
                    batch(i * 2 + 2, 0, False, False)
                batch(B - 1, 1, False, True)
                gate(NT - 1, 1)
                for k in range(6):
                    short_conv(B - 1, 1, k)

            @block.tensor
            def _(pe):
                def transpose(n, u):
                    pe.wait_ge(hn_set, n + 1)
                    for c in range(2):
                        last = nc.tensor.transpose(ps[0:HALF, u, c * P:(c + 1) * P], hn[:, u, c * HALF:(c + 1) * HALF], core.ident[:, :])
                    last.then_inc(t_ready, 1)

                def batch(b, w, last):
                    for i in range(TB):
                        n, u = b * TB + i, i % 2
                        if not (last and i == TB - 1):
                            transpose(n + 1, 1 - u)
                        pe.wait_ge(hnT_set, n + 1)
                        pe.wait_ge(zx_free, n + 1)
                        t = slice(1 + i * P, 1 + (i + 1) * P)
                        for bank, at, c0, cols in ((2, 0, D, 2 * D), (4, 0, 3 * D, D), (4, D, 0, D)):
                            nc.tensor.matmul(ps[:, bank + u, at:at + cols], hnT[0:HALF, w, 0, t], w_in[0:HALF, 0, c0:c0 + cols], start=True, stop=False)
                            mm = nc.tensor.matmul(ps[:, bank + u, at:at + cols], hnT[:, w, 1, t], w_in[:, 1, c0:c0 + cols], start=False, stop=True)
                        mm.then_inc(zx_ready, 1)

                transpose(0, 0)
                pe.wait_ge(w_ready, 48)
                pe.wait_ge(edges, 2)
                pe.wait_ge(ones_set, 1)
                with pe.Fori(0, B // 2 - 1) as i:
                    for w in range(2):
                        batch(i * 2 + w, w, False)
                batch(B - 2, 0, False)
                batch(B - 1, 1, True)

            @block.scalar
            def _(act):
                act.sem_inc(zx_free, 2)

                def silu(n, u):
                    act.wait_ge(zx_ready, n + 1)
                    nc.scalar.activation(sz[:, u, :], ps[:, 2 + u, 0:D], ACT.Silu).then_inc(sz_set, 1)

                def keep_x(n, u):
                    act.wait_ge(g_set, n + 1)
                    nc.scalar.activation(core.XA[:, col(n, D)], ps[:, 4 + u, D:2 * D], ACT.Copy).then_inc(zx_free, 1)

                with act.Fori(0, NT // 2) as i:
                    for u in range(2):
                        silu(i * 2 + u, u)
                        keep_x(i * 2 + u, u)


def conv_phase(core):
    nc, a, ps = core.nc, core.a, core.ps
    with ExitStack() as ctx:
        def sb(name, shape, dt=F32):
            return ctx.enter_context(nc.sbuf_tensor(name, shape, dt))

        def sem(name):
            return ctx.enter_context(nc.semaphore(name))

        phi = sb("phi", [P, TB, P])
        psi = sb("psi", [P, TB, P])
        wf = sb("w_features", [P, D])
        toep = sb("toeplitz", [P, TG, TG, 2 * P])
        xc = sb("x_chunk", [P, CH, 2, 32])
        zw = sb("weighted_features", [P, TB, CH, B])
        edge = sb("edge_rows", [P, 2, TG, P])
        tab_in, xc_zero, xc_set, xc_free = sem("c_tab_in"), sem("c_xc_zero"), sem("c_xc_set"), sem("c_xc_free")
        toep_in = [sem(f"c_toep_in{g}") for g in range(TG)]
        toep_free = sem("c_toep_free")
        z_ready, zw_set, edge_mm, edge_set = sem("c_z_ready"), sem("c_zw_set"), sem("c_edge_mm"), sem("c_edge_set")
        y_ready, y_set, y_free = sem("c_y_ready"), sem("c_y_set"), sem("c_y_free")
        x4 = core.XA[:, :].rearrange("p (b i c) -> p b i c", b=B, i=TB)
        g4 = core.GY[:, :].rearrange("p (b i c) -> p b i c", b=B, i=TB)
        CHAINS = [(0, (0, 1, 2), 0), (1, (5, 4, 3), 5), (0, (3,), 1), (1, (2,), 4), (0, (4,), 2), (1, (1,), 3)]
        with nc.Block() as block:
            @block.sync
            def _(sp):
                sp.dma_start(phi[:, :, :], a["phi"]).then_inc(tab_in, 16)
                sp.dma_start(psi[:, :, :], a["psi"]).then_inc(tab_in, 16)
                sp.dma_start(wf[0:FREQ, :], a["w_filt"]).then_inc(tab_in, 16)
                sp.dma_start(wf[FREQ + 1:P, :], a["w_filt"][1:FREQ, :]).then_inc(tab_in, 16)
                sp.dma_start(wf[FREQ:FREQ + 1, :], a["b_filt"].rearrange("(a c) -> a c", a=1)).then_inc(tab_in, 16)
                with sp.Fori(0, NCHUNK) as q:
                    for g in range(TG):
                        sp.wait_ge(toep_free, q * TG + (g + 1))
                        rows = core.filt_dram[bass.ds(q * CH + g * TG, TG), 0:2 * P]
                        src = bass.AP(rows.tensor, rows.offset, [[1, P], [TROW, TG], [1, 2 * P]])
                        sp.dma_start(toep[:, g, :, :], src).then_inc(toep_in[g], 16)

            @block.gpsimd
            def _(pool):
                nc.gpsimd.memset(xc[:, :, :, :], 0.0).then_inc(xc_zero, 1)
                pool.wait_ge(xc_zero, 1)
                with pool.Fori(0, NCHUNK) as q:
                    pool.wait_ge(xc_free, q + 1)
                    for half in range(2):
                        src = x4[:, :, HB * (1 - half):HB * (2 - half), bass.ds(q * CH, CH)].rearrange("p b i c -> p c i b")
                        dst = xc[:, :, half, 0:HB * B].rearrange("p c (i b) -> p c i b", i=HB)
                        nc.gpsimd.tensor_copy(dst, src).then_inc(xc_set, 1)

            @block.tensor
            def _(pe):
                pe.sem_inc(toep_free, TG)
                pe.sem_inc(xc_free, 1)
                pe.wait_ge(tab_in, 80)
                with pe.Fori(0, NCHUNK) as q:
                    for k, (bank, blocks, out) in enumerate(CHAINS):
                        if k >= 2:
                            pe.wait_ge(zw_set, q * 6 + (k - 1))
                        else:
                            pe.wait_ge(y_free, q * 2 + (k + 1))
                        for j in blocks:
                            mm = nc.tensor.matmul(ps[:, bank, 0:B * CH], phi[:, j, :], x4[:, :, j, bass.ds(q * CH, CH)],
                                                  start=(k < 2 and j == blocks[0]), stop=True, skip_group_check=True)
                        mm.then_inc(z_ready, 1)
                    pe.wait_ge(xc_set, q * 2 + 2)
                    pe.wait_ge(edge_set, q * 2 + 2)
                    for g in range(TG):
                        pe.wait_ge(toep_in[g], (q + 1) * 16)
                        for half in range(2):
                            for j in range(TG):
                                mm = nc.tensor.matmul(ps[32 * j:32 * j + 32, 2 + half, g * P:(g + 1) * P], xc[:, g * TG + j, half, :],
                                                      toep[:, g, j, half * P:(half + 1) * P], start=True, stop=True)
                        mm.then_inc(toep_free, 1)
                    pe.wait_ge(toep_free, q * TG + 2 * TG)
                    pe.sem_inc(xc_free, 1)
                    pe.sem_inc(edge_mm, 1)
                    for half in range(2):
                        for i in range(HB):
                            out = half * HB + i
                            k = [c[2] for c in CHAINS].index(out)
                            pe.wait_ge(zw_set, q * 6 + (k + 1))
                            dst = ps[:, 4 + half, :].rearrange("p (c k) -> p c k", k=32)[:, :, i * B:(i + 1) * B]
                            nc.tensor.matmul(dst, psi[:, out, :], zw[:, out, :, :], start=(i == 0), stop=True, skip_group_check=True)
                        pe.wait_ge(edge_set, q * 2 + (half + 3))
                        for g in range(TG):
                            mm = nc.tensor.matmul(ps[:, 4 + half, g * P:(g + 1) * P], edge[:, half, g, :], core.ident[:, :],
                                                  start=False, stop=True, skip_group_check=True)
                        mm.then_inc(y_ready, 1)

            @block.scalar
            def _(act):
                act.sem_inc(edge_set, 2)
                with act.Fori(0, NCHUNK) as q:
                    act.wait_ge(edge_mm, q + 1)
                    for half in range(2):
                        act.wait_ge(y_free, q * 2 + (half + 1))
                        src = ps[:, 2 + half, :].rearrange("p (g t) -> p g t", g=TG)[:, :, ::-1]
                        nc.scalar.activation(edge[:, half, :, :], src, ACT.Copy).then_inc(edge_set, 1)

            @block.vector
            def _(dve):
                dve.sem_inc(y_free, 2)
                dve.wait_ge(tab_in, 80)
                with dve.Fori(0, NCHUNK) as q:
                    for k, (bank, _, out) in enumerate(CHAINS):
                        dve.wait_ge(z_ready, q * 6 + (k + 1))
                        dst = zw[:, out, :, :].rearrange("p c b -> p b c")
                        src = ps[:, bank, 0:B * CH].rearrange("p (b c) -> p b c", b=B)
                        w = wf[:, bass.ds(q * CH, CH)].rearrange("p (a c) -> p a c", a=1).broadcast_to((P, B, CH))
                        nc.vector.tensor_tensor(dst, src, w, ALU.mult).then_inc(zw_set, 1)
                    for half in range(2):
                        dve.wait_ge(y_ready, q * 2 + (half + 1))
                        src = ps[:, 4 + half, :].rearrange("p (c k) -> p c k", k=32)[:, :, 0:HB * B]
                        src = src.rearrange("p c (i b) -> p b i c", i=HB)
                        y = g4[:, :, half * HB:(half + 1) * HB, bass.ds(q * CH, CH)]
                        nc.vector.tensor_tensor(y, src, y, ALU.mult).then_inc(y_free, 1)


def mix_out_phase(core):
    nc, a, H, ps = core.nc, core.a, core.H, core.ps
    with ExitStack() as ctx:
        def sb(name, shape, dt=F32):
            return ctx.enter_context(nc.sbuf_tensor(name, shape, dt))

        def sem(name):
            return ctx.enter_context(nc.semaphore(name))

        w_out = sb("w_out", [HALF + 1, 2, D])
        yt = sb("y_tile", [P, 2, D])
        sT = sb("sumT", [HALF + 1, 2, 2, P])
        w_ready, ones, yt_set, t_ready, sT_set = sem("o_w_ready"), sem("o_ones"), sem("o_yt_set"), sem("o_t_ready"), sem("o_sT_set")
        o_ready, h_set, st_set, var_set = sem("o_o_ready"), sem("o_h_set"), sem("o_st_set"), sem("o_var_set")
        x_set, st2_set, var2_set, dve_step, dve_step2 = sem("o_x_set"), sem("o_st2_set"), sem("o_var2_set"), sem("o_dve_step"), sem("o_dve_step2")
        pool_step2, rstd_set, rstd2_set = sem("o_pool_step2"), sem("o_rstd_set"), sem("o_rstd2_set")
        stats = sb("h_stats", [P, TB, 6])
        mean, var, dif, rstd = (sb("h_" + k, [P, TB]) for k in ("mean", "var", "dif", "rstd"))
        XS = core.XS[0:HALF, :].rearrange("p (c t) -> p c t", c=2)
        NP = NT // 2
        with nc.Block() as block:
            @block.sync
            def _(sp):
                sp.dma_start(w_out[0:HALF, :, :], a["w_out"].rearrange("(c k) n -> k c n", c=2)).then_inc(w_ready, 16)
                sp.dma_start(w_out[HALF:HALF + 1, 1, :], a["b_out"].rearrange("(a c) -> a c", a=1)).then_inc(w_ready, 16)

            @block.gpsimd
            def _(pool):
                nc.gpsimd.memset(sT[HALF:HALF + 1, :, :, :], 1.0).then_inc(ones, 1)
                pool.wait_ge(ones, 1)
                with pool.Fori(0, B) as b:
                    pool.wait_ge(var_set, b + 1)
                    nc.gpsimd.tensor_tensor(rstd[:, :], var[:, :], core.powers[:, 0:TB], ALU.pow).then_inc(rstd_set, 1)
                rsqrt_on_pool(nc, pool, core, var2_set, pool_step2, rstd2_set)
                pool.wait_ge(rstd2_set, 1)

            @block.scalar
            def _(act):
                for u in range(2):
                    nc.scalar.activation(yt[:, u, :], core.GY[:, col(u, D)], ACT.Copy).then_inc(yt_set, 1)
                with act.Fori(1, NP) as i:
                    for u in range(2):
                        act.wait_ge(t_ready, i * 2 + (u - 1))
                        nc.scalar.activation(yt[:, u, :], core.GY[:, col(i * 2 + u, D)], ACT.Copy).then_inc(yt_set, 1)

            @block.tensor
            def _(pe):
                def transpose(n, u):
                    pe.wait_ge(yt_set, n + 1)
                    for c in range(2):
                        mm = nc.tensor.transpose(ps[0:HALF, u, c * P:(c + 1) * P], yt[:, u, c * HALF:(c + 1) * HALF], core.ident[:, :])
                    mm.then_inc(t_ready, 1)

                def pair(i, last):
                    for u in range(2):
                        n = i * 2 + u
                        if not (last and u == 1):
                            transpose(n + 1, 1 - u)
                        pe.wait_ge(sT_set, n + 1)
                        pe.wait_ge(h_set, n + 1)
                        nc.tensor.matmul(ps[:, 2 + u, 0:D], sT[0:HALF, u, 0, :], w_out[0:HALF, 0, :], start=True, stop=False)
                        nc.tensor.matmul(ps[:, 2 + u, 0:D], sT[:, u, 1, :], w_out[:, 1, :], start=False, stop=True).then_inc(o_ready, 1)

                pe.wait_ge(w_ready, 32)
                pe.wait_ge(ones, 1)
                transpose(0, 0)
                with pe.Fori(0, NP - 1) as i:
                    pair(i, False)
                pair(NP - 1, True)

            @block.vector
            def _(dve):
                dve.sem_inc(h_set, 2)

                def add_short(n, u):
                    dve.wait_ge(t_ready, n + 1)
                    nc.vector.tensor_tensor(sT[0:HALF, u, :, :], ps[0:HALF, u, 0:2 * P].rearrange("p (c t) -> p c t", c=2),
                                            XS[:, :, col(n, P)], ALU.add).then_inc(sT_set, 1)

                def resid(n, u):
                    dve.wait_ge(o_ready, n + 1)
                    dve.wait_ge(h_set, n + 2)
                    nc.vector.tensor_tensor(H[:, col(n, D)], ps[:, 2 + u, 0:D], H[:, col(n, D)], ALU.add).then_inc(h_set, 1)

                def stat_h(n, i):
                    nc.vector.bn_stats(stats[:, i, :], H[:, col(n, D)]).then_inc(st_set, 1)

                def moments(b):
                    def then(k, op):
                        op.then_inc(dve_step, 1)
                        if k in (3, 5, 6):
                            dve.wait_ge(dve_step, b * 6 + k)

                    even, odd, sq_even, sq_odd = stats[:, :, 1], stats[:, :, 4], stats[:, :, 2], stats[:, :, 5]
                    dve.wait_ge(st_set, b * TB + TB)
                    then(1, nc.vector.tensor_tensor(mean[:, :], even, odd, ALU.add))
                    then(2, nc.vector.tensor_tensor(dif[:, :], even, odd, ALU.subtract))
                    then(3, nc.vector.tensor_tensor(var[:, :], sq_even, sq_odd, ALU.add))
                    then(4, nc.vector.tensor_scalar(mean[:, :], mean[:, :], 0.5, None, ALU.mult))
                    then(5, nc.vector.scalar_tensor_tensor(dif[:, :], dif[:, :], 0.25, dif[:, :], ALU.mult, ALU.mult))
                    then(6, nc.vector.scalar_tensor_tensor(var[:, :], var[:, :], 1.0 / D, dif[:, :], ALU.mult, ALU.add))
                    nc.vector.tensor_scalar(var[:, :], var[:, :], EPS, None, ALU.add).then_inc(var_set, 1)

                def norm_h(b, i):
                    if i == 0:
                        dve.wait_ge(rstd_set, b + 1)
                    n = b * TB + i
                    nc.vector.tensor_scalar(core.XA[:, col(n, D)], H[:, col(n, D)], mean[:, i:i + 1], rstd[:, i:i + 1],
                                            ALU.subtract, ALU.mult).then_inc(x_set, 1)

                def stat_x(b, i):
                    n = b * TB + i
                    dve.wait_ge(x_set, n + 1)
                    nc.vector.bn_stats(core.stats[:, col(n, 6)], core.XA[:, col(n, D)]).then_inc(st2_set, 1)

                NORM = {2: (0,), 3: (1, 2), 4: (3, 4), 5: (5,)}
                MEASURE = {3: (0,), 4: (1, 2), 5: (3, 4)}

                def batch(b, before, last):
                    for i in range(TB):
                        n = b * TB + i
                        if not (last and i == TB - 1):
                            add_short(n + 1, (i + 1) % 2)
                        resid(n, i % 2)
                        if i > 0:
                            stat_h(n - 1, i - 1)
                        elif before > 0:
                            stat_h(n - 1, TB - 1)
                            if before > 1:
                                stat_x(b - 2, TB - 1)
                            moments(b - 1)
                        if before > 0:
                            for k in NORM.get(i, ()):
                                norm_h(b - 1, k)
                            for k in MEASURE.get(i, ()):
                                stat_x(b - 1, k)

                add_short(0, 0)
                batch(0, 0, False)
                batch(1, 1, False)
                with dve.Fori(2, B - 1) as b:
                    batch(b, 2, False)
                batch(B - 1, 2, True)
                dve.wait_ge(h_set, NT + 2)
                stat_h(NT - 1, TB - 1)
                stat_x(B - 2, TB - 1)
                moments(B - 1)
                for i in range(TB):
                    norm_h(B - 1, i)
                for i in range(TB):
                    stat_x(B - 1, i)
                mean_and_var(nc, dve, core, st2_set, dve_step2, var2_set)


def attention_phase(core):
    nc, a, ps = core.nc, core.a, core.ps
    X = core.XA
    with ExitStack() as ctx:
        def sb(name, shape, dt=F32):
            return ctx.enter_context(nc.sbuf_tensor(name, shape, dt))

        def sem(name):
            return ctx.enter_context(nc.semaphore("a_" + name))

        QS = core.XS[0:KROWS, 0:HEADS * S // 2].bitcast(BF16).rearrange("p (h t) -> p h t", h=HEADS)
        KS = core.XS[0:KROWS, HEADS * S // 2:HEADS * S].bitcast(BF16).rearrange("p (h t) -> p h t", h=HEADS)
        PT2 = core.XS[:, HEADS * S:NT * P * 2].rearrange("p (u h t) -> p u h t", u=2, h=GH)
        V = core.GY[:, 0:TB * HEADS * 32].rearrange("p (i h c) -> p i h c", i=TB, h=HEADS)
        at = TB * HEADS * 32
        VN = core.GY[:, at:at + TB * D].rearrange("p (i c) -> p i c", i=TB)
        at += TB * D
        PT = [PT2[:, 0], PT2[:, 1], core.GY[:, at:at + GH * QH].rearrange("p (h t) -> p h t", h=GH)]
        at += GH * QH
        parts = core.GY[:, at:at + 9 * S // 2].bitcast(BF16).rearrange("p (k j t) -> p k j t", k=3, j=3)

        qkv_w = sb("qkv_w", [HALF, 2, 3 * D])
        proj_w = sb("proj_w", [HALF + 1, 2, D])
        aff = sb("affine1", [HALF, 2, 4])
        xn = sb("xn", [P, 2, D])
        hT = sb("hT", [HALF, 2, S])
        R = sb("qk_rest", [P, 3, S])
        mx = sb("half_max", [P, NG, GH * TB, 2])
        mxq = sb("score_max", [P, NG, GH * TB])
        nm = sb("minus_max", [GH * TB, 2, P])
        nm_parts = sb("minus_max_parts", [GH * TB, NG, 3, P], BF16)
        ov = sb("numer_denom", [P, QH])
        rc = sb("recip_denom", [P, HB, GH])
        O = sb("attn_out", [P, TB, D])
        oT = sb("attn_outT", [HALF + 1, 2, 2, P])
        qk_dram = nc.dram_tensor("qk_parts", (3, 2 * D, S), BF16, kind="Internal").ap()

        w_in, const_set, xn_set = sem("w_in"), sem("const_set"), sem("xn_set")
        prep_ready, prep_free, h_part, r_set, m_part, l_set = (sem(n) for n in ("prep_ready", "prep_free", "h_part", "r_set", "m_part", "l_set"))
        v_set, v_full, qk_out = sem("v_set"), sem("v_full"), sem("qk_out")
        qk_in = [sem(f"qk_in{g}") for g in range(NG)]
        s_ready, mx_set, nm_step, nm_set, aug_in = (sem(n) for n in ("s_ready", "mx_set", "nm_step", "nm_set", "aug_in"))
        st_ready, exp_set, pv_done, ov_set, rc_set = (sem(n) for n in ("st_ready", "exp_set", "pv_done", "ov_set", "rc_set"))
        b6_ready, b6_free, st_set = sem("b6_ready"), sem("b6_free"), sem("st_set")
        dve_step, var_set, pool_step, rstd_set = sem("dve_step"), sem("var_set"), sem("pool_step"), sem("rstd_set")

        MICRO = 2 * TB
        M_ALL = NG * MICRO
        UNITS = GH * TB * 2
        MAXIMA = UNITS + 1
        AHEAD = 16
        SB, XB = 3, 2
        JOBS = TB + 1 + 6
        PREP_AT = 1
        MIDDLE = {PREP_AT + TB + 4 + 2 * t: t for t in range(3)}
        B6 = {1: "o21"} | {2 + j: f"tail{j}" for j in range(TB + 1)} | {
            9: "m1", 10: "o00", 13: "o01", 19: "o10", 20: "m2", 25: "o11", 31: "o20", 32: "m0"}
        ORDER = list(B6.values())
        LATE = TB + 2

        def b6(b, what):
            if isinstance(b, int) and b < 0:
                return 0
            none = 1 if isinstance(b, int) and b == B else 0
            return b * len(ORDER) + (ORDER.index(what) - LATE + 1 - none)

        def ahead(b, M):
            return (b, M + AHEAD) if M + AHEAD < M_ALL else (b + 1, M + AHEAD - M_ALL)

        with nc.Block() as block:
            @block.sync
            def _(sp):
                sp.dma_start(qkv_w[:, :, :], a["qkv_w"].rearrange("(c k) n -> k c n", c=2)).then_inc(w_in, 16)
                sp.dma_start(proj_w[0:HALF, :, :], a["proj_w"].rearrange("(c k) n -> k c n", c=2)).then_inc(w_in, 16)
                sp.dma_start(proj_w[HALF:HALF + 1, 1, :], a["proj_b"].rearrange("(a c) -> a c", a=1)).then_inc(w_in, 16)
                sp.dma_start(aff[:, :, :], a["affine"].rearrange("(c k) t -> k c t", c=2)).then_inc(w_in, 16)

                def parts_out(nb, blocks):
                    for t in blocks:
                        sp.wait_ge(l_set, nb * 3 + (t + 1))
                        sp.dma_start(qk_dram[:, t * P:(t + 1) * P, :].rearrange("j p t -> p j t"), parts[:, t, :, :]).then_inc(qk_out, 16)

                def load(g):
                    hs = slice(g * GH, (g + 1) * GH)
                    row = 0
                    for part, times in ((0, 3), (1, 2), (2, 1)):
                        for _ in range(times):
                            src = qk_dram[part, g * GH * HD:(g + 1) * GH * HD, :].rearrange("(h r) t -> r h t", h=GH)
                            sp.dma_start(QS[row:row + HD, hs, :], src).then_inc(qk_in[g], 16)
                            row += HD
                    row = 0
                    for n in (3, 2, 1):
                        for part in range(n):
                            src = qk_dram[part, D + g * GH * HD:D + (g + 1) * GH * HD, :].rearrange("(h r) t -> r h t", h=GH)
                            sp.dma_start(KS[row:row + HD, hs, :], src).then_inc(qk_in[g], 16)
                            row += HD

                def maxima_in(b, g):
                    sp.wait_ge(nm_set, b * NG + (g + 1))
                    for j in range(3):
                        dst = QS[SPLIT + j:SPLIT + j + 1, g * GH:(g + 1) * GH, :].rearrange("a h (i t) -> a (h i) t", i=TB)
                        sp.dma_start(dst, nm_parts[:, g, j, :]).then_inc(aug_in, 16)

                def group_done(b, g):
                    sp.wait_ge(st_ready, b * (NG * MICRO * GH) + (g + 1) * MICRO * GH)

                parts_out(0, (0, 1))
                sp.wait_ge(qk_out, 32)
                load(0)
                parts_out(0, (2,))
                sp.wait_ge(qk_out, 48)
                for g in range(1, NG):
                    load(g)
                maxima_in(0, 0)
                with sp.Fori(0, B - 1) as b:
                    maxima_in(b, 1)
                    for g in range(NG):
                        sp.wait_ge(qk_in[g], b * 192 + 192)
                    parts_out(b + 1, (0, 1))
                    sp.wait_ge(qk_out, b * 48 + 80)
                    group_done(b, 0)
                    load(0)
                    parts_out(b + 1, (2,))
                    maxima_in(b, 2)
                    group_done(b, 1)
                    sp.wait_ge(qk_out, (b + 2) * 48)
                    load(1)
                    maxima_in(b + 1, 0)
                    group_done(b, 2)
                    load(2)
                maxima_in(B - 1, 1)
                maxima_in(B - 1, 2)

            @block.gpsimd
            def _(pool):
                nc.gpsimd.memset(KS[SPLIT:KROWS, :, :], 1.0).then_inc(const_set, 1)
                pool.wait_ge(const_set, 1)
                nc.gpsimd.memset(V[:, :, :, HD:HD + 1], 1.0).then_inc(const_set, 1)
                nc.gpsimd.memset(V[:, :, :, HD + 1:32], 0.0).then_inc(const_set, 1)
                pool.wait_ge(const_set, 3)
                nc.gpsimd.memset(oT[HALF:HALF + 1, :, :, :], 1.0).then_inc(const_set, 1)

                def low_parts(nb):
                    for t in range(3):
                        pool.wait_ge(m_part, nb * 3 + (t + 1))
                        nc.gpsimd.tensor_tensor(parts[:, t, 2, :], R[:, t, :], parts[:, t, 1, :], ALU.subtract).then_inc(l_set, 1)

                def place_values(nb, before):
                    pool.wait_ge(v_set, nb * TB + TB)
                    for g in range(NG):
                        hs = slice(g * GH, (g + 1) * GH)
                        ones = V[:, :, hs, HD:HD + 1].broadcast_to((P, TB, GH, HD))
                        if before is not None:
                            pool.wait_ge(pv_done, before * M_ALL + ((g + 1) * MICRO + 3))
                        nc.gpsimd.tensor_tensor(V[:, :, hs, 0:HD], VN[:, :, g * GH * HD:(g + 1) * GH * HD].rearrange("p i (h c) -> p i h c", h=GH),
                                                ones, ALU.mult).then_inc(v_full, 1)

                pool.wait_ge(const_set, 4)
                low_parts(0)
                place_values(0, None)
                with pool.Fori(0, B - 1) as b:
                    low_parts(b + 1)
                    place_values(b + 1, b)
                rsqrt_on_pool(nc, pool, core, var_set, pool_step, rstd_set)
                pool.wait_ge(rstd_set, 1)

            @block.tensor
            def _(pe):
                def prep_job(nb, j):
                    if j <= TB + 1:
                        pe.wait_ge(prep_free, nb * (TB + 1) + (j + 1))
                    if j == 0:
                        pe.wait_ge(r_set, nb * 6 + 1)
                    if j > TB + 1:
                        pe.wait_ge(r_set, nb * 6 + (j - TB))
                    if j < TB:
                        pe.wait_ge(xn_set, nb * TB + (j + 1))
                        for c in range(2):
                            mm = nc.tensor.transpose(ps[0:HALF, 7, c * P:(c + 1) * P], xn[:, j % 2, c * HALF:(c + 1) * HALF], core.ident[:, :])
                    if 0 < j <= TB:
                        for c in range(2):
                            mm = nc.tensor.matmul(ps[:, 7, 2 * P:2 * P + D], hT[:, c, (j - 1) * P:j * P], qkv_w[:, c, 2 * D:3 * D],
                                                  start=(c == 0), stop=(c == 1))
                    if j > TB:
                        t, half = (j - TB - 1) // 2, (j - TB - 1) % 2
                        for c in range(2):
                            mm = nc.tensor.matmul(ps[:, 7, 0:QH], qkv_w[:, c, t * P:(t + 1) * P], hT[:, c, half * QH:(half + 1) * QH],
                                                  start=(c == 0), stop=(c == 1))
                    mm.then_inc(prep_ready, 1)

                def scores(b, t, q):
                    g, k = t // MICRO, t % MICRO * GH + q
                    h, i, half = k // (2 * TB), k // 2 % TB, k % 2
                    if k == 0:
                        pe.wait_ge(qk_in[g], b * 192 + 192)
                    done = g * MAXIMA + (k + 1 if k >= SB else k)
                    if done > 0 or not (isinstance(b, int) and b == 0):
                        pe.wait_ge(mx_set, b * (NG * MAXIMA) + done)
                    nc.tensor.matmul(ps[:, k % SB, 0:QH], QS[0:SPLIT, g * GH + h, i * P:(i + 1) * P],
                                     KS[0:SPLIT, g * GH + h, half * QH:(half + 1) * QH], start=True, stop=True).then_inc(s_ready, 1)

                def exp_scores(b, M, h):
                    g, half, j = M // MICRO, M % MICRO // TB, M % TB
                    c = M * GH + h
                    if M % MICRO == 0 and h == 0:
                        pe.wait_ge(aug_in, b * 144 + (g + 1) * 48)
                    pe.wait_ge(exp_set, b * (M_ALL * GH) + (c + 1))
                    nc.tensor.matmul(ps[:, SB + c % XB, 0:QH], KS[:, g * GH + h, j * P:(j + 1) * P],
                                     QS[:, g * GH + h, half * QH:(half + 1) * QH], start=True, stop=True).then_inc(st_ready, 1)

                def weigh_values(b, M):
                    g, half, j = M // MICRO, M % MICRO // TB, M % TB
                    if M % MICRO == 0:
                        pe.wait_ge(v_full, b * NG + (g + 1))
                    pe.wait_ge(exp_set, b * (M_ALL * GH) + ((M + 1) * GH + XB))
                    if j == 0:
                        pe.wait_ge(ov_set, b * (2 * NG) + (2 * g + half + 1))
                    for h in range(GH):
                        mm = nc.tensor.matmul(ps[32 * h:32 * h + 32, 5, 0:QH], V[:, j, g * GH + h, :], PT[M % 3][:, h, :],
                                              start=(j == 0), stop=(j == TB - 1))
                    mm.then_inc(pv_done, 1)

                def bank6_job(b, what):
                    pe.wait_ge(b6_free, b6(b, what) + 1)
                    if what[0] == "m":
                        g = int(what[1])
                        mb = b + 1 if g == 0 else b
                        pe.wait_ge(mx_set, mb * (NG * MAXIMA) + ((g + 1) * MAXIMA + SB))
                        mm = nc.tensor.transpose(ps[0:GH * TB, 6, 0:P], mxq[:, g, :], core.ident[:, :])
                    elif what[0] == "o":
                        g, half = int(what[1]), int(what[2])
                        ob = b - 1 if what == "o21" else b
                        pe.wait_ge(ov_set, ob * (2 * NG) + (2 * g + half + 2))
                        for i in range(HB):
                            mm = nc.tensor.transpose(ps[:, 6, i * P:(i + 1) * P], ov[:, i * P:(i + 1) * P], core.ident[:, :])
                    else:
                        j = int(what[4])
                        if j < TB:
                            for c in range(2):
                                mm = nc.tensor.transpose(ps[0:HALF, 6, c * P:(c + 1) * P], O[:, j, c * HALF:(c + 1) * HALF], core.ident[:, :])
                        if j > 0:
                            k = j - 1
                            nc.tensor.matmul(ps[:, 6, 2 * P:2 * P + D], oT[0:HALF, k % 2, 0, :], proj_w[0:HALF, 0, :], start=True, stop=False)
                            mm = nc.tensor.matmul(ps[:, 6, 2 * P:2 * P + D], oT[:, k % 2, 1, :], proj_w[:, 1, :], start=False, stop=True)
                    mm.then_inc(b6_ready, 1)

                def batch(b, first, last):
                    for M in range(M_ALL):
                        mb, t = ahead(b, M)
                        more = not last or M + AHEAD < M_ALL
                        for q in range(GH):
                            exp_scores(b, M, q)
                            if more:
                                scores(mb, t, q)
                            if q == 1 and M > 0:
                                weigh_values(b, M - 1)
                            if q == 1 and M == 0 and not first:
                                weigh_values(b - 1, M_ALL - 1)
                        if M in B6 and not (first and M < 2 + TB + 1) and not (last and B6[M] == "m0"):
                            bank6_job(b, B6[M])
                        if not last and 0 <= M - PREP_AT < JOBS:
                            prep_job(b + 1, M - PREP_AT)

                pe.wait_ge(w_in, 64)
                pe.sem_inc(pv_done, 3)
                for j in range(JOBS):
                    prep_job(0, j)
                pe.wait_ge(const_set, 4)
                for t in range(AHEAD):
                    for q in range(GH):
                        scores(0, t, q)
                    if t == MICRO:
                        bank6_job(-1, "m0")
                batch(0, True, False)
                with pe.Fori(1, B - 1) as b:
                    batch(b, False, False)
                batch(B - 1, False, True)
                weigh_values(B - 1, M_ALL - 1)
                for what in ORDER[:LATE]:
                    bank6_job(B, what)

            @block.scalar
            def _(act):
                def read_prep(nb, j):
                    act.wait_ge(prep_ready, nb * JOBS + (j + 1))
                    if 0 < j <= TB:
                        if j == 1 and not (isinstance(nb, int) and nb == 0):
                            act.wait_ge(v_full, nb * NG)
                        op = nc.scalar.activation(VN[:, j - 1, :], ps[:, 7, 2 * P:2 * P + D], ACT.Copy)
                        op.then_inc(v_set, 1)
                    if j < TB:
                        for c in range(2):
                            op = nc.scalar.activation(hT[:, c, j * P:(j + 1) * P], ps[0:HALF, 7, c * P:(c + 1) * P],
                                                      ACT.Identity, scale=aff[:, c, 0:1], bias=aff[:, c, 1:2])
                    if j < TB:
                        op.then_inc(prep_free, 1)
                    elif j == TB:
                        act.wait_ge(v_set, nb * TB + TB)
                        act.sem_inc(prep_free, 1)
                    else:
                        t, half = (j - TB - 1) // 2, (j - TB - 1) % 2
                        if j == TB + 1 and not (isinstance(nb, int) and nb == 0):
                            act.wait_ge(qk_out, nb * 48)
                        nc.scalar.activation(parts[:, t, 0, half * QH:(half + 1) * QH], ps[:, 7, 0:QH], ACT.Copy).then_inc(h_part, 1)

                def middle_part(nb, t):
                    act.wait_ge(r_set, nb * 6 + (2 * t + 3))
                    nc.scalar.activation(parts[:, t, 1, :], R[:, t, :], ACT.Copy).then_inc(m_part, 1)

                def keep_sums(b, g, half):
                    act.wait_ge(pv_done, b * M_ALL + ((2 * g + half + 1) * TB + 3))
                    nc.scalar.activation(ov[:, :], ps[:, 5, 0:QH], ACT.Copy).then_inc(ov_set, 1)

                def batch(b, first, last):
                    for M in range(M_ALL):
                        act.wait_ge(pv_done, b * M_ALL + (M + 1))
                        for h in range(GH):
                            c = M * GH + h
                            act.wait_ge(st_ready, b * (M_ALL * GH) + (c + 1))
                            nc.scalar.activation(PT[M % 3][:, h, :], ps[:, SB + c % XB, 0:QH], ACT.Exp, scale=HD ** -0.5).then_inc(exp_set, 1)
                        if M == 0 and not first:
                            keep_sums(b - 1, NG - 1, 1)
                        if M > 0 and M % TB == 0:
                            keep_sums(b, (M - 1) // MICRO, (M - 1) % MICRO // TB)
                        if not last and 0 <= M - PREP_AT < JOBS:
                            read_prep(b + 1, M - PREP_AT)
                        if not last and M in MIDDLE:
                            middle_part(b + 1, MIDDLE[M])

                act.sem_inc(exp_set, XB)
                act.sem_inc(prep_free, 1)
                act.sem_inc(ov_set, 1)
                act.wait_ge(w_in, 64)
                for j in range(JOBS):
                    read_prep(0, j)
                for t in range(3):
                    middle_part(0, t)
                batch(0, True, False)
                with act.Fori(1, B - 1) as b:
                    batch(b, False, False)
                batch(B - 1, False, True)
                keep_sums(B - 1, NG - 1, 1)

            @block.vector
            def _(dve):
                def norm(nb, i):
                    n = nb * TB + i
                    if i >= 2:
                        dve.wait_ge(prep_ready, nb * JOBS + (i - 1))
                    nc.vector.tensor_scalar(xn[:, i % 2, :], X[:, col(n, D)], core.mean[:, bass.ds(n, 1)],
                                            core.rstd[:, bass.ds(n, 1)], ALU.subtract, ALU.mult).then_inc(xn_set, 1)

                def rest(nb, j):
                    k = j - TB - 1
                    t, half = k // 2, slice(k % 2 * QH, (k % 2 + 1) * QH)
                    dve.wait_ge(h_part, nb * 6 + (k + 1))
                    if k == 0 and not (isinstance(nb, int) and nb == 0):
                        dve.wait_ge(l_set, nb * 3)
                    nc.vector.tensor_tensor(R[:, t, half], ps[:, 7, 0:QH], parts[:, t, 0, half], ALU.subtract).then_inc(r_set, 1)

                def maximum(b, t, q):
                    g, k = t // MICRO, t % MICRO * GH + q
                    dve.wait_ge(s_ready, b * (NG * UNITS) + (g * UNITS + k + 1))
                    nc.vector.tensor_reduce(mx[:, g, k // 2, k % 2:k % 2 + 1], ps[:, k % SB, 0:QH], AX.X, ALU.max).then_inc(mx_set, 1)

                def maxima(b, t, half):
                    for q in range(half * 2, half * 2 + 2):
                        maximum(b, t, q)
                    if half == 1 and t % MICRO == MICRO - 1:
                        g = t // MICRO
                        dve.wait_ge(mx_set, b * (NG * MAXIMA) + (g * MAXIMA + UNITS + SB))
                        nc.vector.tensor_reduce(mxq[:, g, :], mx[:, g, :, :], AX.X, ALU.max).then_inc(mx_set, 1)

                def read_bank6(b, what):
                    dve.wait_ge(b6_ready, b6(b, what) + 1)
                    if what[0] == "m":
                        g = int(what[1])
                        at = ((b + 1 if g == 0 else b) * NG + g) * 4
                        p = nm_parts[:, g, :, :]
                        nc.vector.tensor_scalar(nm[:, 0, :], ps[0:GH * TB, 6, 0:P], -1.0, None, ALU.mult).then_inc(b6_free, 1)
                        dve.wait_ge(b6_free, b6(b, what) + 2)
                        nc.vector.tensor_copy(p[:, 0, :], nm[:, 0, :]).then_inc(nm_step, 1)
                        dve.wait_ge(nm_step, at + 1)
                        nc.vector.tensor_tensor(nm[:, 1, :], nm[:, 0, :], p[:, 0, :], ALU.subtract).then_inc(nm_step, 1)
                        dve.wait_ge(nm_step, at + 2)
                        nc.vector.tensor_copy(p[:, 1, :], nm[:, 1, :]).then_inc(nm_step, 1)
                        dve.wait_ge(nm_step, at + 3)
                        nc.vector.tensor_tensor(p[:, 2, :], nm[:, 1, :], p[:, 1, :], ALU.subtract).then_inc(nm_step, 1)
                        dve.wait_ge(nm_step, at + 4)
                        dve.sem_inc(nm_set, 1)
                    elif what[0] == "o":
                        g, half = int(what[1]), int(what[2])
                        ob = b - 1 if what == "o21" else b
                        src = ps[:, 6, 0:QH].rearrange("p (i h c) -> p i h c", i=HB, h=GH)
                        nc.vector.reciprocal(rc[:, :, :], src[:, :, :, HD]).then_inc(rc_set, 1)
                        dve.wait_ge(rc_set, ob * (2 * NG) + (2 * g + half + 1))
                        dst = O[:, half * HB:(half + 1) * HB, g * GH * HD:(g + 1) * GH * HD].rearrange("p i (h c) -> p i h c", h=GH)
                        scale = rc[:, :, :].rearrange("p i (h a) -> p i h a", a=1).broadcast_to((P, HB, GH, HD))
                        nc.vector.tensor_tensor(dst, src[:, :, :, 0:HD], scale, ALU.mult).then_inc(b6_free, 1)
                    else:
                        j = int(what[4])
                        if j < TB:
                            op = nc.vector.tensor_copy(oT[0:HALF, j % 2, :, :], ps[0:HALF, 6, 0:2 * P].rearrange("p (c t) -> p c t", c=2))
                        if j > 0:
                            n = b * TB + (j - 1 - TB)
                            op = nc.vector.tensor_tensor(X[:, col(n, D)], ps[:, 6, 2 * P:2 * P + D], X[:, col(n, D)], ALU.add)
                        op.then_inc(b6_free, 1)

                def stat(b, i):
                    n = b * TB + (i - TB)
                    dve.wait_ge(b6_free, b6(b, f"tail{TB}") + 2)
                    nc.vector.bn_stats(core.stats[:, col(n, 6)], X[:, col(n, D)]).then_inc(st_set, 1)

                def batch(b, first, last):
                    for M in range(M_ALL):
                        mb, t = ahead(b, M)
                        more = not last or M + AHEAD < M_ALL
                        if more:
                            maxima(mb, t, 0)
                        if not last and 0 <= M - PREP_AT + 1 < TB:
                            norm(b + 1, M - PREP_AT + 1)
                        if more:
                            maxima(mb, t, 1)
                        if M in B6 and not (first and M < 2 + TB + 1) and not (last and B6[M] == "m0"):
                            read_bank6(b, B6[M])
                        if not first and 11 <= M < 11 + TB:
                            stat(b, M - 11)
                        if not last and TB < M - PREP_AT < JOBS:
                            rest(b + 1, M - PREP_AT)

                dve.sem_inc(mx_set, SB)
                dve.sem_inc(b6_free, 1)
                dve.sem_inc(r_set, 1)
                dve.wait_ge(w_in, 64)
                for i in range(TB):
                    norm(0, i)
                for j in range(TB + 1, JOBS):
                    rest(0, j)
                for t in range(AHEAD):
                    maxima(0, t, 0)
                    maxima(0, t, 1)
                    if t == MICRO:
                        read_bank6(-1, "m0")
                batch(0, True, False)
                with dve.Fori(1, B - 1) as b:
                    batch(b, False, False)
                batch(B - 1, False, True)
                for what in ORDER[:LATE]:
                    read_bank6(B, what)
                for i in range(TB):
                    stat(B, i)
                mean_and_var(nc, dve, core, st_set, dve_step, var_set)


def route_phase(core):
    nc, a, ps = core.nc, core.a, core.ps
    X = core.XA
    with ExitStack() as ctx:
        def sb(name, shape, dt=F32):
            return ctx.enter_context(nc.sbuf_tensor(name, shape, dt))

        def sem(name):
            return ctx.enter_context(nc.semaphore(name))

        gate_w = sb("gate_w", [HALF + 1, 2, E])
        aff = sb("affine2", [HALF, 2, 4])
        xn = sb("r_xn", [P, 2, D])
        hT = sb("r_hT", [HALF + 1, 2, 2, P])
        steps = sb("steps", [P, NSLOT])
        ids = sb("ids", [P, NT, TOPK])
        before, ones = sb("before", [P, P]), sb("ones", [P, P])
        logit, at_max, either = sb("logit", [P, NT, E]), sb("at_max", [P, NT, E]), sb("either", [P, NT, E])
        pick = [sb(f"pick{k}", [P, NT, E]) for k in range(TOPK)]
        top = sb("top", [P, TOPK, NT])
        first = sb("first", [P, NT])
        ex, den = sb("exp_dif", [P, NT]), sb("denom", [P, NT])
        run = sb("running", [P, 2, NT, E])
        place, chosen = sb("place", [P, NT, E]), sb("chosen", [P, NT, E])
        slot_f = sb("slot_f", [P, NT, TOPK])
        full = sb("full", [P, E, NT])
        tiles, ends = sb("tiles", [P, E]), sb("ends", [P, 4, E])
        past = sb("past", [P, NSLOT, E - 1])
        past_n = sb("past_n", [P, NSLOT])
        send = sb("send", [P, 4, TOPK, D + 1])
        send_at = sb("send_at", [P, 4, TOPK], U32)
        const_in, w_in, b2_in, const_set = sem("r_const_in"), sem("r_w_in"), sem("r_b2_in"), sem("r_const_set")
        xn_set, t_ready, hT_set, g_ready = sem("r_xn_set"), sem("r_t_ready"), sem("r_hT_set"), sem("r_g_ready")
        pick_set, count_ready, step, dif_set, exp_set = sem("r_pick_set"), sem("r_count_ready"), sem("r_step"), sem("r_dif_set"), sem("r_exp_set")
        send_set, sending, hx_set = sem("r_send_set"), sem("r_sending"), sem("r_hx_set")
        sent = [sem(f"r_sent{u}") for u in range(4)]
        NP = NT // 2
        with nc.Block() as block:
            @block.sync
            def _(sp):
                sp.dma_start(gate_w[0:HALF, :, :], a["gate_w"].rearrange("(c k) n -> k c n", c=2)).then_inc(const_in, 16)
                sp.dma_start(gate_w[HALF:HALF + 1, 1, :], a["gate_b"].rearrange("(a c) -> a c", a=1)).then_inc(const_in, 16)
                sp.dma_start(aff[:, :, :], a["affine"].rearrange("(c k) t -> k c t", c=2)).then_inc(const_in, 16)
                sp.dma_start(steps[:, :], a["steps"]).then_inc(const_in, 16)
                sp.dma_start(ids[:, :, :], a["ids"]).then_inc(const_in, 16)
                sp.dma_start(before[:, :], a["before"]).then_inc(const_in, 16)
                for e in range(E):
                    sp.dma_start(core.W1[0:HALF, e, :, :], a["w1"][e].rearrange("(c k) n -> k c n", c=2)).then_inc(w_in, 16)
                    sp.dma_start(core.W2[:, e, :, :], a["w2"][e].rearrange("(j k) n -> k j n", k=P)).then_inc(w_in, 16)
                sp.dma_start(core.W1[HALF:HALF + 1, :, 1, :], a["b1"].rearrange("(a e) n -> a e n", a=1)).then_inc(w_in, 16)
                sp.wait_ge(w_in, 16 * (2 * E + 1))

            @block.gpsimd
            def _(pool):
                nc.gpsimd.memset(hT[HALF:HALF + 1, :, :, :], 1.0).then_inc(const_set, 1)
                pool.wait_ge(const_set, 1)
                nc.gpsimd.memset(ones[:, :], 1.0).then_inc(const_set, 1)
                for b in range(B):
                    cols = slice(b * TB * D, (b + 1) * TB * D)
                    nc.gpsimd.tensor_tensor(core.H[:, cols], core.H[:, cols], X[:, cols], ALU.add).then_inc(hx_set, 1)
                pool.wait_ge(hx_set, B)
                with pool.Fori(0, NT // 4) as i:
                    for u in range(4):
                        pool.wait_ge(send_set, i * 4 + (u + 1))
                        pool.sem_inc(sending, 1)
                        for k in range(TOPK):
                            pool.indirect_dma_start(core.slot_x, bass.IndirectOffsetOnAxis(ap=send_at[:, u, k:k + 1], axis=0),
                                                    send[:, u, k, :], None).then_inc(sent[u], 16)
                for u in range(4):
                    pool.wait_ge(sent[u], TOPK * 16 * (NT // 4))

            @block.tensor
            def _(pe):
                def transpose(n, u):
                    pe.wait_ge(xn_set, n + 1)
                    pe.wait_ge(hT_set, n + 1)
                    for c in range(2):
                        mm = nc.tensor.transpose(ps[0:HALF, u, c * P:(c + 1) * P], xn[:, u, c * HALF:(c + 1) * HALF], core.ident[:, :])
                    mm.then_inc(t_ready, 1)

                def gate(n, u):
                    pe.wait_ge(hT_set, n + 3)
                    nc.tensor.matmul(ps[:, 2, col(n, E)], hT[0:HALF, u, 0, :], gate_w[0:HALF, 0, :], start=True, stop=False)
                    nc.tensor.matmul(ps[:, 2, col(n, E)], hT[:, u, 1, :], gate_w[:, 1, :], start=False, stop=True).then_inc(g_ready, 1)

                pe.wait_ge(const_in, 96)
                pe.wait_ge(const_set, 2)
                pe.sem_inc(g_ready, 2)
                transpose(0, 0)
                with pe.Fori(0, NP - 1) as i:
                    for u in range(2):
                        transpose(i * 2 + (u + 1), 1 - u)
                        gate(i * 2 + u, u)
                transpose(NT - 1, 1)
                for u in range(2):
                    gate(NT - 2 + u, u)
                pe.wait_ge(pick_set, 1)
                flat = either[:, :, :].rearrange("p n e -> p (n e)")
                nc.tensor.matmul(ps[:, 3, 0:NT * E], before[:, :], flat, start=True, stop=True).then_inc(count_ready, 1)
                nc.tensor.matmul(ps[:, 4, 0:NT * E], ones[:, :], flat, start=True, stop=True).then_inc(count_ready, 1)

            @block.scalar
            def _(act):
                act.dma_start(core.b2[:, :, :], a["b2"].rearrange("(a e) n -> a e n", a=1).broadcast_to((P, E, D))).then_inc(b2_in, 16)

                def affine(n, u):
                    act.wait_ge(t_ready, n + 1)
                    act.wait_ge(g_ready, n + 1)
                    for c in range(2):
                        op = nc.scalar.activation(hT[0:HALF, u, c, :], ps[0:HALF, u, c * P:(c + 1) * P], ACT.Identity,
                                                  scale=aff[:, c, 2:3], bias=aff[:, c, 3:4])
                    op.then_inc(hT_set, 1)

                act.sem_inc(hT_set, 2)
                act.wait_ge(const_in, 96)
                with act.Fori(0, NP) as i:
                    for u in range(2):
                        affine(i * 2 + u, u)
                act.wait_ge(dif_set, 1)
                nc.scalar.activation(ex[:, :], ex[:, :], ACT.Exp).then_inc(exp_set, 1)
                act.wait_ge(exp_set, 1)
                act.wait_ge(b2_in, 16)

            @block.vector
            def _(dve):
                def norm(n, u):
                    nc.vector.tensor_scalar(xn[:, u, :], X[:, col(n, D)], core.mean[:, bass.ds(n, 1)],
                                            core.rstd[:, bass.ds(n, 1)], ALU.subtract, ALU.mult).then_inc(xn_set, 1)

                dve.wait_ge(const_in, 96)
                for u in range(2):
                    norm(u, u)
                with dve.Fori(1, NP) as i:
                    for u in range(2):
                        dve.wait_ge(t_ready, i * 2 + (u - 1))
                        norm(i * 2 + u, u)

                done = 0

                def then(op):
                    nonlocal done
                    done += 1
                    op.then_inc(step, 1)
                    dve.wait_ge(step, done)

                def per_expert(ap):
                    return ap.rearrange("p (n a) -> p n a", a=1).broadcast_to((P, NT, E))

                expert = steps[:, 0:E].rearrange("p (a e) -> p a e", a=1).broadcast_to((P, NT, E))
                dve.wait_ge(g_ready, NT + 2)
                then(nc.vector.tensor_copy(logit[:, :, :], ps[:, 2, 0:NT * E].rearrange("p (n e) -> p n e", e=E)))
                for k in range(TOPK):
                    then(nc.vector.tensor_reduce(top[:, k, :], logit[:, :, :], AX.X, ALU.max))
                    then(nc.vector.tensor_tensor(at_max[:, :, :], logit[:, :, :], per_expert(top[:, k, :]), ALU.is_ge))
                    then(nc.vector.scalar_tensor_tensor(at_max[:, :, :], expert, float(E), at_max[:, :, :], ALU.subtract, ALU.mult))
                    then(nc.vector.tensor_reduce(first[:, :], at_max[:, :, :], AX.X, ALU.min))
                    then(nc.vector.scalar_tensor_tensor(pick[k][:, :, :], expert, float(E), per_expert(first[:, :]), ALU.subtract, ALU.is_equal))
                    if k == 0:
                        then(nc.vector.scalar_tensor_tensor(logit[:, :, :], pick[0][:, :, :], -3.0e38, logit[:, :, :], ALU.mult, ALU.add))
                then(nc.vector.tensor_tensor(either[:, :, :], pick[0][:, :, :], pick[1][:, :, :], ALU.add))
                dve.sem_inc(pick_set, 1)
                then(nc.vector.tensor_tensor(ex[:, :], top[:, 1, :], top[:, 0, :], ALU.subtract))
                dve.sem_inc(dif_set, 1)
                dve.wait_ge(exp_set, 1)
                then(nc.vector.tensor_scalar(den[:, :], ex[:, :], 1.0, None, ALU.add))
                then(nc.vector.reciprocal(core.weight[:, 0, :], den[:, :]))
                then(nc.vector.tensor_tensor(core.weight[:, 1, :], core.weight[:, 0, :], ex[:, :], ALU.mult))
                dve.wait_ge(count_ready, 2)
                total = ps[:, 4, 0:NT * E].rearrange("p (n e) -> p n e", e=E)
                then(nc.vector.tensor_copy(run[:, 0, :, :], total))
                reach, r = 1, 0
                while reach < NT:
                    then(nc.vector.tensor_copy(run[:, 1 - r, 0:reach, :], run[:, r, 0:reach, :]))
                    then(nc.vector.tensor_tensor(run[:, 1 - r, reach:NT, :], run[:, r, reach:NT, :], run[:, r, 0:NT - reach, :], ALU.add))
                    reach, r = 2 * reach, 1 - r
                count = run[:, r, NT - 1, :].rearrange("p (e a) -> p e a", a=1).broadcast_to((P, E, NT))
                mult = steps[:, 0:NT].rearrange("p (a n) -> p a n", a=1).broadcast_to((P, E, NT))
                then(nc.vector.scalar_tensor_tensor(full[:, :, :], mult, float(P), count, ALU.mult, ALU.is_lt))
                then(nc.vector.tensor_reduce(tiles[:, :], full[:, :, :], AX.X, ALU.add))
                then(nc.vector.tensor_copy(ends[:, 0, :], tiles[:, :]))
                reach, s = 1, 0
                while reach < E:
                    then(nc.vector.tensor_copy(ends[:, s + 1, 0:reach], ends[:, s, 0:reach]))
                    then(nc.vector.tensor_tensor(ends[:, s + 1, reach:E], ends[:, s, reach:E], ends[:, s, 0:E - reach], ALU.add))
                    reach, s = 2 * reach, s + 1
                then(nc.vector.tensor_tensor(tiles[:, :], ends[:, s, :], tiles[:, :], ALU.subtract))
                tile_no = steps[:, :].rearrange("p (s a) -> p s a", a=1).broadcast_to((P, NSLOT, E - 1))
                end = ends[:, s, 0:E - 1].rearrange("p (a e) -> p a e", a=1).broadcast_to((P, NSLOT, E - 1))
                then(nc.vector.tensor_tensor(past[:, :, :], tile_no, end, ALU.is_ge))
                then(nc.vector.tensor_reduce(past_n[:, :], past[:, :, :], AX.X, ALU.add))
                then(nc.vector.tensor_copy(core.tile_expert[:, :], past_n[:, :]))
                then(nc.vector.tensor_tensor(place[:, :, :], run[:, r, :, :], total, ALU.subtract))
                then(nc.vector.tensor_tensor(place[:, :, :], ps[:, 3, 0:NT * E].rearrange("p (n e) -> p n e", e=E), place[:, :, :], ALU.add))
                begin = tiles[:, :].rearrange("p (a e) -> p a e", a=1).broadcast_to((P, NT, E))
                then(nc.vector.scalar_tensor_tensor(place[:, :, :], begin, float(P), place[:, :, :], ALU.mult, ALU.add))
                for k in range(TOPK):
                    then(nc.vector.tensor_tensor(chosen[:, :, :], pick[k][:, :, :], place[:, :, :], ALU.mult))
                    then(nc.vector.tensor_reduce(slot_f[:, :, k], chosen[:, :, :], AX.X, ALU.add))
                def rows_to_send(n, u):
                    for k in range(TOPK):
                        nc.vector.tensor_scalar(send[:, u, k, 0:D], X[:, col(n, D)], core.mean[:, bass.ds(n, 1)],
                                                core.rstd[:, bass.ds(n, 1)], ALU.subtract, ALU.mult)
                    nc.vector.tensor_copy(send[:, u, :, D], ids[:, bass.ds(n, 1), :].rearrange("p a k -> p (a k)"))
                    nc.vector.tensor_copy(send_at[:, u, :], slot_f[:, bass.ds(n, 1), :].rearrange("p a k -> p (a k)")).then_inc(send_set, 1)

                for u in range(4):
                    rows_to_send(u, u)
                with dve.Fori(1, NT // 4) as i:
                    for u in range(4):
                        dve.wait_ge(sent[u], i * (TOPK * 16))
                        rows_to_send(i * 4 + u, u)


def expert_phase(core):
    nc, a, ps = core.nc, core.a, core.ps
    with ExitStack() as ctx:
        def sb(name, shape, dt=F32):
            return ctx.enter_context(nc.sbuf_tensor(name, shape, dt))

        def sem(name):
            return ctx.enter_context(nc.semaphore(name))

        U = 8
        assert NSLOT % U == 0
        aff = sb("x_affine2", [HALF, 2, 4])
        xs = sb("slot_rows", [P, U, D + 1])
        hT = sb("x_hT", [HALF + 1, 2, 2, P])
        he = sb("hidden", [P, 2, HID])
        heT = sb("hiddenT", [P, 2, KH, P])
        ys = sb("slot_out", [P, 4, D])
        ys_at = sb("slot_out_at", [P, 4, 1], U32)
        aff_in, ones_set = sem("x_aff_in"), sem("x_ones_set")
        x_in = [sem(f"x_x_in{u}") for u in range(U)]
        xT_ready, hT_set, h_ready, he_set = sem("x_xT_ready"), sem("x_hT_set"), sem("x_h_ready"), sem("x_he_set")
        heT_ready, heT_set, y_ready, y_set = sem("x_heT_ready"), sem("x_heT_set"), sem("x_y_ready"), sem("x_y_set")
        sum_set, sending = sem("x_sum_set"), sem("x_sending")
        y_out = [sem(f"x_y_out{u}") for u in range(4)]

        def has(j, back):
            return j is None or 0 <= j - back < NSLOT

        def steps(engine, step):
            for u in range(U):
                step(u, u, 0)
            with engine.Fori(1, NSLOT // U) as i:
                for u in range(U):
                    step(None, u, i)
            for u in range(3):
                step(NSLOT + u, u, NSLOT // U)

        def tile(i, u, back):
            return i * U + (u - back)

        def expert_of(engine, s):
            return engine.value_load(core.tile_expert[0:1, bass.ds(s, 1)], min_val=0, max_val=E - 1)

        with nc.Block() as block:
            @block.sync
            def _(sp):
                sp.dma_start(aff[:, :, :], a["affine"].rearrange("(c k) t -> k c t", c=2)).then_inc(aff_in, 16)
                for u in range(U):
                    sp.dma_start(xs[:, u, :], core.slot_x[u * P:(u + 1) * P, :]).then_inc(x_in[u], 16)
                with sp.Fori(1, NSLOT // U) as i:
                    for u in range(U):
                        sp.wait_ge(y_set, tile(i, u, U) + 1)
                        sp.dma_start(xs[:, u, :], core.slot_x[bass.ds((i * U + u) * P, P), :]).then_inc(x_in[u], 16)

            @block.gpsimd
            def _(pool):
                nc.gpsimd.memset(hT[HALF:HALF + 1, :, :, :], 1.0).then_inc(ones_set, 1)
                with pool.Fori(0, NSLOT // 4) as i:
                    for u in range(4):
                        pool.wait_ge(y_set, i * 4 + (u + 1))
                        pool.sem_inc(sending, 1)
                        pool.indirect_dma_start(core.tok_y, bass.IndirectOffsetOnAxis(ap=ys_at[:, u, 0:1], axis=0),
                                                ys[:, u, :], None).then_inc(y_out[u], 16)
                for u in range(4):
                    pool.wait_ge(y_out[u], 16 * (NSLOT // 4))

            @block.tensor
            def _(pe):
                def step(j, u, i):
                    if has(j, 0):
                        s = tile(i, u, 0)
                        pe.wait_ge(x_in[u], (i + 1) * 16)
                        pe.wait_ge(hT_set, s)
                        for c in range(2):
                            mm = nc.tensor.transpose(ps[0:HALF, 0, c * P:(c + 1) * P], xs[:, u, c * HALF:(c + 1) * HALF], core.ident[:, :])
                        mm.then_inc(xT_ready, 1)
                    if has(j, 1):
                        s, v = tile(i, u, 1), (u - 1) % 2
                        e = expert_of(pe, s)
                        pe.wait_ge(hT_set, s + 1)
                        if has(j, 3):
                            pe.wait_ge(he_set, tile(i, u, 3) + 1)
                        for half in range(2):
                            for c in range(2):
                                rows = HALF + c
                                w = core.W1[0:rows, bass.ds(e, 1), c, half * QH:(half + 1) * QH].rearrange("p a n -> p (a n)")
                                mm = nc.tensor.matmul(ps[:, 1 + 2 * v + half, 0:QH], hT[0:rows, v, c, :], w, start=(c == 0), stop=(c == 1))
                        mm.then_inc(h_ready, 1)
                    if has(j, 2):
                        s, v = tile(i, u, 2), u % 2
                        pe.wait_ge(he_set, s + 1)
                        pe.wait_ge(heT_set, s)
                        for k in range(KH):
                            mm = nc.tensor.transpose(ps[:, 5 + k // 3, k % 3 * P:(k % 3 + 1) * P], he[:, v, k * P:(k + 1) * P], core.ident[:, :])
                        mm.then_inc(heT_ready, 1)
                    if has(j, 3):
                        s, v = tile(i, u, 3), (u - 3) % 2
                        e = expert_of(pe, s)
                        pe.wait_ge(heT_set, s + 1)
                        pe.wait_ge(sum_set, s)
                        for k in range(KH):
                            w = core.W2[:, bass.ds(e, 1), k, :].rearrange("p a n -> p (a n)")
                            mm = nc.tensor.matmul(ps[:, 7, 0:D], heT[:, v, k, :], w, start=(k == 0), stop=(k == KH - 1))
                        mm.then_inc(y_ready, 1)

                pe.wait_ge(ones_set, 1)
                steps(pe, step)

            @block.scalar
            def _(act):
                def step(j, u, i):
                    if has(j, 1):
                        s, v = tile(i, u, 1), (u - 1) % 2
                        act.wait_ge(h_ready, s + 1)
                        if has(j, 3):
                            act.wait_ge(heT_ready, tile(i, u, 3) + 1)
                        src = ps[:, 1 + 2 * v:3 + 2 * v, 0:QH]
                        nc.scalar.activation(he[:, v, :].rearrange("p (a n) -> p a n", a=2), src, ACT.Gelu).then_inc(he_set, 1)

                steps(act, step)

            @block.vector
            def _(dve):
                def step(j, u, i):
                    if has(j, 0):
                        s, v = tile(i, u, 0), u % 2
                        dve.wait_ge(xT_ready, s + 1)
                        if has(j, 2):
                            dve.wait_ge(h_ready, tile(i, u, 2) + 1)
                        for c in range(2):
                            op = nc.vector.tensor_scalar(hT[0:HALF, v, c, :], ps[0:HALF, 0, c * P:(c + 1) * P],
                                                         aff[:, c, 2:3], aff[:, c, 3:4], ALU.mult, ALU.add)
                        op.then_inc(hT_set, 1)
                    if has(j, 2):
                        s, v = tile(i, u, 2), u % 2
                        dve.wait_ge(heT_ready, s + 1)
                        if has(j, 4):
                            dve.wait_ge(y_ready, tile(i, u, 4) + 1)
                        nc.vector.tensor_copy(heT[:, v, :, :].rearrange("p (a k) t -> p a (k t)", a=2), ps[:, 5:7, 0:QH]).then_inc(heT_set, 1)
                    if has(j, 3):
                        s, v = tile(i, u, 3), (u - 3) % 4
                        e = expert_of(dve, s)
                        dve.wait_ge(y_ready, s + 1)
                        if has(j, 7):
                            dve.wait_ge(y_out[v], (tile(i, u, 3) - v) * 4)
                        bias = core.b2[:, bass.ds(e, 1), :].rearrange("p a n -> p (a n)")
                        nc.vector.tensor_tensor(ys[:, v, :], ps[:, 7, 0:D], bias, ALU.add).then_inc(sum_set, 1)
                        nc.vector.tensor_copy(ys_at[:, v, :], xs[:, (u - 3) % U, D:D + 1]).then_inc(y_set, 1)

                dve.wait_ge(aff_in, 16)
                steps(dve, step)


def combine_phase(core):
    nc, H = core.nc, core.H
    with ExitStack() as ctx:
        def sb(name, shape, dt=F32):
            return ctx.enter_context(nc.sbuf_tensor(name, shape, dt))

        def sem(name):
            return ctx.enter_context(nc.semaphore(name))

        y = sb("expert_rows", [P, 2, TOPK, TB, D])
        y_in = [sem(f"f_y_in{u}") for u in range(2)]
        part_set, out_set, out_done = sem("f_part_set"), sem("f_out_set"), sem("f_out_done")
        rows = core.tok_y[0:TOPK * NT * P, :].rearrange("(k b i p) c -> b k p i c", k=TOPK, b=B, i=TB)
        with nc.Block() as block:
            @block.sync
            def _(sp):
                for b in range(B):
                    if b >= 2:
                        sp.wait_ge(out_set, (b - 1) * TB)
                    for k in range(TOPK):
                        sp.dma_start(y[:, b % 2, k, :, :], rows[b, k]).then_inc(y_in[b % 2], 16)

            @block.vector
            def _(dve):
                with dve.Fori(0, B // 2) as i:
                    for u in range(2):
                        for k in range(TOPK):
                            for t in range(TB):
                                n = i * (2 * TB) + (u * TB + t)
                                if k == 0:
                                    dve.wait_ge(y_in[u], (i + 1) * (16 * TOPK))
                                else:
                                    dve.wait_ge(part_set, n + 1)
                                nc.vector.scalar_tensor_tensor(H[:, col(n, D)], y[:, u, k, t, :], core.weight[:, k, bass.ds(n, 1)],
                                                               H[:, col(n, D)], ALU.mult, ALU.add).then_inc((part_set, out_set)[k], 1)

            @block.scalar
            def _(act):
                for b in range(B):
                    act.wait_ge(out_set, (b + 1) * TB)
                    act.dma_start(core.out[b].rearrange("(i p) c -> p i c", p=P),
                                  H[:, b * TB * D:(b + 1) * TB * D].rearrange("p (i c) -> p i c", i=TB)).then_inc(out_done, 16)
                act.wait_ge(out_done, 16 * B)



PHASES = (embed_phase, project_phase, conv_phase, mix_out_phase, attention_phase, route_phase, expert_phase,
          combine_phase)


def build_program(nc, a, out):
    with ExitStack() as ctx:
        core = Core(nc, a, out, ctx)
        for phase in PHASES:
            phase(core)


_OUT = ((B, S, D), "float32")


def lay_out(x, txt, L0_tok_W, L0_tok_b, L0_attn_w_in, L0_attn_b_in, L0_attn_w_filt, L0_attn_b_filt,
            L0_attn_w_short, L0_attn_b_short, L0_attn_w_out, L0_attn_b_out, L0_ffn_ln1_g, L0_ffn_ln1_b,
            L0_ffn_qkv_w, L0_ffn_proj_w, L0_ffn_proj_b, L0_ffn_ln2_g, L0_ffn_ln2_b, L0_ffn_gate_w,
            L0_ffn_gate_b, L0_ffn_w1, L0_ffn_b1, L0_ffn_w2, L0_ffn_b2):
    x, w = np.asarray(x), np.asarray(L0_tok_W)
    patches = x.reshape(B, C, GRID, PATCH, GRID, PATCH).transpose(1, 3, 5, 0, 2, 4).reshape(KP, P, B * NPATCH)
    wtok = w.reshape(D, KP, P).transpose(2, 1, 0)
    ins = {
        "patches": patches.transpose(1, 0, 2).reshape(P, KP * B * NPATCH),
        "wtok": wtok.reshape(P, KP * D),
        "txt": txt, "tok_b": L0_tok_b, "w_in": L0_attn_w_in, "b_in": L0_attn_b_in, "w_filt": L0_attn_w_filt,
        "b_filt": L0_attn_b_filt, "short": np.concatenate([np.asarray(L0_attn_w_short)[:, 0, :], np.asarray(L0_attn_b_short)[:, None]], 1), "w_out": L0_attn_w_out,
        "b_out": L0_attn_b_out, "affine": np.stack([L0_ffn_ln1_g, L0_ffn_ln1_b, L0_ffn_ln2_g, L0_ffn_ln2_b], 1), "qkv_w": L0_ffn_qkv_w,
        "proj_w": L0_ffn_proj_w, "proj_b": L0_ffn_proj_b,
        "gate_w": L0_ffn_gate_w, "gate_b": L0_ffn_gate_b, "w1": L0_ffn_w1, "b1": L0_ffn_b1, "w2": L0_ffn_w2,
        "b2": L0_ffn_b2,
    } | shape_tables()
    return {k: np.ascontiguousarray(v) for k, v in ins.items()}


def kernel(**inputs):
    import concourse.bacc as bacc
    from concourse.bass_utils import run_bass_kernel_spmd
    arrays = lay_out(**inputs)
    nc = bacc.Bacc("TRN2", target_bir_lowering=False, num_devices=1)
    a = {k: nc.dram_tensor("in_" + k, v.shape, mybir.dt.from_np(v.dtype), kind="ExternalInput").ap() for k, v in arrays.items()}
    out = nc.dram_tensor("out_0_dram", _OUT[0], F32, kind="ExternalOutput").ap()
    build_program(nc, a, out)
    if not nc.is_finalized():
        nc.finalize()
    r = run_bass_kernel_spmd(nc, [{"in_" + k: v for k, v in arrays.items()}], core_ids=[0])
    return np.asarray(r.results[0]["out_0_dram"])
```

```python
from contextlib import ExitStack

import numpy as np

import concourse.bass as bass
from concourse import mybir

F32 = mybir.dt.float32
BF16 = mybir.dt.bfloat16
U32 = mybir.dt.uint32
I32 = mybir.dt.int32
ALU = mybir.AluOpType
ACT = mybir.ActivationFunctionType
AX = mybir.AxisListType

P = 128
B, C, IMG, PATCH, D = 8, 3, 96, 16, 192
GRID = IMG // PATCH
NPATCH = GRID * GRID
N_IMG, N_TXT = 256, 512
S = N_IMG + N_TXT
TB = S // P
NT = B * TB
T_IMG = N_IMG // P
KPATCH = C * PATCH * PATCH
KP = KPATCH // P
HALF = D // 2
FREQ = 64
EPS = 1e-5
CH = 16
NCHUNK = D // CH
TG = 4
TROW = 384
HB = TB // 2
HEADS, HD = 12, 16
GH = 4
NG = HEADS // GH
QH = S // 2
SPLIT = 6 * HD
AUG = 3
KROWS = SPLIT + AUG
VW = HD + 1
E, TOPK, HID = 8, 2, 768
KH = HID // P
NSLOT = NT * TOPK + E
SPARE = 2 * E * P


def hilbert_points(p):
    n = 1 << p
    pts = np.zeros((n * n, 2), dtype=np.int32)
    for d in range(n * n):
        t, x, y, s = d, 0, 0, 1
        while s < n:
            rx = 1 & t // 2
            ry = 1 & (t ^ rx)
            if ry == 0:
                if rx == 1:
                    x, y = s - 1 - x, s - 1 - y
                x, y = y, x
            x, y = x + s * rx, y + s * ry
            t //= 4
            s *= 2
        pts[d] = x, y
    return pts


def shape_tables():
    f32 = np.float32
    f = np.arange(FREQ, dtype=np.float64)
    taps = np.r_[np.arange(S - P + 1, S), np.arange(P)].astype(np.float64)
    basis = np.ones((FREQ + 1, len(taps)))
    basis[:FREQ] = np.sin(f[:, None] * taps[None, :] / FREQ)
    s = np.arange(S, dtype=np.float64)
    phi = np.concatenate([np.sin(s[:, None] * f / FREQ), np.cos(s[:, None] * f / FREQ)], 1)
    u = s - S // 2
    psi = np.concatenate([np.cos(f[:, None] * u / FREQ), -np.sin(f[:, None] * u / FREQ)], 0)
    psi[FREQ] = 1.0
    pts = np.minimum(hilbert_points(4), GRID - 1)
    pick = np.zeros((2 * NPATCH, 2, T_IMG, P))
    for d in range(N_IMG):
        for r in range(2):
            pick[r * NPATCH + pts[d, 0] * GRID + pts[d, 1], r, d // P, d % P] = 1.0
    return {
        "basis": basis.astype(f32),
        "phi": phi.reshape(TB, P, 2 * FREQ).transpose(1, 0, 2).astype(f32).copy(),
        "psi": psi.reshape(2 * FREQ, TB, P).astype(f32).copy(),
        "pick": pick.astype(f32).reshape(2 * NPATCH, 2 * T_IMG * P),
        "ident": np.eye(P, dtype=f32),
        "steps": np.broadcast_to(np.arange(NSLOT, dtype=f32), (P, NSLOT)),
        "ids": (np.arange(P)[:, None, None] + P * np.arange(NT)[None, :, None] + NT * P * np.arange(TOPK)).astype(f32),
        "spare": (TOPK * NT * P + np.arange(SPARE)).reshape(2, E, P).transpose(2, 0, 1).astype(f32),
        "unread": ((E * NT + E) * P + np.arange(P)[:, None] + P * np.arange(E)).astype(f32),
        "before": np.triu(np.ones((P, P), f32), 1),
    }


def col(n, width):
    return bass.ds(n * width, width)


class Core:

    def __init__(self, nc, a, out, ctx):
        self.nc, self.a, self.out, self.ctx = nc, a, out, ctx

        def sb(name, shape, dt=F32):
            return ctx.enter_context(nc.sbuf_tensor(name, shape, dt))

        self.H = sb("h_resid", [P, NT * D])
        self.XA = sb("x_proj_then_x", [P, NT * D])
        self.GY = sb("gate_then_w2", [P, NT * D])
        self.XS = sb("short_then_w1", [P, NT * P * 2])
        self.ident = sb("ident", [P, P])
        self.stats = sb("ln_stats", [P, NT * 6])
        self.mean = sb("ln_mean", [P, NT])
        self.var = sb("ln_var", [P, NT])
        self.dif = sb("ln_dif", [P, NT])
        self.rstd = sb("rstd", [P, NT])
        self.powers = sb("minus_half", [P, NT])
        self.ps = ctx.enter_context(nc.psum_tensor("ps", [P, 8, 512], F32))
        self.filt_dram = nc.dram_tensor("filt_rows", (D, TROW), F32, kind="Internal").ap()
        self.slot_x = nc.dram_tensor("slot_x", ((E * NT + 2 * E) * P, D + 1), F32, kind="Internal").ap()
        self.tok_y = nc.dram_tensor("tok_y", (TOPK * NT * P + SPARE, D), F32, kind="Internal").ap()
        self.weight = sb("expert_weight", [P, TOPK, NT])
        self.b2 = sb("expert_b2", [P, E, D])
        self.tile_expert = sb("tile_expert", [P, NSLOT], I32)
        self.tile_at = sb("tile_at", [P, NSLOT], I32)
        self.W1 = self.XS[0:HALF + 1, :].rearrange("p (e c n) -> p e c n", e=E, c=2)
        self.W2 = self.GY[:, :].rearrange("p (e j n) -> p e j n", e=E, j=KH)


def rsqrt_on_pool(nc, pool, core, var_set, step, rstd_set, tiles, part):
    var, rstd, minus_half = tiles(core.var[:, :]), tiles(core.rstd[:, :]), tiles(core.powers[:, :])
    pool.wait_ge(var_set, part + 1)
    nc.gpsimd.tensor_scalar(rstd, var, EPS, None, ALU.add).then_inc(step, 1)
    pool.wait_ge(step, part + 1)
    nc.gpsimd.tensor_tensor(rstd, rstd, minus_half, ALU.pow).then_inc(rstd_set, 1)


def mean_and_var(nc, dve, core, st_set, count, step, var_set, tiles, part):
    st = core.stats[:, :].rearrange("p (n k) -> p n k", k=6)
    even, odd, sq_even, sq_odd = (tiles(st[:, :, k]) for k in (1, 4, 2, 5))
    mean, dif, var = tiles(core.mean[:, :]), tiles(core.dif[:, :]), tiles(core.var[:, :])
    dve.wait_ge(st_set, count)
    nc.vector.tensor_tensor(mean, even, odd, ALU.add).then_inc(step, 1)
    nc.vector.tensor_tensor(dif, even, odd, ALU.subtract).then_inc(step, 1)
    nc.vector.tensor_tensor(var, sq_even, sq_odd, ALU.add).then_inc(step, 1)
    dve.wait_ge(step, part * 5 + 3)
    nc.vector.tensor_scalar(mean, mean, 0.5, None, ALU.mult).then_inc(step, 1)
    nc.vector.scalar_tensor_tensor(dif, dif, 0.25, dif, ALU.mult, ALU.mult).then_inc(step, 1)
    dve.wait_ge(step, part * 5 + 5)
    nc.vector.scalar_tensor_tensor(var, var, 1.0 / D, dif, ALU.mult, ALU.add).then_inc(var_set, 1)


def between(first, end):
    return lambda ap: ap[:, first:end]


def embed_phase(core):
    nc, a, H, ps = core.nc, core.a, core.H, core.ps
    with ExitStack() as ctx:
        def sb(name, shape, dt=F32):
            return ctx.enter_context(nc.sbuf_tensor(name, shape, dt))

        def sem(name):
            return ctx.enter_context(nc.semaphore(name))

        patches = sb("patches", [P, KP * B * NPATCH])
        wtok = sb("wtok", [P, KP * D])
        tokb = sb("tokb", [2 * NPATCH, D])
        emb = sb("emb", [2 * NPATCH, 4 * D])
        pick = sb("pick", [2 * NPATCH, 2 * T_IMG * P])
        basis = sb("basis", [FREQ + 1, 2 * P - 1])
        wfilt = sb("wfilt_bias", [FREQ + 1, D])
        rows = sb("filter_rows", [HALF, 2, TROW])
        filt_in, tok_in, pick_in, txt_in = sem("e_filt_in"), sem("e_tok_in"), sem("e_pick_in"), sem("e_txt_in")
        filt_mm, rows_set, rows_zero, rows_out = sem("e_filt_mm"), sem("e_rows_set"), sem("e_rows_zero"), sem("e_rows_out")
        emb_mm, emb_set, tok_mm, tok_set = sem("e_emb_mm"), sem("e_emb_set"), sem("e_tok_mm"), sem("e_tok_set")
        st_set, dve_step, var_set, pool_step, rstd_set = sem("e_st_set"), sem("e_dve_step"), sem("e_var_set"), sem("e_pool_step"), sem("e_rstd_set")
        powers_set = sem("e_powers_set")
        h_tiles = H[:, :].rearrange("p (b i c) -> p b i c", b=B, i=TB)

        def image(ap):
            return ap.rearrange("p (b i) -> p b i", b=B)[:, :, 0:T_IMG]

        def text(ap):
            return ap.rearrange("p (b i) -> p b i", b=B)[:, :, T_IMG:TB]

        with nc.Block() as block:
            @block.sync
            def _(sp):
                sp.dma_start(wfilt[0:FREQ, :], a["w_filt"]).then_inc(filt_in, 16)
                sp.dma_start(wfilt[FREQ:FREQ + 1, :], a["b_filt"].rearrange("(a c) -> a c", a=1)).then_inc(filt_in, 16)
                sp.dma_start(basis[:, :], a["basis"]).then_inc(filt_in, 16)
                sp.dma_start(wtok[:, :], a["wtok"]).then_inc(tok_in, 16)
                sp.dma_start(patches[:, :], a["patches"]).then_inc(tok_in, 16)
                sp.dma_start(tokb[:, :], a["tok_b"].rearrange("(a c) -> a c", a=1).broadcast_to((2 * NPATCH, D))).then_inc(tok_in, 16)
                sp.dma_start(pick[:, :], a["pick"]).then_inc(pick_in, 16)
                sp.wait_ge(rows_out, 16)

            @block.scalar
            def _(act):
                act.dma_start(core.ident[:, :], a["ident"]).then_inc(pick_in, 16)
                for b in range(B):
                    act.dma_start(h_tiles[:, b, T_IMG:TB, :], a["txt"][b].rearrange("(i p) c -> p i c", p=P)).then_inc(txt_in, 16)
                act.wait_ge(rows_set, 2)
                act.dma_start(core.filt_dram.rearrange("(h c) t -> c h t", h=2), rows[:, :, :]).then_inc(rows_out, 16)

            @block.gpsimd
            def _(pool):
                nc.gpsimd.memset(rows[:, :, :], 0.0).then_inc(rows_zero, 1)
                nc.gpsimd.memset(core.powers[:, :], -0.5).then_inc(powers_set, 1)
                pool.wait_ge(powers_set, 1)
                rsqrt_on_pool(nc, pool, core, var_set, pool_step, rstd_set, text, 0)
                rsqrt_on_pool(nc, pool, core, var_set, pool_step, rstd_set, image, 1)
                pool.wait_ge(rstd_set, 2)

            @block.tensor
            def _(pe):
                pe.wait_ge(filt_in, 48)
                for h in range(2):
                    nc.tensor.matmul(ps[0:HALF, h, 0:2 * P - 1], wfilt[:, h * HALF:(h + 1) * HALF], basis[:, :],
                                     start=True, stop=True).then_inc(filt_mm, 1)
                pe.wait_ge(tok_in, 48)
                for m in range(4):
                    for k in range(KP):
                        off = k * B * NPATCH + m * 2 * NPATCH
                        last = nc.tensor.matmul(ps[0:2 * NPATCH, 2 + m, 0:D], patches[:, off:off + 2 * NPATCH],
                                                wtok[:, k * D:(k + 1) * D], start=(k == 0), stop=(k == KP - 1))
                    last.then_inc(emb_mm, 1)
                pe.wait_ge(emb_set, 4)
                pe.wait_ge(pick_in, 32)
                for t in range(B * T_IMG):
                    b, i = t // T_IMG, t % T_IMG
                    m, r = b // 2, b % 2
                    if t >= 4:
                        pe.wait_ge(tok_set, t - 3)
                    off = (r * T_IMG + i) * P
                    nc.tensor.matmul(ps[:, 4 + t % 4, 0:D], pick[:, off:off + P], emb[:, m * D:(m + 1) * D],
                                     start=True, stop=True).then_inc(tok_mm, 1)

            @block.vector
            def _(dve):
                def statistics(first, end):
                    with dve.Fori(0, B // 4) as q:
                        for b in range(4):
                            for i in range(first, end):
                                n = q * (4 * TB) + (b * TB + i)
                                nc.vector.bn_stats(core.stats[:, col(n, 6)], H[:, col(n, D)]).then_inc(st_set, 1)

                dve.wait_ge(rows_zero, 1)
                for h in range(2):
                    dve.wait_ge(filt_mm, h + 1)
                    nc.vector.tensor_copy(rows[:, h, 0:P - 1], ps[0:HALF, h, 0:P - 1])
                    nc.vector.tensor_copy(rows[:, h, 2 * P - 1:3 * P - 1], ps[0:HALF, h, P - 1:2 * P - 1]).then_inc(rows_set, 1)
                dve.wait_ge(txt_in, 16 * B)
                statistics(T_IMG, TB)
                mean_and_var(nc, dve, core, st_set, B * (TB - T_IMG), dve_step, var_set, text, 0)
                for m in range(4):
                    dve.wait_ge(emb_mm, m + 1)
                    nc.vector.tensor_tensor(emb[:, m * D:(m + 1) * D], ps[0:2 * NPATCH, 2 + m, 0:D], tokb[:, :],
                                            ALU.add).then_inc(emb_set, 1)
                for t in range(B * T_IMG):
                    b, i = t // T_IMG, t % T_IMG
                    dve.wait_ge(tok_mm, t + 1)
                    nc.vector.tensor_copy(h_tiles[:, b, i, :], ps[:, 4 + t % 4, 0:D]).then_inc(tok_set, 1)
                dve.wait_ge(tok_set, B * T_IMG)
                statistics(0, T_IMG)
                mean_and_var(nc, dve, core, st_set, NT, dve_step, var_set, image, 1)


def project_phase(core):
    nc, a, H, ps = core.nc, core.a, core.H, core.ps
    with ExitStack() as ctx:
        def sb(name, shape, dt=F32):
            return ctx.enter_context(nc.sbuf_tensor(name, shape, dt))

        def sem(name):
            return ctx.enter_context(nc.semaphore(name))

        w_in = sb("w_in", [HALF + 1, 2, 4 * D])
        hn = sb("hn", [P, 2, D])
        hnT = sb("hnT", [HALF + 1, 2, 2, S + 2])
        sz = sb("silu_z", [P, 2, D])
        szv = sb("silu_z_v1", [P, 2, D])
        wsh = sb("w_short", [HALF, 2, 4])
        w_ready, hn_set, t_ready, hnT_set = sem("p_w_ready"), sem("p_hn_set"), sem("p_t_ready"), sem("p_hnT_set")
        zx_ready, zx_free, sz_set, szv_set, g_set = sem("p_zx_ready"), sem("p_zx_free"), sem("p_sz_set"), sem("p_szv_set"), sem("p_g_set")
        edges, ones_set, xs_step = sem("p_edges"), sem("p_ones_set"), sem("p_xs_step")
        XS = core.XS[0:HALF, :].rearrange("p (c t) -> p c t", c=2)
        with nc.Block() as block:
            @block.sync
            def _(sp):
                sp.dma_start(w_in[0:HALF, :, :], a["w_in"].rearrange("(c k) n -> k c n", c=2)).then_inc(w_ready, 16)
                sp.dma_start(w_in[HALF:HALF + 1, 1, :], a["b_in"].rearrange("(a c) -> a c", a=1)).then_inc(w_ready, 16)
                sp.dma_start(wsh[:, :, :], a["short"].rearrange("(c k) t -> k c t", c=2)).then_inc(w_ready, 16)

            @block.gpsimd
            def _(pool):
                nc.gpsimd.memset(hnT[0:HALF, :, :, 0:1], 0.0).then_inc(edges, 1)
                nc.gpsimd.memset(hnT[0:HALF, :, :, S + 1:S + 2], 0.0).then_inc(edges, 1)

            @block.vector
            def _(dve):
                def norm(n, u):
                    nc.vector.tensor_scalar(hn[:, u, :], H[:, col(n, D)], core.mean[:, bass.ds(n, 1)],
                                            core.rstd[:, bass.ds(n, 1)], ALU.subtract, ALU.mult).then_inc(hn_set, 1)

                def gate(n, u):
                    dve.wait_ge(sz_set, n + 1)
                    nc.vector.tensor_tensor(szv[:, u, :], sz[:, u, :], ps[:, 2 + u, D:2 * D], ALU.mult).then_inc(szv_set, 1)
                    dve.wait_ge(szv_set, n + 1)
                    nc.vector.tensor_tensor(core.GY[:, col(n, D)], szv[:, u, :], ps[:, 4 + u, 0:D], ALU.mult).then_inc(g_set, 1)

                def short_conv(b, w, k):
                    tap, c = k // 2, k % 2
                    out = XS[:, c, bass.ds(b * S, S)]
                    if tap == 0:
                        nc.vector.tensor_scalar(out, hnT[0:HALF, w, c, 0:S], wsh[:, c, 0:1], wsh[:, c, 3:4],
                                                ALU.mult, ALU.add).then_inc(xs_step, 1)
                    else:
                        dve.wait_ge(xs_step, b * 6 + k)
                        nc.vector.scalar_tensor_tensor(out, hnT[0:HALF, w, c, tap:tap + S], wsh[:, c, tap:tap + 1], out,
                                                       ALU.mult, ALU.add).then_inc(xs_step, 1)

                def batch(b, w, first, last):
                    for i in range(TB):
                        n, u = b * TB + i, i % 2
                        if not (last and i == TB - 1):
                            norm(n + 1, 1 - u)
                        dve.wait_ge(t_ready, n + 1)
                        if i == 0 and not first:
                            dve.wait_ge(xs_step, (b - 1) * 6 + 1)
                        nc.vector.tensor_copy(hnT[0:HALF, w, :, 1 + i * P:1 + (i + 1) * P],
                                              ps[0:HALF, u, 0:2 * P].rearrange("p (c t) -> p c t", c=2)).then_inc(hnT_set, 1)
                        if not (first and i == 0):
                            gate(n - 1, 1 - u)
                        if not first:
                            short_conv(b - 1, 1 - w, i)

                dve.sem_inc(xs_step, 1)
                norm(0, 0)
                nc.vector.memset(hnT[HALF:HALF + 1, :, 1, :], 1.0).then_inc(ones_set, 1)
                dve.wait_ge(w_ready, 48)
                dve.wait_ge(edges, 2)
                batch(0, 0, True, False)
                with dve.Fori(0, B // 2 - 1) as i:
                    batch(i * 2 + 1, 1, False, False)
                    batch(i * 2 + 2, 0, False, False)
                batch(B - 1, 1, False, True)
                gate(NT - 1, 1)
                for k in range(6):
                    short_conv(B - 1, 1, k)

            @block.tensor
            def _(pe):
                def transpose(n, u):
                    pe.wait_ge(hn_set, n + 1)
                    for c in range(2):
                        last = nc.tensor.transpose(ps[0:HALF, u, c * P:(c + 1) * P], hn[:, u, c * HALF:(c + 1) * HALF], core.ident[:, :])
                    last.then_inc(t_ready, 1)

                def batch(b, w, last):
                    for i in range(TB):
                        n, u = b * TB + i, i % 2
                        if not (last and i == TB - 1):
                            transpose(n + 1, 1 - u)
                        pe.wait_ge(hnT_set, n + 1)
                        pe.wait_ge(zx_free, n + 1)
                        t = slice(1 + i * P, 1 + (i + 1) * P)
                        for bank, at, c0, cols in ((2, 0, D, 2 * D), (4, 0, 3 * D, D), (4, D, 0, D)):
                            nc.tensor.matmul(ps[:, bank + u, at:at + cols], hnT[0:HALF, w, 0, t], w_in[0:HALF, 0, c0:c0 + cols], start=True, stop=False)
                            mm = nc.tensor.matmul(ps[:, bank + u, at:at + cols], hnT[:, w, 1, t], w_in[:, 1, c0:c0 + cols], start=False, stop=True)
                        mm.then_inc(zx_ready, 1)

                transpose(0, 0)
                pe.wait_ge(w_ready, 48)
                pe.wait_ge(edges, 2)
                pe.wait_ge(ones_set, 1)
                with pe.Fori(0, B // 2 - 1) as i:
                    for w in range(2):
                        batch(i * 2 + w, w, False)
                batch(B - 2, 0, False)
                batch(B - 1, 1, True)

            @block.scalar
            def _(act):
                act.sem_inc(zx_free, 2)

                def silu(n, u):
                    act.wait_ge(zx_ready, n + 1)
                    nc.scalar.activation(sz[:, u, :], ps[:, 2 + u, 0:D], ACT.Silu).then_inc(sz_set, 1)

                def keep_x(n, u):
                    act.wait_ge(g_set, n + 1)
                    nc.scalar.activation(core.XA[:, col(n, D)], ps[:, 4 + u, D:2 * D], ACT.Copy).then_inc(zx_free, 1)

                with act.Fori(0, NT // 2) as i:
                    for u in range(2):
                        silu(i * 2 + u, u)
                        keep_x(i * 2 + u, u)


def conv_phase(core):
    nc, a, ps = core.nc, core.a, core.ps
    with ExitStack() as ctx:
        def sb(name, shape, dt=F32):
            return ctx.enter_context(nc.sbuf_tensor(name, shape, dt))

        def sem(name):
            return ctx.enter_context(nc.semaphore(name))

        phi = sb("phi", [P, TB, P])
        psi = sb("psi", [P, TB, P])
        wf = sb("w_features", [P, D])
        toep = sb("toeplitz", [P, TG, TG, 2 * P])
        xc = sb("x_chunk", [P, CH, 2, 32])
        zw = sb("weighted_features", [P, TB, CH, B])
        edge = sb("edge_rows", [P, 2, TG, P])
        tab_in, xc_zero, xc_set = sem("c_tab_in"), sem("c_xc_zero"), sem("c_xc_set")
        toep_in = [sem(f"c_toep_in{g}") for g in range(TG)]
        toep_free = sem("c_toep_free")
        z_ready, zw_set, edge_set = sem("c_z_ready"), sem("c_zw_set"), sem("c_edge_set")
        y_ready, y_free = sem("c_y_ready"), sem("c_y_free")
        x4 = core.XA[:, :].rearrange("p (b i c) -> p b i c", b=B, i=TB)
        g4 = core.GY[:, :].rearrange("p (b i c) -> p b i c", b=B, i=TB)
        CHAINS = [(0, (0, 1, 2), 0), (1, (5, 4, 3), 5), (0, (3,), 1), (1, (2,), 4), (0, (4,), 2), (1, (1,), 3)]
        with nc.Block() as block:
            @block.sync
            def _(sp):
                sp.dma_start(phi[:, :, :], a["phi"]).then_inc(tab_in, 16)
                sp.dma_start(psi[:, :, :], a["psi"]).then_inc(tab_in, 16)
                sp.dma_start(wf[0:FREQ, :], a["w_filt"]).then_inc(tab_in, 16)
                sp.dma_start(wf[FREQ + 1:P, :], a["w_filt"][1:FREQ, :]).then_inc(tab_in, 16)
                sp.dma_start(wf[FREQ:FREQ + 1, :], a["b_filt"].rearrange("(a c) -> a c", a=1)).then_inc(tab_in, 16)
                with sp.Fori(0, NCHUNK) as q:
                    for g in range(TG):
                        sp.wait_ge(toep_free, q * TG + (g + 1))
                        rows = core.filt_dram[bass.ds(q * CH + g * TG, TG), 0:2 * P]
                        src = bass.AP(rows.tensor, rows.offset, [[1, P], [TROW, TG], [1, 2 * P]])
                        sp.dma_start(toep[:, g, :, :], src).then_inc(toep_in[g], 16)

            @block.gpsimd
            def _(pool):
                nc.gpsimd.memset(xc[:, :, :, :], 0.0).then_inc(xc_zero, 1)
                pool.wait_ge(xc_zero, 1)
                with pool.Fori(0, NCHUNK) as q:
                    pool.wait_ge(toep_free, q * TG + TG)
                    for half in range(2):
                        src = x4[:, :, HB * (1 - half):HB * (2 - half), bass.ds(q * CH, CH)].rearrange("p b i c -> p c i b")
                        dst = xc[:, :, half, 0:HB * B].rearrange("p c (i b) -> p c i b", i=HB)
                        nc.gpsimd.tensor_copy(dst, src).then_inc(xc_set, 1)

            @block.tensor
            def _(pe):
                pe.sem_inc(toep_free, TG)
                pe.wait_ge(tab_in, 80)

                def feature_sums(q, k):
                    bank, blocks, out = CHAINS[k]
                    if k >= 2:
                        pe.wait_ge(zw_set, q * 6 + (k - 1))
                    else:
                        pe.wait_ge(y_free, q * 2 + (k + 1))
                    for j in blocks:
                        mm = nc.tensor.matmul(ps[:, bank, 0:B * CH], phi[:, j, :], x4[:, :, j, bass.ds(q * CH, CH)],
                                              start=(k < 2 and j == blocks[0]), stop=True, skip_group_check=True)
                    mm.then_inc(z_ready, 1)

                def edge_products(q, g):
                    pe.wait_ge(toep_in[g], (q + 1) * 16)
                    for half in range(2):
                        for j in range(TG):
                            mm = nc.tensor.matmul(ps[32 * j:32 * j + 32, 2 + half, g * P:(g + 1) * P], xc[:, g * TG + j, half, :],
                                                  toep[:, g, j, half * P:(half + 1) * P], start=True, stop=True)
                    mm.then_inc(toep_free, 1)

                with pe.Fori(0, NCHUNK) as q:
                    feature_sums(q, 0)
                    feature_sums(q, 1)
                    pe.wait_ge(xc_set, q * 2 + 2)
                    pe.wait_ge(edge_set, q * 2 + 2)
                    edge_products(q, 0)
                    feature_sums(q, 2)
                    feature_sums(q, 3)
                    edge_products(q, 1)
                    feature_sums(q, 4)
                    feature_sums(q, 5)
                    edge_products(q, 2)
                    edge_products(q, 3)
                    for half in range(2):
                        for i in range(HB):
                            out = half * HB + i
                            k = [c[2] for c in CHAINS].index(out)
                            pe.wait_ge(zw_set, q * 6 + (k + 1))
                            dst = ps[:, 4 + half, :].rearrange("p (c k) -> p c k", k=32)[:, :, i * B:(i + 1) * B]
                            nc.tensor.matmul(dst, psi[:, out, :], zw[:, out, :, :], start=(i == 0), stop=True, skip_group_check=True)
                        pe.wait_ge(edge_set, q * 2 + (half + 3))
                        for g in range(TG):
                            mm = nc.tensor.matmul(ps[:, 4 + half, g * P:(g + 1) * P], edge[:, half, g, :], core.ident[:, :],
                                                  start=False, stop=True, skip_group_check=True)
                        mm.then_inc(y_ready, 1)

            @block.scalar
            def _(act):
                act.sem_inc(edge_set, 2)
                with act.Fori(0, NCHUNK) as q:
                    act.wait_ge(toep_free, q * TG + 2 * TG)
                    for half in range(2):
                        act.wait_ge(y_free, q * 2 + (half + 1))
                        src = ps[:, 2 + half, :].rearrange("p (g t) -> p g t", g=TG)[:, :, ::-1]
                        nc.scalar.activation(edge[:, half, :, :], src, ACT.Copy).then_inc(edge_set, 1)

            @block.vector
            def _(dve):
                dve.sem_inc(y_free, 2)
                dve.wait_ge(tab_in, 80)
                with dve.Fori(0, NCHUNK) as q:
                    for k, (bank, _, out) in enumerate(CHAINS):
                        dve.wait_ge(z_ready, q * 6 + (k + 1))
                        dst = zw[:, out, :, :].rearrange("p c b -> p b c")
                        src = ps[:, bank, 0:B * CH].rearrange("p (b c) -> p b c", b=B)
                        w = wf[:, bass.ds(q * CH, CH)].rearrange("p (a c) -> p a c", a=1).broadcast_to((P, B, CH))
                        nc.vector.tensor_tensor(dst, src, w, ALU.mult).then_inc(zw_set, 1)
                    for half in range(2):
                        dve.wait_ge(y_ready, q * 2 + (half + 1))
                        src = ps[:, 4 + half, :].rearrange("p (c k) -> p c k", k=32)[:, :, 0:HB * B]
                        src = src.rearrange("p c (i b) -> p b i c", i=HB)
                        y = g4[:, :, half * HB:(half + 1) * HB, bass.ds(q * CH, CH)]
                        nc.vector.tensor_tensor(y, src, y, ALU.mult).then_inc(y_free, 1)


def mix_out_phase(core):
    nc, a, H, ps = core.nc, core.a, core.H, core.ps
    with ExitStack() as ctx:
        def sb(name, shape, dt=F32):
            return ctx.enter_context(nc.sbuf_tensor(name, shape, dt))

        def sem(name):
            return ctx.enter_context(nc.semaphore(name))

        w_out = sb("w_out", [HALF + 1, 2, D])
        yt = sb("y_tile", [P, 2, D])
        sT = sb("sumT", [HALF + 1, 2, 2, P])
        w_ready, ones, yt_set, t_ready, sT_set = sem("o_w_ready"), sem("o_ones"), sem("o_yt_set"), sem("o_t_ready"), sem("o_sT_set")
        o_ready, h_set, st_set, var_set = sem("o_o_ready"), sem("o_h_set"), sem("o_st_set"), sem("o_var_set")
        x_set, st2_set, var2_set, dve_step, dve_step2 = sem("o_x_set"), sem("o_st2_set"), sem("o_var2_set"), sem("o_dve_step"), sem("o_dve_step2")
        pool_step2, rstd_set, rstd2_set = sem("o_pool_step2"), sem("o_rstd_set"), sem("o_rstd2_set")
        stats = sb("h_stats", [P, TB, 6])
        mean, var, dif, rstd = (sb("h_" + k, [P, TB]) for k in ("mean", "var", "dif", "rstd"))
        XS = core.XS[0:HALF, :].rearrange("p (c t) -> p c t", c=2)
        NP = NT // 2
        with nc.Block() as block:
            @block.sync
            def _(sp):
                sp.dma_start(w_out[0:HALF, :, :], a["w_out"].rearrange("(c k) n -> k c n", c=2)).then_inc(w_ready, 16)
                sp.dma_start(w_out[HALF:HALF + 1, 1, :], a["b_out"].rearrange("(a c) -> a c", a=1)).then_inc(w_ready, 16)

            @block.gpsimd
            def _(pool):
                nc.gpsimd.memset(sT[HALF:HALF + 1, :, :, :], 1.0).then_inc(ones, 1)
                pool.wait_ge(ones, 1)
                with pool.Fori(0, B - 1) as b:
                    pool.wait_ge(var_set, b + 1)
                    nc.gpsimd.tensor_tensor(rstd[:, :], var[:, :], core.powers[:, 0:TB], ALU.pow).then_inc(rstd_set, 1)
                rsqrt_on_pool(nc, pool, core, var2_set, pool_step2, rstd2_set, between(0, NT - 2 * TB), 0)
                pool.wait_ge(var_set, B)
                nc.gpsimd.tensor_tensor(rstd[:, :], var[:, :], core.powers[:, 0:TB], ALU.pow).then_inc(rstd_set, 1)
                rsqrt_on_pool(nc, pool, core, var2_set, pool_step2, rstd2_set, between(NT - 2 * TB, NT), 1)
                pool.wait_ge(rstd2_set, 2)

            @block.scalar
            def _(act):
                for u in range(2):
                    nc.scalar.activation(yt[:, u, :], core.GY[:, col(u, D)], ACT.Copy).then_inc(yt_set, 1)
                with act.Fori(1, NP) as i:
                    for u in range(2):
                        act.wait_ge(t_ready, i * 2 + (u - 1))
                        nc.scalar.activation(yt[:, u, :], core.GY[:, col(i * 2 + u, D)], ACT.Copy).then_inc(yt_set, 1)

            @block.tensor
            def _(pe):
                def transpose(n, u):
                    pe.wait_ge(yt_set, n + 1)
                    for c in range(2):
                        mm = nc.tensor.transpose(ps[0:HALF, u, c * P:(c + 1) * P], yt[:, u, c * HALF:(c + 1) * HALF], core.ident[:, :])
                    mm.then_inc(t_ready, 1)

                def pair(i, last):
                    for u in range(2):
                        n = i * 2 + u
                        if not (last and u == 1):
                            transpose(n + 1, 1 - u)
                        pe.wait_ge(sT_set, n + 1)
                        pe.wait_ge(h_set, n + 1)
                        nc.tensor.matmul(ps[:, 2 + u, 0:D], sT[0:HALF, u, 0, :], w_out[0:HALF, 0, :], start=True, stop=False)
                        nc.tensor.matmul(ps[:, 2 + u, 0:D], sT[:, u, 1, :], w_out[:, 1, :], start=False, stop=True).then_inc(o_ready, 1)

                pe.wait_ge(w_ready, 32)
                pe.wait_ge(ones, 1)
                transpose(0, 0)
                with pe.Fori(0, NP - 1) as i:
                    pair(i, False)
                pair(NP - 1, True)

            @block.vector
            def _(dve):
                dve.sem_inc(h_set, 2)

                def add_short(n, u):
                    dve.wait_ge(t_ready, n + 1)
                    nc.vector.tensor_tensor(sT[0:HALF, u, :, :], ps[0:HALF, u, 0:2 * P].rearrange("p (c t) -> p c t", c=2),
                                            XS[:, :, col(n, P)], ALU.add).then_inc(sT_set, 1)

                def resid(n, u):
                    dve.wait_ge(o_ready, n + 1)
                    dve.wait_ge(h_set, n + 2)
                    nc.vector.tensor_tensor(H[:, col(n, D)], ps[:, 2 + u, 0:D], H[:, col(n, D)], ALU.add).then_inc(h_set, 1)

                def stat_h(n, i):
                    nc.vector.bn_stats(stats[:, i, :], H[:, col(n, D)]).then_inc(st_set, 1)

                def moments(b):
                    def then(k, op):
                        op.then_inc(dve_step, 1)
                        if k in (3, 5, 6):
                            dve.wait_ge(dve_step, b * 6 + k)

                    even, odd, sq_even, sq_odd = stats[:, :, 1], stats[:, :, 4], stats[:, :, 2], stats[:, :, 5]
                    dve.wait_ge(st_set, b * TB + TB)
                    then(1, nc.vector.tensor_tensor(mean[:, :], even, odd, ALU.add))
                    then(2, nc.vector.tensor_tensor(dif[:, :], even, odd, ALU.subtract))
                    then(3, nc.vector.tensor_tensor(var[:, :], sq_even, sq_odd, ALU.add))
                    then(4, nc.vector.tensor_scalar(mean[:, :], mean[:, :], 0.5, None, ALU.mult))
                    then(5, nc.vector.scalar_tensor_tensor(dif[:, :], dif[:, :], 0.25, dif[:, :], ALU.mult, ALU.mult))
                    then(6, nc.vector.scalar_tensor_tensor(var[:, :], var[:, :], 1.0 / D, dif[:, :], ALU.mult, ALU.add))
                    nc.vector.tensor_scalar(var[:, :], var[:, :], EPS, None, ALU.add).then_inc(var_set, 1)

                def norm_h(b, i):
                    if i == 0:
                        dve.wait_ge(rstd_set, b + 1)
                    n = b * TB + i
                    nc.vector.tensor_scalar(core.XA[:, col(n, D)], H[:, col(n, D)], mean[:, i:i + 1], rstd[:, i:i + 1],
                                            ALU.subtract, ALU.mult).then_inc(x_set, 1)

                def stat_x(b, i):
                    n = b * TB + i
                    dve.wait_ge(x_set, n + 1)
                    nc.vector.bn_stats(core.stats[:, col(n, 6)], core.XA[:, col(n, D)]).then_inc(st2_set, 1)

                NORM = {2: (0,), 3: (1, 2), 4: (3, 4), 5: (5,)}
                MEASURE = {3: (0,), 4: (1, 2), 5: (3, 4)}

                def batch(b, before, last):
                    for i in range(TB):
                        n = b * TB + i
                        if not (last and i == TB - 1):
                            add_short(n + 1, (i + 1) % 2)
                        resid(n, i % 2)
                        if i > 0:
                            stat_h(n - 1, i - 1)
                        elif before > 0:
                            stat_h(n - 1, TB - 1)
                            if before > 1:
                                stat_x(b - 2, TB - 1)
                            moments(b - 1)
                            if last:
                                mean_and_var(nc, dve, core, st2_set, NT - 2 * TB, dve_step2, var2_set, between(0, NT - 2 * TB), 0)
                        if before > 0:
                            for k in NORM.get(i, ()):
                                norm_h(b - 1, k)
                            for k in MEASURE.get(i, ()):
                                stat_x(b - 1, k)

                add_short(0, 0)
                batch(0, 0, False)
                batch(1, 1, False)
                with dve.Fori(2, B - 1) as b:
                    batch(b, 2, False)
                batch(B - 1, 2, True)
                dve.wait_ge(h_set, NT + 2)
                stat_h(NT - 1, TB - 1)
                stat_x(B - 2, TB - 1)
                moments(B - 1)
                for i in range(TB):
                    norm_h(B - 1, i)
                for i in range(TB):
                    stat_x(B - 1, i)
                mean_and_var(nc, dve, core, st2_set, NT, dve_step2, var2_set, between(NT - 2 * TB, NT), 1)


def attention_phase(core):
    nc, a, ps = core.nc, core.a, core.ps
    X = core.XA
    with ExitStack() as ctx:
        def sb(name, shape, dt=F32):
            return ctx.enter_context(nc.sbuf_tensor(name, shape, dt))

        def sem(name):
            return ctx.enter_context(nc.semaphore("a_" + name))

        QS = core.XS[0:KROWS, 0:HEADS * S // 2].bitcast(BF16).rearrange("p (h t) -> p h t", h=HEADS)
        KS = core.XS[0:KROWS, HEADS * S // 2:HEADS * S].bitcast(BF16).rearrange("p (h t) -> p h t", h=HEADS)
        PT2 = core.XS[:, HEADS * S:NT * P * 2].rearrange("p (u h t) -> p u h t", u=2, h=GH)
        V = core.GY[:, 0:TB * HEADS * 32].rearrange("p (i h c) -> p i h c", i=TB, h=HEADS)
        at = TB * HEADS * 32
        VN = core.GY[:, at:at + TB * D].rearrange("p (i c) -> p i c", i=TB)
        at += TB * D
        PT = [PT2[:, 0], PT2[:, 1], core.GY[:, at:at + GH * QH].rearrange("p (h t) -> p h t", h=GH)]
        at += GH * QH
        parts = core.GY[:, at:at + 9 * S // 2].bitcast(BF16).rearrange("p (k j t) -> p k j t", k=3, j=3)

        qkv_w = sb("qkv_w", [HALF, 2, 3 * D])
        proj_w = sb("proj_w", [HALF + 1, 2, D])
        aff = sb("affine1", [HALF, 2, 4])
        xn = sb("xn", [P, 2, D])
        hT = sb("hT", [HALF, 2, S])
        R = sb("qk_rest", [P, 3, S])
        mx = sb("half_max", [P, NG, GH * TB, 2])
        mxq = sb("score_max", [P, NG, GH * TB])
        nm = sb("minus_max", [GH * TB, 2, P])
        nm_parts = sb("minus_max_parts", [GH * TB, NG, 3, P], BF16)
        ov = sb("numer_denom", [P, QH])
        rc = sb("recip_denom", [P, HB, GH])
        O = sb("attn_out", [P, TB, D])
        oT = sb("attn_outT", [HALF + 1, 2, 2, P])
        qk_dram = nc.dram_tensor("qk_parts", (3, 2 * D, S), BF16, kind="Internal").ap()

        w_in, const_set, xn_set = sem("w_in"), sem("const_set"), sem("xn_set")
        prep_ready, prep_free, h_part, r_set, m_part, l_set = (sem(n) for n in ("prep_ready", "prep_free", "h_part", "r_set", "m_part", "l_set"))
        v_set, v_full, qk_out = sem("v_set"), sem("v_full"), sem("qk_out")
        qk_in = [sem(f"qk_in{g}") for g in range(NG)]
        s_ready, mx_set, nm_step, nm_set, aug_in = (sem(n) for n in ("s_ready", "mx_set", "nm_step", "nm_set", "aug_in"))
        st_ready, exp_set, pv_done, ov_set, rc_set = (sem(n) for n in ("st_ready", "exp_set", "pv_done", "ov_set", "rc_set"))
        b6_ready, b6_free, st_set = sem("b6_ready"), sem("b6_free"), sem("st_set")
        dve_step, var_set, pool_step, rstd_set = sem("dve_step"), sem("var_set"), sem("pool_step"), sem("rstd_set")

        MICRO = 2 * TB
        M_ALL = NG * MICRO
        UNITS = GH * TB * 2
        MAXIMA = UNITS + 1
        AHEAD = 15
        SB, XB = 3, 2
        JOBS = TB + 1 + 6
        PREP_AT = 1
        MIDDLE = {PREP_AT + TB + 4 + 2 * t: t for t in range(3)}
        B6 = {1: "o21"} | {2 + j: f"tail{j}" for j in range(TB + 1)} | {
            9: "m1", 10: "o00", 13: "o01", 19: "o10", 21: "m2", 25: "o11", 31: "o20", 33: "m0"}
        ORDER = list(B6.values())
        LATE = TB + 2

        def b6(b, what):
            if isinstance(b, int) and b < 0:
                return 0
            none = 1 if isinstance(b, int) and b == B else 0
            return b * len(ORDER) + (ORDER.index(what) - LATE + 1 - none)

        def prep_bank(j, banks):
            return 7 if banks == 1 else 6 + j % 2

        def ahead(b, M):
            return (b, M + AHEAD) if M + AHEAD < M_ALL else (b + 1, M + AHEAD - M_ALL)

        with nc.Block() as block:
            @block.sync
            def _(sp):
                sp.dma_start(qkv_w[:, :, :], a["qkv_w"].rearrange("(c k) n -> k c n", c=2)).then_inc(w_in, 16)
                sp.dma_start(proj_w[0:HALF, :, :], a["proj_w"].rearrange("(c k) n -> k c n", c=2)).then_inc(w_in, 16)
                sp.dma_start(proj_w[HALF:HALF + 1, 1, :], a["proj_b"].rearrange("(a c) -> a c", a=1)).then_inc(w_in, 16)
                sp.dma_start(aff[:, :, :], a["affine"].rearrange("(c k) t -> k c t", c=2)).then_inc(w_in, 16)

                def parts_out(nb, blocks):
                    for t in blocks:
                        sp.wait_ge(l_set, nb * 3 + (t + 1))
                        sp.dma_start(qk_dram[:, t * P:(t + 1) * P, :].rearrange("j p t -> p j t"), parts[:, t, :, :]).then_inc(qk_out, 16)

                def load(g):
                    hs = slice(g * GH, (g + 1) * GH)
                    row = 0
                    for part, times in ((0, 3), (1, 2), (2, 1)):
                        for _ in range(times):
                            src = qk_dram[part, g * GH * HD:(g + 1) * GH * HD, :].rearrange("(h r) t -> r h t", h=GH)
                            sp.dma_start(QS[row:row + HD, hs, :], src).then_inc(qk_in[g], 16)
                            row += HD
                    row = 0
                    for n in (3, 2, 1):
                        for part in range(n):
                            src = qk_dram[part, D + g * GH * HD:D + (g + 1) * GH * HD, :].rearrange("(h r) t -> r h t", h=GH)
                            sp.dma_start(KS[row:row + HD, hs, :], src).then_inc(qk_in[g], 16)
                            row += HD

                def maxima_in(b, g):
                    sp.wait_ge(nm_set, b * NG + (g + 1))
                    for j in range(3):
                        dst = QS[SPLIT + j:SPLIT + j + 1, g * GH:(g + 1) * GH, :].rearrange("a h (i t) -> a (h i) t", i=TB)
                        sp.dma_start(dst, nm_parts[:, g, j, :]).then_inc(aug_in, 16)

                def group_done(b, g):
                    sp.wait_ge(st_ready, b * (NG * MICRO * GH) + (g + 1) * MICRO * GH)

                parts_out(0, (0, 1))
                sp.wait_ge(qk_out, 32)
                load(0)
                parts_out(0, (2,))
                sp.wait_ge(qk_out, 48)
                for g in range(1, NG):
                    load(g)
                maxima_in(0, 0)
                with sp.Fori(0, B - 1) as b:
                    maxima_in(b, 1)
                    for g in range(NG):
                        sp.wait_ge(qk_in[g], b * 192 + 192)
                    parts_out(b + 1, (0, 1))
                    sp.wait_ge(qk_out, b * 48 + 80)
                    group_done(b, 0)
                    load(0)
                    parts_out(b + 1, (2,))
                    maxima_in(b, 2)
                    group_done(b, 1)
                    sp.wait_ge(qk_out, (b + 2) * 48)
                    load(1)
                    maxima_in(b + 1, 0)
                    group_done(b, 2)
                    load(2)
                maxima_in(B - 1, 1)
                maxima_in(B - 1, 2)

            @block.gpsimd
            def _(pool):
                nc.gpsimd.memset(KS[SPLIT:KROWS, :, :], 1.0).then_inc(const_set, 1)
                pool.wait_ge(const_set, 1)
                nc.gpsimd.memset(V[:, :, :, HD:HD + 1], 1.0).then_inc(const_set, 1)
                nc.gpsimd.memset(V[:, :, :, HD + 1:32], 0.0).then_inc(const_set, 1)
                pool.wait_ge(const_set, 3)
                nc.gpsimd.memset(oT[HALF:HALF + 1, :, :, :], 1.0).then_inc(const_set, 1)

                def low_parts(nb):
                    for t in range(3):
                        pool.wait_ge(m_part, nb * 3 + (t + 1))
                        nc.gpsimd.tensor_tensor(parts[:, t, 2, :], R[:, t, :], parts[:, t, 1, :], ALU.subtract).then_inc(l_set, 1)

                def place_values(nb, before):
                    pool.wait_ge(v_set, nb * TB + TB)
                    for g in range(NG):
                        hs = slice(g * GH, (g + 1) * GH)
                        ones = V[:, :, hs, HD:HD + 1].broadcast_to((P, TB, GH, HD))
                        if before is not None:
                            pool.wait_ge(pv_done, before * M_ALL + ((g + 1) * MICRO + 3))
                        nc.gpsimd.tensor_tensor(V[:, :, hs, 0:HD], VN[:, :, g * GH * HD:(g + 1) * GH * HD].rearrange("p i (h c) -> p i h c", h=GH),
                                                ones, ALU.mult).then_inc(v_full, 1)

                pool.wait_ge(const_set, 4)
                low_parts(0)
                place_values(0, None)
                with pool.Fori(0, B - 1) as b:
                    low_parts(b + 1)
                    place_values(b + 1, b)
                rsqrt_on_pool(nc, pool, core, var_set, pool_step, rstd_set, between(0, NT - TB), 0)
                rsqrt_on_pool(nc, pool, core, var_set, pool_step, rstd_set, between(NT - TB, NT), 1)
                pool.wait_ge(rstd_set, 2)

            @block.tensor
            def _(pe):
                def prep_job(nb, j, banks=1):
                    bank = prep_bank(j, banks)
                    if j <= TB + 1 and j + 2 - banks > 0:
                        pe.wait_ge(prep_free, nb * (TB + 1) + (j + 2 - banks))
                    if j == 0:
                        pe.wait_ge(r_set, nb * 6 + 1)
                    if j > TB + 1:
                        pe.wait_ge(r_set, nb * 6 + (j - TB + 1 - banks))
                    if j < TB:
                        pe.wait_ge(xn_set, nb * TB + (j + 1))
                        for c in range(2):
                            mm = nc.tensor.transpose(ps[0:HALF, bank, c * P:(c + 1) * P], xn[:, j % 2, c * HALF:(c + 1) * HALF], core.ident[:, :])
                    if banks == 2 and 0 < j <= TB + 1:
                        pe.wait_ge(prep_free, nb * (TB + 1) + (j + 1))
                    if 0 < j <= TB:
                        for c in range(2):
                            mm = nc.tensor.matmul(ps[:, bank, 2 * P:2 * P + D], hT[:, c, (j - 1) * P:j * P], qkv_w[:, c, 2 * D:3 * D],
                                                  start=(c == 0), stop=(c == 1))
                    if j > TB:
                        t, half = (j - TB - 1) // 2, (j - TB - 1) % 2
                        for c in range(2):
                            mm = nc.tensor.matmul(ps[:, bank, 0:QH], qkv_w[:, c, t * P:(t + 1) * P], hT[:, c, half * QH:(half + 1) * QH],
                                                  start=(c == 0), stop=(c == 1))
                    mm.then_inc(prep_ready, 1)

                def scores(b, t, q):
                    g, k = t // MICRO, t % MICRO * GH + q
                    h, i, half = k // (2 * TB), k // 2 % TB, k % 2
                    if k == 0:
                        pe.wait_ge(qk_in[g], b * 192 + 192)
                    done = g * MAXIMA + (k + 1 if k >= SB else k)
                    if done > 0 or not (isinstance(b, int) and b == 0):
                        pe.wait_ge(mx_set, b * (NG * MAXIMA) + done)
                    nc.tensor.matmul(ps[:, k % SB, 0:QH], QS[0:SPLIT, g * GH + h, i * P:(i + 1) * P],
                                     KS[0:SPLIT, g * GH + h, half * QH:(half + 1) * QH], start=True, stop=True).then_inc(s_ready, 1)

                def exp_scores(b, M, h):
                    g, half, j = M // MICRO, M % MICRO // TB, M % TB
                    c = M * GH + h
                    if M % MICRO == 0 and h == 0:
                        pe.wait_ge(aug_in, b * 144 + (g + 1) * 48)
                    pe.wait_ge(exp_set, b * (M_ALL * GH) + (c + 1))
                    nc.tensor.matmul(ps[:, SB + c % XB, 0:QH], KS[:, g * GH + h, j * P:(j + 1) * P],
                                     QS[:, g * GH + h, half * QH:(half + 1) * QH], start=True, stop=True).then_inc(st_ready, 1)

                def weigh_values(b, M):
                    g, half, j = M // MICRO, M % MICRO // TB, M % TB
                    if M % MICRO == 0:
                        pe.wait_ge(v_full, b * NG + (g + 1))
                    pe.wait_ge(exp_set, b * (M_ALL * GH) + ((M + 1) * GH + XB))
                    if j == 0:
                        pe.wait_ge(ov_set, b * (2 * NG) + (2 * g + half + 1))
                    for h in range(GH):
                        mm = nc.tensor.matmul(ps[32 * h:32 * h + 32, 5, 0:QH], V[:, j, g * GH + h, :], PT[M % 3][:, h, :],
                                              start=(j == 0), stop=(j == TB - 1))
                    mm.then_inc(pv_done, 1)

                def bank6_job(b, what):
                    pe.wait_ge(b6_free, b6(b, what) + 1)
                    if what[0] == "m":
                        g = int(what[1])
                        mb = b + 1 if g == 0 else b
                        pe.wait_ge(mx_set, mb * (NG * MAXIMA) + ((g + 1) * MAXIMA + SB))
                        mm = nc.tensor.transpose(ps[0:GH * TB, 6, 0:P], mxq[:, g, :], core.ident[:, :])
                    elif what[0] == "o":
                        g, half = int(what[1]), int(what[2])
                        ob = b - 1 if what == "o21" else b
                        pe.wait_ge(ov_set, ob * (2 * NG) + (2 * g + half + 2))
                        for i in range(HB):
                            mm = nc.tensor.transpose(ps[:, 6, i * P:(i + 1) * P], ov[:, i * P:(i + 1) * P], core.ident[:, :])
                    else:
                        j = int(what[4])
                        if j < TB:
                            for c in range(2):
                                mm = nc.tensor.transpose(ps[0:HALF, 6, c * P:(c + 1) * P], O[:, j, c * HALF:(c + 1) * HALF], core.ident[:, :])
                        if j > 0:
                            k = j - 1
                            nc.tensor.matmul(ps[:, 6, 2 * P:2 * P + D], oT[0:HALF, k % 2, 0, :], proj_w[0:HALF, 0, :], start=True, stop=False)
                            mm = nc.tensor.matmul(ps[:, 6, 2 * P:2 * P + D], oT[:, k % 2, 1, :], proj_w[:, 1, :], start=False, stop=True)
                    mm.then_inc(b6_ready, 1)

                def batch(b, first, last):
                    for M in range(M_ALL):
                        mb, t = ahead(b, M)
                        more = not last or M + AHEAD < M_ALL
                        for q in range(GH):
                            exp_scores(b, M, q)
                            if more:
                                scores(mb, t, q)
                            if q == 1 and M > 0:
                                weigh_values(b, M - 1)
                            if q == 1 and M == 0 and not first:
                                weigh_values(b - 1, M_ALL - 1)
                        if M in B6 and not (first and M < 2 + TB + 1) and not (last and B6[M] == "m0"):
                            bank6_job(b, B6[M])
                        if not last and 0 <= M - PREP_AT < JOBS:
                            prep_job(b + 1, M - PREP_AT)

                pe.wait_ge(w_in, 64)
                pe.sem_inc(pv_done, 3)
                for j in range(JOBS):
                    prep_job(0, j, 2)
                pe.wait_ge(const_set, 4)
                for t in range(AHEAD):
                    for q in range(GH):
                        scores(0, t, q)
                    if t == MICRO:
                        bank6_job(-1, "m0")
                batch(0, True, False)
                with pe.Fori(1, B - 1) as b:
                    batch(b, False, False)
                batch(B - 1, False, True)
                weigh_values(B - 1, M_ALL - 1)
                for what in ORDER[:LATE]:
                    bank6_job(B, what)

            @block.scalar
            def _(act):
                def read_prep(nb, j, banks=1):
                    bank = prep_bank(j, banks)
                    act.wait_ge(prep_ready, nb * JOBS + (j + 1))
                    if 0 < j <= TB:
                        if j == 1 and not (isinstance(nb, int) and nb == 0):
                            act.wait_ge(v_full, nb * NG)
                        op = nc.scalar.activation(VN[:, j - 1, :], ps[:, bank, 2 * P:2 * P + D], ACT.Copy)
                        op.then_inc(v_set, 1)
                    if j < TB:
                        for c in range(2):
                            op = nc.scalar.activation(hT[:, c, j * P:(j + 1) * P], ps[0:HALF, bank, c * P:(c + 1) * P],
                                                      ACT.Identity, scale=aff[:, c, 0:1], bias=aff[:, c, 1:2])
                    if j < TB:
                        op.then_inc(prep_free, 1)
                    elif j == TB:
                        act.wait_ge(v_set, nb * TB + TB)
                        act.sem_inc(prep_free, 1)
                    else:
                        t, half = (j - TB - 1) // 2, (j - TB - 1) % 2
                        if j == TB + 1 and not (isinstance(nb, int) and nb == 0):
                            act.wait_ge(qk_out, nb * 48)
                        nc.scalar.activation(parts[:, t, 0, half * QH:(half + 1) * QH], ps[:, bank, 0:QH], ACT.Copy).then_inc(h_part, 1)

                def middle_part(nb, t):
                    act.wait_ge(r_set, nb * 6 + (2 * t + 3))
                    nc.scalar.activation(parts[:, t, 1, :], R[:, t, :], ACT.Copy).then_inc(m_part, 1)

                def keep_sums(b, g, half):
                    act.wait_ge(pv_done, b * M_ALL + ((2 * g + half + 1) * TB + 3))
                    nc.scalar.activation(ov[:, :], ps[:, 5, 0:QH], ACT.Copy).then_inc(ov_set, 1)

                def batch(b, first, last):
                    for M in range(M_ALL):
                        act.wait_ge(pv_done, b * M_ALL + (M + 1))
                        for h in range(GH):
                            c = M * GH + h
                            act.wait_ge(st_ready, b * (M_ALL * GH) + (c + 1))
                            nc.scalar.activation(PT[M % 3][:, h, :], ps[:, SB + c % XB, 0:QH], ACT.Exp, scale=HD ** -0.5).then_inc(exp_set, 1)
                        if M == 0 and not first:
                            keep_sums(b - 1, NG - 1, 1)
                        if M > 0 and M % TB == 0:
                            keep_sums(b, (M - 1) // MICRO, (M - 1) % MICRO // TB)
                        if not last and 0 <= M - PREP_AT < JOBS:
                            read_prep(b + 1, M - PREP_AT)
                        if not last and M in MIDDLE:
                            middle_part(b + 1, MIDDLE[M])

                act.sem_inc(exp_set, XB)
                act.sem_inc(prep_free, 1)
                act.sem_inc(ov_set, 1)
                act.wait_ge(w_in, 64)
                for j in range(JOBS):
                    read_prep(0, j, 2)
                for t in range(3):
                    middle_part(0, t)
                batch(0, True, False)
                with act.Fori(1, B - 1) as b:
                    batch(b, False, False)
                batch(B - 1, False, True)
                keep_sums(B - 1, NG - 1, 1)

            @block.vector
            def _(dve):
                def norm(nb, i):
                    n = nb * TB + i
                    if i >= 2:
                        dve.wait_ge(prep_ready, nb * JOBS + (i - 1))
                    nc.vector.tensor_scalar(xn[:, i % 2, :], X[:, col(n, D)], core.mean[:, bass.ds(n, 1)],
                                            core.rstd[:, bass.ds(n, 1)], ALU.subtract, ALU.mult).then_inc(xn_set, 1)

                def rest(nb, j, banks=1):
                    k = j - TB - 1
                    t, half = k // 2, slice(k % 2 * QH, (k % 2 + 1) * QH)
                    dve.wait_ge(h_part, nb * 6 + (k + 1))
                    if k == 0 and not (isinstance(nb, int) and nb == 0):
                        dve.wait_ge(l_set, nb * 3)
                    nc.vector.tensor_tensor(R[:, t, half], ps[:, prep_bank(j, banks), 0:QH], parts[:, t, 0, half], ALU.subtract).then_inc(r_set, 1)

                def maximum(b, t, q):
                    g, k = t // MICRO, t % MICRO * GH + q
                    dve.wait_ge(s_ready, b * (NG * UNITS) + (g * UNITS + k + 1))
                    nc.vector.tensor_reduce(mx[:, g, k // 2, k % 2:k % 2 + 1], ps[:, k % SB, 0:QH], AX.X, ALU.max).then_inc(mx_set, 1)

                def maxima(b, t, half):
                    for q in range(half * 2, half * 2 + 2):
                        maximum(b, t, q)
                    if half == 1 and t % MICRO == MICRO - 1:
                        g = t // MICRO
                        dve.wait_ge(mx_set, b * (NG * MAXIMA) + (g * MAXIMA + UNITS + SB))
                        nc.vector.tensor_reduce(mxq[:, g, :], mx[:, g, :, :], AX.X, ALU.max).then_inc(mx_set, 1)

                def read_bank6(b, what):
                    dve.wait_ge(b6_ready, b6(b, what) + 1)
                    if what[0] == "m":
                        g = int(what[1])
                        at = ((b + 1 if g == 0 else b) * NG + g) * 4
                        p = nm_parts[:, g, :, :]
                        nc.vector.tensor_scalar(nm[:, 0, :], ps[0:GH * TB, 6, 0:P], -1.0, None, ALU.mult).then_inc(b6_free, 1)
                        dve.wait_ge(b6_free, b6(b, what) + 2)
                        nc.vector.tensor_copy(p[:, 0, :], nm[:, 0, :]).then_inc(nm_step, 1)
                        dve.wait_ge(nm_step, at + 1)
                        nc.vector.tensor_tensor(nm[:, 1, :], nm[:, 0, :], p[:, 0, :], ALU.subtract).then_inc(nm_step, 1)
                        dve.wait_ge(nm_step, at + 2)
                        nc.vector.tensor_copy(p[:, 1, :], nm[:, 1, :]).then_inc(nm_step, 1)
                        dve.wait_ge(nm_step, at + 3)
                        nc.vector.tensor_tensor(p[:, 2, :], nm[:, 1, :], p[:, 1, :], ALU.subtract).then_inc(nm_step, 1)
                        dve.wait_ge(nm_step, at + 4)
                        dve.sem_inc(nm_set, 1)
                    elif what[0] == "o":
                        g, half = int(what[1]), int(what[2])
                        ob = b - 1 if what == "o21" else b
                        src = ps[:, 6, 0:QH].rearrange("p (i h c) -> p i h c", i=HB, h=GH)
                        nc.vector.reciprocal(rc[:, :, :], src[:, :, :, HD]).then_inc(rc_set, 1)
                        dve.wait_ge(rc_set, ob * (2 * NG) + (2 * g + half + 1))
                        dst = O[:, half * HB:(half + 1) * HB, g * GH * HD:(g + 1) * GH * HD].rearrange("p i (h c) -> p i h c", h=GH)
                        scale = rc[:, :, :].rearrange("p i (h a) -> p i h a", a=1).broadcast_to((P, HB, GH, HD))
                        nc.vector.tensor_tensor(dst, src[:, :, :, 0:HD], scale, ALU.mult).then_inc(b6_free, 1)
                    else:
                        j = int(what[4])
                        if j < TB:
                            op = nc.vector.tensor_copy(oT[0:HALF, j % 2, :, :], ps[0:HALF, 6, 0:2 * P].rearrange("p (c t) -> p c t", c=2))
                        if j > 0:
                            n = b * TB + (j - 1 - TB)
                            op = nc.vector.tensor_tensor(X[:, col(n, D)], ps[:, 6, 2 * P:2 * P + D], X[:, col(n, D)], ALU.add)
                        op.then_inc(b6_free, 1)

                def stat(b, i):
                    n = b * TB + (i - TB)
                    dve.wait_ge(b6_free, b6(b, f"tail{TB}") + 2)
                    nc.vector.bn_stats(core.stats[:, col(n, 6)], X[:, col(n, D)]).then_inc(st_set, 1)

                def batch(b, first, last):
                    for M in range(M_ALL):
                        mb, t = ahead(b, M)
                        more = not last or M + AHEAD < M_ALL
                        if more:
                            maxima(mb, t, 0)
                        if not last and 0 <= M - PREP_AT + 1 < TB:
                            norm(b + 1, M - PREP_AT + 1)
                        if more:
                            maxima(mb, t, 1)
                        if M in B6 and not (first and M < 2 + TB + 1) and not (last and B6[M] == "m0"):
                            read_bank6(b, B6[M])
                        if not first and 11 <= M < 11 + TB:
                            stat(b, M - 11)
                        if not last and TB < M - PREP_AT < JOBS:
                            rest(b + 1, M - PREP_AT)
                        if last and M == 11 + TB:
                            mean_and_var(nc, dve, core, st_set, NT - TB, dve_step, var_set, between(0, NT - TB), 0)

                dve.sem_inc(mx_set, SB)
                dve.sem_inc(b6_free, 1)
                dve.sem_inc(r_set, 1)
                dve.wait_ge(w_in, 64)
                for i in range(TB):
                    norm(0, i)
                for j in range(TB + 1, JOBS):
                    rest(0, j, 2)
                for t in range(AHEAD):
                    maxima(0, t, 0)
                    maxima(0, t, 1)
                    if t == MICRO:
                        read_bank6(-1, "m0")
                batch(0, True, False)
                with dve.Fori(1, B - 1) as b:
                    batch(b, False, False)
                batch(B - 1, False, True)
                for what in ORDER[:LATE]:
                    read_bank6(B, what)
                for i in range(TB):
                    stat(B, i)
                mean_and_var(nc, dve, core, st_set, NT, dve_step, var_set, between(NT - TB, NT), 1)


def route_phase(core):
    nc, a, ps = core.nc, core.a, core.ps
    X = core.XA
    with ExitStack() as ctx:
        def sb(name, shape, dt=F32):
            return ctx.enter_context(nc.sbuf_tensor(name, shape, dt))

        def sem(name):
            return ctx.enter_context(nc.semaphore(name))

        RT = NT // 4
        gate_w = sb("gate_w", [HALF + 1, 2, E])
        aff = sb("affine2", [HALF, 2, 4])
        xn = sb("r_xn", [P, 2, D])
        hT = sb("r_hT", [HALF + 1, 2, 2, P])
        steps = sb("steps", [P, NSLOT])
        ids = sb("ids", [P, NT, TOPK])
        before, ones = sb("before", [P, P]), sb("ones", [P, P])
        logit, at_max, either = sb("logit", [P, RT, E]), sb("at_max", [P, RT, E]), sb("either", [P, RT, E])
        pick = [sb(f"pick{k}", [P, RT, E]) for k in range(TOPK)]
        top = sb("top", [P, TOPK, RT])
        first = sb("first", [P, RT])
        ex, den = sb("exp_dif", [P, RT]), sb("denom", [P, RT])
        run = sb("running", [P, 2, RT, E])
        count = sb("count", [P, E])
        place, chosen = sb("place", [P, RT, E]), sb("chosen", [P, RT, E])
        slot_f = sb("slot_f", [P, NT, TOPK])
        full = sb("full", [P, E, NT])
        tiles, ends, gap = sb("tiles", [P, E]), sb("ends", [P, 4, E]), sb("gap", [P, E])
        past = sb("past", [P, NSLOT, E])
        past_n = sb("past_n", [P, NSLOT])
        spare, unread = sb("spare", [P, 2, E]), sb("unread", [P, E])
        empty = sb("empty_rows", [P, E, D + 1])
        miss, fill_f = sb("missing", [P, E]), sb("fill_f", [P, E])
        fill_at = sb("fill_at", [P, E], U32)
        send = sb("send", [P, 4, TOPK, D + 1])
        send_at = sb("send_at", [P, 4, TOPK], U32)
        const_in, w_in, b2_in, const_set = sem("r_const_in"), sem("r_w_in"), sem("r_b2_in"), sem("r_const_set")
        xn_set, t_ready, hT_set, g_ready = sem("r_xn_set"), sem("r_t_ready"), sem("r_hT_set"), sem("r_g_ready")
        pick_set, count_ready, step, dif_set, exp_set = sem("r_pick_set"), sem("r_count_ready"), sem("r_step"), sem("r_dif_set"), sem("r_exp_set")
        send_set, sending, hx_set = sem("r_send_set"), sem("r_sending"), sem("r_hx_set")
        sent = [sem(f"r_sent{u}") for u in range(4)]
        zero_set, spare_set, empty_out, fill_set, filled = (sem("r_" + n) for n in ("zero_set", "spare_set", "empty_out", "fill_set", "filled"))
        with nc.Block() as block:
            @block.sync
            def _(sp):
                sp.dma_start(gate_w[0:HALF, :, :], a["gate_w"].rearrange("(c k) n -> k c n", c=2)).then_inc(const_in, 16)
                sp.dma_start(gate_w[HALF:HALF + 1, 1, :], a["gate_b"].rearrange("(a c) -> a c", a=1)).then_inc(const_in, 16)
                sp.dma_start(aff[:, :, :], a["affine"].rearrange("(c k) t -> k c t", c=2)).then_inc(const_in, 16)
                sp.dma_start(steps[:, :], a["steps"]).then_inc(const_in, 16)
                sp.dma_start(ids[:, :, :], a["ids"]).then_inc(const_in, 16)
                sp.dma_start(before[:, :], a["before"]).then_inc(const_in, 16)
                sp.dma_start(spare[:, :, :], a["spare"]).then_inc(const_in, 16)
                sp.dma_start(unread[:, :], a["unread"]).then_inc(const_in, 16)
                sp.wait_ge(spare_set, 1)
                sp.dma_start(core.slot_x[E * NT * P:(E * NT + E) * P, :].rearrange("(e p) c -> p e c", p=P),
                             empty[:, :, :]).then_inc(empty_out, 16)
                for e in range(E):
                    if e > 0:
                        sp.wait_ge(send_set, 5 * e)
                    sp.dma_start(core.W1[0:HALF, e, :, :], a["w1"][e].rearrange("(c k) n -> k c n", c=2)).then_inc(w_in, 16)
                    sp.dma_start(core.W2[:, e, :, :], a["w2"][e].rearrange("(j k) n -> k j n", k=P)).then_inc(w_in, 16)
                sp.dma_start(core.W1[HALF:HALF + 1, :, 1, :], a["b1"].rearrange("(a e) n -> a e n", a=1)).then_inc(w_in, 16)
                sp.wait_ge(w_in, 16 * (2 * E + 1))

            @block.gpsimd
            def _(pool):
                nc.gpsimd.memset(hT[HALF:HALF + 1, :, :, :], 1.0).then_inc(const_set, 1)
                pool.wait_ge(const_set, 1)
                nc.gpsimd.memset(ones[:, :], 1.0).then_inc(const_set, 1)
                for b in range(B):
                    cols = slice(b * TB * D, (b + 1) * TB * D)
                    nc.gpsimd.tensor_tensor(core.H[:, cols], core.H[:, cols], X[:, cols], ALU.add).then_inc(hx_set, 1)
                pool.wait_ge(hx_set, B)
                nc.gpsimd.memset(empty[:, :, :], 0.0).then_inc(zero_set, 1)
                pool.wait_ge(zero_set, 1)
                pool.wait_ge(const_in, 128)
                nc.gpsimd.tensor_copy(empty[:, :, D], spare[:, 0, :]).then_inc(spare_set, 1)
                pool.wait_ge(empty_out, 16)
                nc.gpsimd.tensor_copy(empty[:, :, D], spare[:, 1, :]).then_inc(spare_set, 1)
                pool.wait_ge(spare_set, 2)
                with pool.Fori(0, NT // 4) as i:
                    for u in range(4):
                        pool.wait_ge(send_set, i * 4 + (u + 1))
                        pool.sem_inc(sending, 1)
                        for k in range(TOPK):
                            pool.indirect_dma_start(core.slot_x, bass.IndirectOffsetOnAxis(ap=send_at[:, u, k:k + 1], axis=0),
                                                    send[:, u, k, :], None).then_inc(sent[u], 16)
                pool.wait_ge(fill_set, 1)
                for e in range(E):
                    pool.indirect_dma_start(core.slot_x, bass.IndirectOffsetOnAxis(ap=fill_at[:, e:e + 1], axis=0),
                                            empty[:, e, :], None).then_inc(filled, 16)
                for u in range(4):
                    pool.wait_ge(sent[u], TOPK * 16 * (NT // 4))
                pool.wait_ge(filled, 16 * E)

            @block.tensor
            def _(pe):
                def transpose(n, u):
                    pe.wait_ge(xn_set, n + 1)
                    pe.wait_ge(hT_set, n + 1)
                    for c in range(2):
                        mm = nc.tensor.transpose(ps[0:HALF, u, c * P:(c + 1) * P], xn[:, u, c * HALF:(c + 1) * HALF], core.ident[:, :])
                    mm.then_inc(t_ready, 1)

                def gate(n, u):
                    pe.wait_ge(hT_set, n + 3)
                    nc.tensor.matmul(ps[:, 2, col(n, E)], hT[0:HALF, u, 0, :], gate_w[0:HALF, 0, :], start=True, stop=False)
                    nc.tensor.matmul(ps[:, 2, col(n, E)], hT[:, u, 1, :], gate_w[:, 1, :], start=False, stop=True).then_inc(g_ready, 1)

                pe.wait_ge(const_in, 128)
                pe.wait_ge(const_set, 2)
                pe.sem_inc(g_ready, 2)
                flat = either[:, :, :].rearrange("p n e -> p (n e)")
                for c in range(4):
                    transpose(c * RT, 0)
                    with pe.Fori(0, RT // 2 - 1) as i:
                        for u in range(2):
                            transpose(i * 2 + (c * RT + u + 1), 1 - u)
                            gate(i * 2 + (c * RT + u), u)
                    transpose(c * RT + RT - 1, 1)
                    for u in range(2):
                        gate(c * RT + RT - 2 + u, u)
                    pe.wait_ge(pick_set, c + 1)
                    nc.tensor.matmul(ps[:, 3, 0:RT * E], before[:, :], flat, start=True, stop=True).then_inc(count_ready, 1)
                    nc.tensor.matmul(ps[:, 4, 0:RT * E], ones[:, :], flat, start=True, stop=True).then_inc(count_ready, 1)

            @block.scalar
            def _(act):
                act.dma_start(core.b2[:, :, :], a["b2"].rearrange("(a e) n -> a e n", a=1).broadcast_to((P, E, D))).then_inc(b2_in, 16)

                def affine(n, u):
                    act.wait_ge(t_ready, n + 1)
                    act.wait_ge(g_ready, n + 1)
                    for c in range(2):
                        op = nc.scalar.activation(hT[0:HALF, u, c, :], ps[0:HALF, u, c * P:(c + 1) * P], ACT.Identity,
                                                  scale=aff[:, c, 2:3], bias=aff[:, c, 3:4])
                    op.then_inc(hT_set, 1)

                act.sem_inc(hT_set, 2)
                act.wait_ge(const_in, 128)
                for c in range(4):
                    with act.Fori(0, RT // 2) as i:
                        for u in range(2):
                            affine(i * 2 + (c * RT + u), u)
                    act.wait_ge(dif_set, c + 1)
                    nc.scalar.activation(ex[:, :], ex[:, :], ACT.Exp).then_inc(exp_set, 1)
                act.wait_ge(exp_set, 4)
                act.wait_ge(b2_in, 16)

            @block.vector
            def _(dve):
                def norm(n, u):
                    nc.vector.tensor_scalar(xn[:, u, :], X[:, col(n, D)], core.mean[:, bass.ds(n, 1)],
                                            core.rstd[:, bass.ds(n, 1)], ALU.subtract, ALU.mult).then_inc(xn_set, 1)

                def rows_to_send(n, u):
                    for k in range(TOPK):
                        nc.vector.tensor_scalar(send[:, u, k, 0:D], X[:, col(n, D)], core.mean[:, bass.ds(n, 1)],
                                                core.rstd[:, bass.ds(n, 1)], ALU.subtract, ALU.mult)
                    nc.vector.tensor_copy(send[:, u, :, D], ids[:, bass.ds(n, 1), :].rearrange("p a k -> p (a k)"))
                    nc.vector.tensor_copy(send_at[:, u, :], slot_f[:, bass.ds(n, 1), :].rearrange("p a k -> p (a k)")).then_inc(send_set, 1)

                def four_tiles(c, i):
                    for u in range(4):
                        if c < 4:
                            n = i * 4 + (c * RT + u)
                            if not (isinstance(i, int) and i == 0 and c == 0 and u < 2):
                                dve.wait_ge(t_ready, i * 4 + (c * RT + u - 1))
                            norm(n, u % 2)
                        if c > 0:
                            if not (isinstance(i, int) and i == 0 and c == 1):
                                dve.wait_ge(sent[u], i * (TOPK * 16) + (c - 1) * (RT // 4) * TOPK * 16)
                            rows_to_send(i * 4 + ((c - 1) * RT + u), u)

                done = 0

                def then(op):
                    nonlocal done
                    done += 1
                    op.then_inc(step, 1)
                    dve.wait_ge(step, done)

                def per_expert(ap):
                    return ap.rearrange("p (n a) -> p n a", a=1).broadcast_to((P, RT, E))

                def per_tile(ap):
                    return ap.rearrange("p (a e) -> p a e", a=1).broadcast_to((P, RT, E))

                expert = per_tile(steps[:, 0:E])

                def route(c):
                    ns = slice(c * RT, (c + 1) * RT)
                    dve.wait_ge(g_ready, (c + 1) * RT + 2)
                    then(nc.vector.tensor_copy(logit[:, :, :], ps[:, 2, c * RT * E:(c + 1) * RT * E].rearrange("p (n e) -> p n e", e=E)))
                    for k in range(TOPK):
                        then(nc.vector.tensor_reduce(top[:, k, :], logit[:, :, :], AX.X, ALU.max))
                        then(nc.vector.tensor_tensor(at_max[:, :, :], logit[:, :, :], per_expert(top[:, k, :]), ALU.is_ge))
                        then(nc.vector.scalar_tensor_tensor(at_max[:, :, :], expert, float(E), at_max[:, :, :], ALU.subtract, ALU.mult))
                        then(nc.vector.tensor_reduce(first[:, :], at_max[:, :, :], AX.X, ALU.min))
                        then(nc.vector.scalar_tensor_tensor(pick[k][:, :, :], expert, float(E), per_expert(first[:, :]), ALU.subtract, ALU.is_equal))
                        if k == 0:
                            then(nc.vector.scalar_tensor_tensor(logit[:, :, :], pick[0][:, :, :], -3.0e38, logit[:, :, :], ALU.mult, ALU.add))
                    then(nc.vector.tensor_tensor(either[:, :, :], pick[0][:, :, :], pick[1][:, :, :], ALU.add))
                    dve.sem_inc(pick_set, 1)
                    then(nc.vector.tensor_tensor(ex[:, :], top[:, 1, :], top[:, 0, :], ALU.subtract))
                    dve.sem_inc(dif_set, 1)
                    dve.wait_ge(exp_set, c + 1)
                    then(nc.vector.tensor_scalar(den[:, :], ex[:, :], 1.0, None, ALU.add))
                    then(nc.vector.reciprocal(core.weight[:, 0, ns], den[:, :]))
                    then(nc.vector.tensor_tensor(core.weight[:, 1, ns], core.weight[:, 0, ns], ex[:, :], ALU.mult))
                    dve.wait_ge(count_ready, 2 * c + 2)
                    total = ps[:, 4, 0:RT * E].rearrange("p (n e) -> p n e", e=E)
                    then(nc.vector.tensor_copy(run[:, 0, :, :], total))
                    reach, r = 1, 0
                    while reach < RT:
                        then(nc.vector.tensor_copy(run[:, 1 - r, 0:reach, :], run[:, r, 0:reach, :]))
                        then(nc.vector.tensor_tensor(run[:, 1 - r, reach:RT, :], run[:, r, reach:RT, :], run[:, r, 0:RT - reach, :], ALU.add))
                        reach, r = 2 * reach, 1 - r
                    then(nc.vector.tensor_tensor(place[:, :, :], run[:, r, :, :], total, ALU.subtract))
                    then(nc.vector.tensor_tensor(place[:, :, :], ps[:, 3, 0:RT * E].rearrange("p (n e) -> p n e", e=E), place[:, :, :], ALU.add))
                    then(nc.vector.scalar_tensor_tensor(place[:, :, :], expert, float(NT * P), place[:, :, :], ALU.mult, ALU.add))
                    if c > 0:
                        then(nc.vector.tensor_tensor(place[:, :, :], place[:, :, :], per_tile(count[:, :]), ALU.add))
                        then(nc.vector.tensor_tensor(count[:, :], count[:, :], run[:, r, RT - 1, :], ALU.add))
                    else:
                        then(nc.vector.tensor_copy(count[:, :], run[:, r, RT - 1, :]))
                    for k in range(TOPK):
                        then(nc.vector.tensor_tensor(chosen[:, :, :], pick[k][:, :, :], place[:, :, :], ALU.mult))
                        then(nc.vector.tensor_reduce(slot_f[:, ns, k], chosen[:, :, :], AX.X, ALU.add))

                def tile_tables():
                    each = count[:, :].rearrange("p (e a) -> p e a", a=1).broadcast_to((P, E, NT))
                    mult = steps[:, 0:NT].rearrange("p (a n) -> p a n", a=1).broadcast_to((P, E, NT))
                    then(nc.vector.scalar_tensor_tensor(full[:, :, :], mult, float(P), each, ALU.mult, ALU.is_lt))
                    then(nc.vector.tensor_reduce(tiles[:, :], full[:, :, :], AX.X, ALU.add))
                    part = ids[:, 0, 0:1].broadcast_to((P, E))
                    then(nc.vector.scalar_tensor_tensor(miss[:, :], tiles[:, :], float(P), count[:, :], ALU.mult, ALU.subtract))
                    then(nc.vector.tensor_tensor(miss[:, :], part, miss[:, :], ALU.is_lt))
                    then(nc.vector.scalar_tensor_tensor(fill_f[:, :], steps[:, 0:E], float(NT * P), count[:, :], ALU.mult, ALU.add))
                    then(nc.vector.tensor_tensor(fill_f[:, :], fill_f[:, :], part, ALU.add))
                    then(nc.vector.tensor_tensor(fill_f[:, :], fill_f[:, :], unread[:, :], ALU.subtract))
                    then(nc.vector.tensor_tensor(fill_f[:, :], fill_f[:, :], miss[:, :], ALU.mult))
                    then(nc.vector.tensor_tensor(fill_f[:, :], fill_f[:, :], unread[:, :], ALU.add))
                    then(nc.vector.tensor_copy(fill_at[:, :], fill_f[:, :]))
                    dve.sem_inc(fill_set, 1)
                    then(nc.vector.tensor_copy(ends[:, 0, :], tiles[:, :]))
                    reach, s = 1, 0
                    while reach < E:
                        then(nc.vector.tensor_copy(ends[:, s + 1, 0:reach], ends[:, s, 0:reach]))
                        then(nc.vector.tensor_tensor(ends[:, s + 1, reach:E], ends[:, s, reach:E], ends[:, s, 0:E - reach], ALU.add))
                        reach, s = 2 * reach, s + 1
                    tile_no = steps[:, :].rearrange("p (s a) -> p s a", a=1).broadcast_to((P, NSLOT, E))
                    end = ends[:, s, :].rearrange("p (a e) -> p a e", a=1).broadcast_to((P, NSLOT, E))
                    then(nc.vector.tensor_tensor(past[:, :, :], tile_no, end, ALU.is_ge))
                    then(nc.vector.tensor_reduce(past_n[:, :], past[:, :, 0:E - 1], AX.X, ALU.add))
                    then(nc.vector.tensor_copy(core.tile_expert[:, :], past_n[:, :]))
                    then(nc.vector.tensor_scalar(gap[:, :], tiles[:, :], -1.0, float(NT), ALU.mult, ALU.add))
                    unused = gap[:, :].rearrange("p (a e) -> p a e", a=1).broadcast_to((P, NSLOT, E))
                    then(nc.vector.tensor_tensor(past[:, :, :], past[:, :, :], unused, ALU.mult))
                    then(nc.vector.tensor_reduce(past_n[:, :], past[:, :, :], AX.X, ALU.add))
                    then(nc.vector.tensor_tensor(past_n[:, :], past_n[:, :], steps[:, :], ALU.add))
                    then(nc.vector.tensor_copy(core.tile_at[:, :], past_n[:, :]))

                dve.wait_ge(const_in, 128)
                for c in range(5):
                    four_tiles(c, 0)
                    with dve.Fori(1, RT // 4) as i:
                        four_tiles(c, i)
                    if c < 4:
                        route(c)
                tile_tables()


def expert_phase(core):
    nc, a, ps = core.nc, core.a, core.ps
    with ExitStack() as ctx:
        def sb(name, shape, dt=F32):
            return ctx.enter_context(nc.sbuf_tensor(name, shape, dt))

        def sem(name):
            return ctx.enter_context(nc.semaphore(name))

        U = 8
        assert NSLOT % U == 0
        aff = sb("x_affine2", [HALF, 2, 4])
        xs = sb("slot_rows", [P, U, D + 1])
        hT = sb("x_hT", [HALF + 1, 2, 2, P])
        he = sb("hidden", [P, 2, HID])
        heT = sb("hiddenT", [P, 2, KH, P])
        ys = sb("slot_out", [P, 4, D])
        ys_at = sb("slot_out_at", [P, 4, 1], U32)
        aff_in, ones_set = sem("x_aff_in"), sem("x_ones_set")
        x_in = [sem(f"x_x_in{u}") for u in range(U)]
        xT_ready, hT_set, h_ready, he_set = sem("x_xT_ready"), sem("x_hT_set"), sem("x_h_ready"), sem("x_he_set")
        heT_ready, heT_set, y_ready, y_set = sem("x_heT_ready"), sem("x_heT_set"), sem("x_y_ready"), sem("x_y_set")
        sum_set, sending = sem("x_sum_set"), sem("x_sending")
        y_out = [sem(f"x_y_out{u}") for u in range(4)]

        def has(j, back):
            return j is None or 0 <= j - back < NSLOT

        def steps(engine, step):
            for u in range(U):
                step(u, u, 0)
            with engine.Fori(1, NSLOT // U) as i:
                for u in range(U):
                    step(None, u, i)
            for u in range(3):
                step(NSLOT + u, u, NSLOT // U)

        def tile(i, u, back):
            return i * U + (u - back)

        def expert_of(engine, s):
            return engine.value_load(core.tile_expert[0:1, bass.ds(s, 1)], min_val=0, max_val=E - 1)

        with nc.Block() as block:
            @block.sync
            def _(sp):
                sp.dma_start(aff[:, :, :], a["affine"].rearrange("(c k) t -> k c t", c=2)).then_inc(aff_in, 16)

                def place_of(s):
                    return sp.value_load(core.tile_at[0:1, bass.ds(s, 1)], min_val=0, max_val=E * NT + E - 1)

                for u in range(U):
                    at = place_of(u)
                    sp.dma_start(xs[:, u, :], core.slot_x[bass.ds(at * P, P), :]).then_inc(x_in[u], 16)
                with sp.Fori(1, NSLOT // U) as i:
                    for u in range(U):
                        at = place_of(i * U + u)
                        sp.wait_ge(y_set, tile(i, u, U) + 1)
                        sp.dma_start(xs[:, u, :], core.slot_x[bass.ds(at * P, P), :]).then_inc(x_in[u], 16)

            @block.gpsimd
            def _(pool):
                nc.gpsimd.memset(hT[HALF:HALF + 1, :, :, :], 1.0).then_inc(ones_set, 1)
                with pool.Fori(0, NSLOT // 4) as i:
                    for u in range(4):
                        pool.wait_ge(y_set, i * 4 + (u + 1))
                        pool.sem_inc(sending, 1)
                        pool.indirect_dma_start(core.tok_y, bass.IndirectOffsetOnAxis(ap=ys_at[:, u, 0:1], axis=0),
                                                ys[:, u, :], None).then_inc(y_out[u], 16)
                for u in range(4):
                    pool.wait_ge(y_out[u], 16 * (NSLOT // 4))

            @block.tensor
            def _(pe):
                def step(j, u, i):
                    if has(j, 0):
                        s = tile(i, u, 0)
                        pe.wait_ge(x_in[u], (i + 1) * 16)
                        pe.wait_ge(hT_set, s)
                        for c in range(2):
                            mm = nc.tensor.transpose(ps[0:HALF, 0, c * P:(c + 1) * P], xs[:, u, c * HALF:(c + 1) * HALF], core.ident[:, :])
                        mm.then_inc(xT_ready, 1)
                    if has(j, 1):
                        s, v = tile(i, u, 1), (u - 1) % 2
                        e = expert_of(pe, s)
                        pe.wait_ge(hT_set, s + 1)
                        if has(j, 3):
                            pe.wait_ge(he_set, tile(i, u, 3) + 1)
                        for half in range(2):
                            for c in range(2):
                                rows = HALF + c
                                w = core.W1[0:rows, bass.ds(e, 1), c, half * QH:(half + 1) * QH].rearrange("p a n -> p (a n)")
                                mm = nc.tensor.matmul(ps[:, 1 + 2 * v + half, 0:QH], hT[0:rows, v, c, :], w, start=(c == 0), stop=(c == 1))
                        mm.then_inc(h_ready, 1)
                    if has(j, 2):
                        s, v = tile(i, u, 2), u % 2
                        pe.wait_ge(he_set, s + 1)
                        pe.wait_ge(heT_set, s)
                        for k in range(KH):
                            mm = nc.tensor.transpose(ps[:, 5 + k // 3, k % 3 * P:(k % 3 + 1) * P], he[:, v, k * P:(k + 1) * P], core.ident[:, :])
                        mm.then_inc(heT_ready, 1)
                    if has(j, 3):
                        s, v = tile(i, u, 3), (u - 3) % 2
                        e = expert_of(pe, s)
                        pe.wait_ge(heT_set, s + 1)
                        pe.wait_ge(sum_set, s)
                        for k in range(KH):
                            w = core.W2[:, bass.ds(e, 1), k, :].rearrange("p a n -> p (a n)")
                            mm = nc.tensor.matmul(ps[:, 7, 0:D], heT[:, v, k, :], w, start=(k == 0), stop=(k == KH - 1))
                        mm.then_inc(y_ready, 1)

                pe.wait_ge(ones_set, 1)
                steps(pe, step)

            @block.scalar
            def _(act):
                def step(j, u, i):
                    if has(j, 1):
                        s, v = tile(i, u, 1), (u - 1) % 2
                        act.wait_ge(h_ready, s + 1)
                        if has(j, 3):
                            act.wait_ge(heT_ready, tile(i, u, 3) + 1)
                        src = ps[:, 1 + 2 * v:3 + 2 * v, 0:QH]
                        nc.scalar.activation(he[:, v, :].rearrange("p (a n) -> p a n", a=2), src, ACT.Gelu).then_inc(he_set, 1)

                steps(act, step)

            @block.vector
            def _(dve):
                def step(j, u, i):
                    if has(j, 0):
                        s, v = tile(i, u, 0), u % 2
                        dve.wait_ge(xT_ready, s + 1)
                        if has(j, 2):
                            dve.wait_ge(h_ready, tile(i, u, 2) + 1)
                        for c in range(2):
                            op = nc.vector.tensor_scalar(hT[0:HALF, v, c, :], ps[0:HALF, 0, c * P:(c + 1) * P],
                                                         aff[:, c, 2:3], aff[:, c, 3:4], ALU.mult, ALU.add)
                        op.then_inc(hT_set, 1)
                    if has(j, 2):
                        s, v = tile(i, u, 2), u % 2
                        dve.wait_ge(heT_ready, s + 1)
                        if has(j, 4):
                            dve.wait_ge(y_ready, tile(i, u, 4) + 1)
                        nc.vector.tensor_copy(heT[:, v, :, :].rearrange("p (a k) t -> p a (k t)", a=2), ps[:, 5:7, 0:QH]).then_inc(heT_set, 1)
                    if has(j, 3):
                        s, v = tile(i, u, 3), (u - 3) % 4
                        e = expert_of(dve, s)
                        dve.wait_ge(y_ready, s + 1)
                        if has(j, 7):
                            dve.wait_ge(y_out[v], (tile(i, u, 3) - v) * 4)
                        bias = core.b2[:, bass.ds(e, 1), :].rearrange("p a n -> p (a n)")
                        nc.vector.tensor_tensor(ys[:, v, :], ps[:, 7, 0:D], bias, ALU.add).then_inc(sum_set, 1)
                        nc.vector.tensor_copy(ys_at[:, v, :], xs[:, (u - 3) % U, D:D + 1]).then_inc(y_set, 1)

                dve.wait_ge(aff_in, 16)
                steps(dve, step)


def combine_phase(core):
    nc, H = core.nc, core.H
    with ExitStack() as ctx:
        def sb(name, shape, dt=F32):
            return ctx.enter_context(nc.sbuf_tensor(name, shape, dt))

        def sem(name):
            return ctx.enter_context(nc.semaphore(name))

        U = 4
        y = sb("expert_rows", [P, U, TOPK, TB, D])
        y_in = [sem(f"f_y_in{u}") for u in range(U)]
        part_set, out_set, out_done = sem("f_part_set"), sem("f_out_set"), sem("f_out_done")
        rows = core.tok_y[0:TOPK * NT * P, :].rearrange("(k b i p) c -> b k p i c", k=TOPK, b=B, i=TB)
        with nc.Block() as block:
            @block.sync
            def _(sp):
                for b in range(B):
                    if b >= U:
                        sp.wait_ge(out_set, (b - U + 1) * TB)
                    for k in range(TOPK):
                        sp.dma_start(y[:, b % U, k, :, :], rows[b, k]).then_inc(y_in[b % U], 16)

            @block.vector
            def _(dve):
                with dve.Fori(0, B // U) as i:
                    for u in range(U):
                        for k in range(TOPK):
                            for t in range(TB):
                                n = i * (U * TB) + (u * TB + t)
                                if k == 0:
                                    dve.wait_ge(y_in[u], (i + 1) * (16 * TOPK))
                                else:
                                    dve.wait_ge(part_set, n + 1)
                                nc.vector.scalar_tensor_tensor(H[:, col(n, D)], y[:, u, k, t, :], core.weight[:, k, bass.ds(n, 1)],
                                                               H[:, col(n, D)], ALU.mult, ALU.add).then_inc((part_set, out_set)[k], 1)

            @block.scalar
            def _(act):
                for b in range(B):
                    act.wait_ge(out_set, (b + 1) * TB)
                    act.dma_start(core.out[b].rearrange("(i p) c -> p i c", p=P),
                                  H[:, b * TB * D:(b + 1) * TB * D].rearrange("p (i c) -> p i c", i=TB)).then_inc(out_done, 16)
                act.wait_ge(out_done, 16 * B)



PHASES = (embed_phase, project_phase, conv_phase, mix_out_phase, attention_phase, route_phase, expert_phase,
          combine_phase)


def build_program(nc, a, out):
    with ExitStack() as ctx:
        core = Core(nc, a, out, ctx)
        for phase in PHASES:
            phase(core)


_OUT = ((B, S, D), "float32")


def lay_out(x, txt, L0_tok_W, L0_tok_b, L0_attn_w_in, L0_attn_b_in, L0_attn_w_filt, L0_attn_b_filt,
            L0_attn_w_short, L0_attn_b_short, L0_attn_w_out, L0_attn_b_out, L0_ffn_ln1_g, L0_ffn_ln1_b,
            L0_ffn_qkv_w, L0_ffn_proj_w, L0_ffn_proj_b, L0_ffn_ln2_g, L0_ffn_ln2_b, L0_ffn_gate_w,
            L0_ffn_gate_b, L0_ffn_w1, L0_ffn_b1, L0_ffn_w2, L0_ffn_b2):
    x, w = np.asarray(x), np.asarray(L0_tok_W)
    patches = x.reshape(B, C, GRID, PATCH, GRID, PATCH).transpose(1, 3, 5, 0, 2, 4).reshape(KP, P, B * NPATCH)
    wtok = w.reshape(D, KP, P).transpose(2, 1, 0)
    ins = {
        "patches": patches.transpose(1, 0, 2).reshape(P, KP * B * NPATCH),
        "wtok": wtok.reshape(P, KP * D),
        "txt": txt, "tok_b": L0_tok_b, "w_in": L0_attn_w_in, "b_in": L0_attn_b_in, "w_filt": L0_attn_w_filt,
        "b_filt": L0_attn_b_filt, "short": np.concatenate([np.asarray(L0_attn_w_short)[:, 0, :], np.asarray(L0_attn_b_short)[:, None]], 1), "w_out": L0_attn_w_out,
        "b_out": L0_attn_b_out, "affine": np.stack([L0_ffn_ln1_g, L0_ffn_ln1_b, L0_ffn_ln2_g, L0_ffn_ln2_b], 1), "qkv_w": L0_ffn_qkv_w,
        "proj_w": L0_ffn_proj_w, "proj_b": L0_ffn_proj_b,
        "gate_w": L0_ffn_gate_w, "gate_b": L0_ffn_gate_b, "w1": L0_ffn_w1, "b1": L0_ffn_b1, "w2": L0_ffn_w2,
        "b2": L0_ffn_b2,
    } | shape_tables()
    return {k: np.ascontiguousarray(v) for k, v in ins.items()}


def kernel(**inputs):
    import concourse.bacc as bacc
    from concourse.bass_utils import run_bass_kernel_spmd
    arrays = lay_out(**inputs)
    nc = bacc.Bacc("TRN2", target_bir_lowering=False, num_devices=1)
    a = {k: nc.dram_tensor("in_" + k, v.shape, mybir.dt.from_np(v.dtype), kind="ExternalInput").ap() for k, v in arrays.items()}
    out = nc.dram_tensor("out_0_dram", _OUT[0], F32, kind="ExternalOutput").ap()
    build_program(nc, a, out)
    if not nc.is_finalized():
        nc.finalize()
    r = run_bass_kernel_spmd(nc, [{"in_" + k: v for k, v in arrays.items()}], core_ids=[0])
    return np.asarray(r.results[0]["out_0_dram"])
```
